# Optimizing a Trainium2 kernel written in Bass

```python
import numpy as np
import jax
import jax.numpy as jnp

def _softmax(x, axis=-1):
    return jax.nn.softmax(x, axis=axis)

def _gelu(x):
    return jax.nn.gelu(x, approximate=True)

def _silu(x):
    return jax.nn.silu(x)

def _sigmoid(x):
    return jax.nn.sigmoid(x)

def _layernorm(x, axis=-1, eps=1e-05):
    m = jnp.mean(x, axis=axis, keepdims=True)
    v = jnp.var(x, axis=axis, keepdims=True)
    return (x - m) / jnp.sqrt(v + eps)

def _scatter_add(tgt, idx, src, axis=0):
    return tgt.at[idx].add(src)

def _segment_sum(src, seg, n):
    return jax.ops.segment_sum(src, seg, n)
kernel_name = 'mk_prb_d1_jaxref_r8_5d59aa'

def setup_inputs(seed: int=0):
    np.random.seed(seed)
    _w = jnp.asarray

    def _L0_attn_setup():
        import jax, jax.numpy as jnp
        import numpy as np
        B, L, E, H, WINDOW = (4, 128, 128, 16, 4)
        D = E // H
        SCALING = D ** (-0.5)

        def _get_relative_embeddings(emb, length):
            pad_length = max(length - (WINDOW + 1), 0)
            if pad_length > 0:
                emb = jnp.pad(emb, ((0, 0), (pad_length, pad_length), (0, 0)))
            start = max(WINDOW + 1 - length, 0)
            return emb[:, start:start + 2 * length - 1]

        def _rel_to_abs(x):
            bh, length, _ = x.shape
            x = jnp.pad(x, ((0, 0), (0, 0), (0, 1)))
            xf = x.reshape(bh, length * 2 * length)
            xf = jnp.pad(xf, ((0, 0), (0, length - 1)))
            xfin = xf.reshape(bh, length + 1, 2 * length - 1)
            return xfin[:, :length, length - 1:]

        def _abs_to_rel(x):
            bh, length, _ = x.shape
            x = jnp.pad(x, ((0, 0), (0, 0), (0, length - 1)))
            xf = x.reshape(bh, length * (2 * length - 1))
            xf = jnp.pad(xf, ((0, 0), (length, 0)))
            xfin = xf.reshape(bh, length, 2 * length)
            return xfin[:, :, 1:]
        key = jax.random.key(seed)
        ks = jax.random.split(key, 12)
        s = E ** (-0.5)
        return {'hidden_states': jax.random.normal(ks[0], (B, L, E), dtype=jnp.float32), 'Wq': jax.random.normal(ks[1], (E, E), dtype=jnp.float32) * s, 'bq': jnp.zeros((E,), dtype=jnp.float32), 'Wk': jax.random.normal(ks[2], (E, E), dtype=jnp.float32) * s, 'bk': jnp.zeros((E,), dtype=jnp.float32), 'Wv': jax.random.normal(ks[3], (E, E), dtype=jnp.float32) * s, 'bv': jnp.zeros((E,), dtype=jnp.float32), 'Wo': jax.random.normal(ks[4], (E, E), dtype=jnp.float32) * s, 'bo': jnp.zeros((E,), dtype=jnp.float32), 'emb_rel_k': jax.random.normal(ks[5], (1, 2 * WINDOW + 1, D), dtype=jnp.float32) * SCALING, 'emb_rel_v': jax.random.normal(ks[6], (1, 2 * WINDOW + 1, D), dtype=jnp.float32) * SCALING}
    _L0_attn_in = _L0_attn_setup()

    def _L0_ffn_setup():
        import jax, jax.numpy as jnp
        import numpy as np
        TOPK = 2
        CAPACITY_FACTOR = 1.0
        EPS = 1e-06
        B, S, D = (4, 512, 128)
        E = 8
        SUB_H = 256 // E
        key = jax.random.key(seed)
        ks = jax.random.split(key, 7)
        x = jax.random.normal(ks[0], (B, S, D), dtype=jnp.float32)
        w_gate_w = jax.random.normal(ks[1], (D, E), dtype=jnp.float32) * 0.02
        w_gate_b = jnp.zeros((E,), jnp.float32)
        W1 = jax.random.normal(ks[2], (E, D, SUB_H), dtype=jnp.float32) * 0.02
        b1 = jnp.zeros((E, SUB_H), jnp.float32)
        W2 = jax.random.normal(ks[3], (E, SUB_H, D), dtype=jnp.float32) * 0.02
        b2 = jnp.zeros((E, D), jnp.float32)
        return {'x': x, 'w_gate_w': w_gate_w, 'w_gate_b': w_gate_b, 'W1': W1, 'b1': b1, 'W2': W2, 'b2': b2}
    _L0_ffn_in = _L0_ffn_setup()
    _d = {'L0_attn_hidden_states': _L0_attn_in['hidden_states'], 'L0_attn_Wq': _L0_attn_in['Wq'], 'L0_attn_bq': _L0_attn_in['bq'], 'L0_attn_Wk': _L0_attn_in['Wk'], 'L0_attn_bk': _L0_attn_in['bk'], 'L0_attn_Wv': _L0_attn_in['Wv'], 'L0_attn_bv': _L0_attn_in['bv'], 'L0_attn_Wo': _L0_attn_in['Wo'], 'L0_attn_bo': _L0_attn_in['bo'], 'L0_attn_emb_rel_k': _L0_attn_in['emb_rel_k'], 'L0_attn_emb_rel_v': _L0_attn_in['emb_rel_v'], 'L0_ffn_w_gate_w': _L0_ffn_in['w_gate_w'], 'L0_ffn_w_gate_b': _L0_ffn_in['w_gate_b'], 'L0_ffn_W1': _L0_ffn_in['W1'], 'L0_ffn_b1': _L0_ffn_in['b1'], 'L0_ffn_W2': _L0_ffn_in['W2'], 'L0_ffn_b2': _L0_ffn_in['b2']}
    _x0 = _d['L0_attn_hidden_states']
    _d['L0_attn_hidden_states'] = jax.random.normal(jax.random.fold_in(jax.random.key(seed), 1), (8, 512, 128), dtype=_x0.dtype)
    del _x0
    return _d

def reference(L0_attn_hidden_states, L0_attn_Wq, L0_attn_bq, L0_attn_Wk, L0_attn_bk, L0_attn_Wv, L0_attn_bv, L0_attn_Wo, L0_attn_bo, L0_attn_emb_rel_k, L0_attn_emb_rel_v, L0_ffn_w_gate_w, L0_ffn_w_gate_b, L0_ffn_W1, L0_ffn_b1, L0_ffn_W2, L0_ffn_b2):

    def _L0_attn_ref(hidden_states, Wq, bq, Wk, bk, Wv, bv, Wo, bo, emb_rel_k, emb_rel_v):
        import jax, jax.numpy as jnp
        import numpy as np
        B, L, E, H, WINDOW = (4, 128, 128, 16, 4)
        D = E // H
        SCALING = D ** (-0.5)

        def _get_relative_embeddings(emb, length):
            pad_length = max(length - (WINDOW + 1), 0)
            if pad_length > 0:
                emb = jnp.pad(emb, ((0, 0), (pad_length, pad_length), (0, 0)))
            start = max(WINDOW + 1 - length, 0)
            return emb[:, start:start + 2 * length - 1]

        def _rel_to_abs(x):
            bh, length, _ = x.shape
            x = jnp.pad(x, ((0, 0), (0, 0), (0, 1)))
            xf = x.reshape(bh, length * 2 * length)
            xf = jnp.pad(xf, ((0, 0), (0, length - 1)))
            xfin = xf.reshape(bh, length + 1, 2 * length - 1)
            return xfin[:, :length, length - 1:]

        def _abs_to_rel(x):
            bh, length, _ = x.shape
            x = jnp.pad(x, ((0, 0), (0, 0), (0, length - 1)))
            xf = x.reshape(bh, length * (2 * length - 1))
            xf = jnp.pad(xf, ((0, 0), (length, 0)))
            xfin = xf.reshape(bh, length, 2 * length)
            return xfin[:, :, 1:]
        bsz, tgt_len, _ = hidden_states.shape

        def shape(t):
            return t.reshape(bsz, tgt_len, H, D).transpose(0, 2, 1, 3).reshape(bsz * H, tgt_len, D)
        q = shape((hidden_states @ Wq + bq) * SCALING)
        k = shape(hidden_states @ Wk + bk)
        v = shape(hidden_states @ Wv + bv)
        src_len = k.shape[1]
        attn_weights = jnp.einsum('btd,bsd->bts', q, k)
        rel_k = _get_relative_embeddings(emb_rel_k, src_len)
        rel_logits = jnp.einsum('btd,md->btm', q, rel_k[0])
        attn_weights = attn_weights + _rel_to_abs(rel_logits)
        attn_probs = jax.nn.softmax(attn_weights, axis=-1)
        attn_output = jnp.einsum('bts,bsd->btd', attn_probs, v)
        rel_v = _get_relative_embeddings(emb_rel_v, src_len)
        rel_weights = _abs_to_rel(attn_probs)
        attn_output = attn_output + jnp.einsum('btm,md->btd', rel_weights, rel_v[0])
        out = attn_output.reshape(bsz, H, tgt_len, D).transpose(0, 2, 1, 3).reshape(bsz, tgt_len, E)
        return out @ Wo + bo

    def _L0_ffn_ref(x, w_gate_w, w_gate_b, W1, b1, W2, b2):
        import jax, jax.numpy as jnp
        import numpy as np
        TOPK = 2
        CAPACITY_FACTOR = 1.0
        EPS = 1e-06
        B, S, D = (4, 512, 128)
        E = 8
        SUB_H = 256 // E
        Bx, Sx, Dx = x.shape
        Ex = w_gate_b.shape[0]
        K = Sx // 2
        capacity = int(CAPACITY_FACTOR * Bx)
        gate_scores = jax.nn.softmax(x @ w_gate_w + w_gate_b, axis=-1)
        _, top_idx = jax.lax.top_k(gate_scores, TOPK)
        mask = jax.nn.one_hot(top_idx, Ex, dtype=gate_scores.dtype).sum(axis=-2)
        masked = gate_scores * mask
        denom = masked.sum(axis=0, keepdims=True) + EPS
        route = masked / denom * capacity
        route_eb = jnp.transpose(route, (2, 0, 1))
        _, seq_ids = jax.lax.top_k(route_eb, K)
        seq_ids = jnp.sort(seq_ids, axis=-1)
        xg = jax.vmap(lambda idx: jnp.take_along_axis(x, idx[..., None], axis=1))(seq_ids)
        h = jnp.einsum('ebkd,edh->ebkh', xg, W1) + b1[:, None, None, :]
        h = jax.nn.gelu(h, approximate=False)
        o = jnp.einsum('ebkh,ehd->ebkd', h, W2) + b2[:, None, None, :]
        flat_ids = (jnp.arange(Bx)[None, :, None] * Sx + seq_ids).reshape(-1)
        outs = jnp.zeros((Bx * Sx, Dx), x.dtype).at[flat_ids].add(o.reshape(-1, Dx))
        return outs.reshape(Bx, Sx, Dx)
    x = L0_attn_hidden_states
    xn = _layernorm(x, axis=-1)
    x = x + _L0_attn_ref(xn, L0_attn_Wq, L0_attn_bq, L0_attn_Wk, L0_attn_bk, L0_attn_Wv, L0_attn_bv, L0_attn_Wo, L0_attn_bo, L0_attn_emb_rel_k, L0_attn_emb_rel_v) + _L0_ffn_ref(xn, L0_ffn_w_gate_w, L0_ffn_w_gate_b, L0_ffn_W1, L0_ffn_b1, L0_ffn_W2, L0_ffn_b2)
    return x

_drawn_inputs = setup_inputs


def setup_inputs(seed=0):
    import zlib

    import numpy as np

    out = dict(_drawn_inputs(seed))
    spreads = {'L0_attn_bq': (0.0, 0.799),
     'L0_attn_bk': (0.0, 2.0),
     'L0_attn_bv': (0.0, 0.1),
     'L0_attn_bo': (0.0, 0.1),
     'L0_ffn_w_gate_b': (0.0, 0.1),
     'L0_ffn_b1': (0.0, 0.705),
     'L0_ffn_b2': (0.0, 0.1)}
    factors = {'L0_attn_emb_rel_k': 8.0, 'L0_attn_emb_rel_v': 8.0, 'L0_ffn_W1': 3.023}
    for name, (base, spread) in spreads.items():
        noise = np.random.default_rng([zlib.crc32(name.encode()), seed]).standard_normal(out[name].shape)
        drawn = base * np.exp(spread * noise) if base else spread * noise
        out[name] = jnp.asarray(drawn.astype(out[name].dtype))
    for name, factor in factors.items():
        out[name] = (out[name] * factor).astype(out[name].dtype)
    return out
```

```python
import numpy as np
import concourse.bass as bass
from concourse import mybir
from contextlib import ExitStack

fp32 = mybir.dt.float32
bf16 = mybir.dt.bfloat16
int32 = mybir.dt.int32
ALU = mybir.AluOpType
ACT = mybir.ActivationFunctionType
AX = mybir.AxisListType

B, T, E, H = 8, 512, 128, 16
D = E // H
WINDOW = 4
J = 2 * WINDOW + 1
P = 128
TB = T // P
NEXP = 8
HID = 32
TOPK = 2
KEEP = T // 2
CAPACITY = float(B)
GATE_EPS = 1e-6
LN_EPS = 1e-5
SCALING = D ** -0.5
QUADS = 4
G = H // QUADS
UNITS = G * TB
NPROJ = 3 * E + NEXP
JH = J * H
PARTS = 3
QK_ROWS = 48
C_ROW = QK_ROWS
BAND = P + 2 * WINDOW
NEG = -1e30
VW = 32
SEARCH_BITS = 31


def build_program(nc, x_in, wcat_in, brow_in, bqk_in, wo_in, bo_in, ek_in, ev_in, w1_in, b1_in, w2_in, b2_in,
                  ident_in, band_in, edge_in, headmask_in, relmask_in, earlier_in, batchmask_in, out):
    ctx = ExitStack()
    with ctx:
        def sb(name, shape, dt=fp32):
            return ctx.enter_context(nc.sbuf_tensor(name, shape, dt))

        def sem(name):
            return ctx.enter_context(nc.semaphore(name))

        def dram(name, shape, dt=fp32):
            return nc.dram_tensor(name, shape, dt, kind="Internal").ap()

        k_rows = dram("k_rows", [B, T + 2 * WINDOW, E])
        v_rows = dram("v_rows", [B, T + 2 * WINDOW, E])
        q_parts_dram = dram("q_parts_dram", [B, PARTS, D, H, T], bf16)
        xnT_dram = dram("xnT_dram", [B, P, T])
        k_parts_dram = dram("k_parts_dram", [B, PARTS, D, H, T], bf16)

        ident = sb("ident", [P, P])
        ident_b = sb("ident_b", [P, P], bf16)
        band_f = sb("band_f", [P, BAND])
        band_b = sb("band_b", [P, BAND], bf16)
        edge = sb("edge", [P, 2, JH])
        headmask = sb("headmask", [P, H])
        relmask = sb("relmask", [P, H])
        earlier = sb("earlier", [P, NEXP * NEXP])
        batchmask = sb("batchmask", [P, B])
        wcat = sb("wcat", [P, NPROJ])
        brow_parts = sb("brow_parts", [P, NPROJ + E], bf16)
        ones_rows = sb("ones_rows", [P, P], bf16)
        bqk = sb("bqk", [P, 2])
        wo = sb("wo", [P, E])
        ek = sb("ek", [P, J])
        ev0 = sb("ev0", [P, D])
        ev1 = sb("ev1", [H, D])
        ek_block = sb("ek_block", [P, J, H])
        ev_block0 = sb("ev_block0", [P, H, D])
        ev_block1 = sb("ev_block1", [H, H, D])
        w1 = sb("w1", [P, NEXP * HID])
        b1 = sb("b1", [P, 2])
        w2 = sb("w2", [P, 2, E])
        b2 = sb("b2", [P, E])
        b2_rest = sb("b2_rest", [P, E])
        b2_parts = sb("b2_parts", [P, PARTS, E], bf16)
        zero_rows = sb("zero_rows", [2, G * T], bf16)
        one_col = sb("one_col", [P, 1])
        minus_half = sb("minus_half", [P, B * TB])

        x_all = sb("x_all", [P, B, TB, E])
        stats = sb("stats", [P, B * TB, 6])
        mean_var = sb("mean_var", [P, B * TB, 2])
        var_eps = sb("var_eps", [P, B * TB])
        rstd = sb("rstd", [P, B * TB])
        shift = sb("shift", [P, B * TB])
        gates = sb("gates", [P, TB, B, NEXP])

        xn = sb("xn", [P, TB, E])
        xnT = sb("xnT", [P, T])
        nat = sb("nat", [P, TB, NPROJ])
        qT = sb("qT", [P, T])
        kT = sb("kT", [P, T])
        rest1 = sb("rest1", [P, T])
        q_parts = sb("q_parts", [P, PARTS, T], bf16)
        k_parts = sb("k_parts", [P, PARTS, T], bf16)
        Q = sb("Q", [P, QUADS, G, T], bf16)
        K = sb("K", [P, QUADS, G, T], bf16)
        vaug = sb("vaug", [P, QUADS, TB, G, D + 1])

        k_near = sb("k_near", [P, TB, J * E])
        v_near = sb("v_near", [P, TB, J * E])
        qk_prod = sb("qk_prod", [P, 2, J * E])
        pv_prod = sb("pv_prod", [P, J, E])
        near_qk = sb("near_qk", [P, JH])
        rel = sb("rel", [P, TB, JH])
        near = sb("near", [P, TB, J, H])
        near_p = sb("near_p", [P, TB, J, H])
        near_pT = sb("near_pT", [P, 2, 2, P])
        near_ev = sb("near_ev", [P, TB, E])
        near_v = sb("near_v", [P, TB, E])
        near_den = sb("near_den", [P, TB, H])

        neg_max = sb("neg_max", [P, G, TB])
        neg_near = sb("neg_near", [P, TB, G])
        neg_c = sb("neg_c", [P, G, TB])
        c_parts = sb("c_parts", [P, 2, G, TB], bf16)
        c_used = sb("c_used", [P, TB, H])
        cT = sb("cT", [2 * UNITS, P], bf16)
        PT = sb("PT", [P, TB, G, T])
        pvT = sb("pvT", [P, T])
        o_raw = sb("o_raw", [P, TB, H, D + 1])
        den = sb("den", [P, TB, H])
        rden = sb("rden", [P, TB, H])
        o_nat = sb("o_nat", [P, TB, E])
        oT = sb("oT", [P, T])

        s_bank = [ctx.enter_context(nc.psum_tensor(f"s_bank{i}", [P, T], fp32)) for i in range(2)]
        st_bank = [ctx.enter_context(nc.psum_tensor(f"st_bank{i}", [P, T], fp32)) for i in range(2)]
        pv_bank = ctx.enter_context(nc.psum_tensor("pv_bank", [P, T], fp32))
        m0 = ctx.enter_context(nc.psum_tensor("m0", [P, T], fp32))
        m1 = ctx.enter_context(nc.psum_tensor("m1", [P, T], fp32))
        m2 = ctx.enter_context(nc.psum_tensor("m2", [P, T], fp32))
        m0_b = m0[:, :].bitcast(bf16)

        PT_flat = PT[:, :, :, :].rearrange("p a g t -> p (a g t)")
        one_rows = PT_flat[0:2, 0:QUADS * G * T // 2].bitcast(bf16)
        zero_pad = PT_flat[0:WINDOW, 4096:4096 + B * E].rearrange("p (b e) -> p b e", e=E)
        brow = PT_flat[0:PARTS, 6144:6144 + NPROJ + E]

        xnT_all = Q[:, :, :, :].rearrange("p q g t -> p (q g t)").bitcast(fp32).rearrange("p (b t) -> p b t", t=T)
        b2_rows = K[:, :, :, :].rearrange("p q g t -> p (q g t)")[:, 0:B * PARTS * E].rearrange("p (b i e) -> p b i e", i=PARTS, e=E)
        g_hid = PT[:, :, :, :].rearrange("p a g t -> p (a g t)")[:, 0:4 * T].rearrange("p (i c t) -> p i c t", i=2, c=2)
        ffn_out = PT[:, :, :, :].rearrange("p a g t -> p (a g t)")[:, 4 * T:6 * T].rearrange("p (i n) -> p i n", i=2)
        gtmp = k_near[:, :, :].rearrange("p a n -> p (a n)")
        g_max = gtmp[:, 0:32]
        g_exp = gtmp[:, 32:288].rearrange("p (n e) -> p n e", e=NEXP)
        g_sum = gtmp[:, 288:320]
        g_cnt = gtmp[:, 320:576].rearrange("p (n e) -> p n e", e=NEXP)
        g_den = gtmp[:, 576:608].rearrange("p (t e) -> p t e", e=NEXP)
        expert_rows = gtmp[:, 3200:3200 + B * NEXP * HID // 2].bitcast(bf16).rearrange("p (n h) -> p n h", h=HID)
        route = gtmp[:, 640:896].rearrange("p (t n) -> p t n", t=TB)
        score = gtmp[:, 896:1152].rearrange("p (n e) -> p n e", e=NEXP)
        pair_gt = qk_prod[:, :, :].rearrange("p a n -> p (a n)")[:, 0:2048].rearrange("p (n e f) -> p n e f", e=NEXP, f=NEXP)
        pair_eq = gtmp[:, 1152:3200].rearrange("p (n e f) -> p n e f", e=NEXP, f=NEXP)
        SROW = B * NEXP
        srow = v_near[0:SROW, :, :].rearrange("p a n -> p (a n)")
        route_rows = srow[:, 0:T]
        above = srow[:, T:2 * T]
        equal = srow[:, 2 * T:3 * T]
        ones_t = srow[:, 3 * T:4 * T]
        order = srow[:, 4 * T:5 * T]
        picked = srow[:, 5 * T:6 * T]
        small = sb("small", [SROW, 8])
        cand = sb("cand", [SROW, 1], int32)
        drop = sb("drop", [SROW, 1], int32)
        sel = sb("sel", [P, T], bf16)
        sel_m1 = sb("sel_m1", [P, T], bf16)

        names = ("x0_in x_rest_in weights_in consts_ready pads_written ones_in zeros_ready setup_dve setup_pool bias_ready "
                 "stats0_ready stats_ready eps0_ready eps_ready pow0_ready pow_ready "
                 "xn_ready xnT_ps xnT_ready xnT_saved xnT_back pv_clear nat_ps nat_ready qkT_ps qkT_ready split_ready parts_saved kv_saved "
                 "k_near_in v_near_in qk_prod_ready near_qk_ready rel_ps rel_ready near_ready gates_ready vaug_ready "
                 "st_ps exp_ready s_ps max_ready pv_ps pvT_ready o_ps o_raw_ready c_ready cT_ps cT_ready "
                 "near_c_ready near_p_ready near_pT_ps near_pT_ready ev_ps near_ev_ready near_v_ready near_den_ready "
                 "o_ready oT_ps oT_ready wo_ps x_res_ready dve_step pool_step "
                 "g_shift_ready g_exp_ready route_ready route_ps sel_ready h_ps g_ready y_ps ffn_ready out_even out_odd").split()
        S = {n: sem(n) for n in names}
        packed = [sem(f"packed{q}") for q in range(QUADS)]
        c_rows_in = [sem(f"c_rows_in{q}") for q in range(QUADS)]
        PACK_DMAS = 10

        block = ctx.enter_context(nc.Block())

        def wait(eng, s, value):
            if isinstance(value, int) and value <= 0:
                return
            eng.wait_ge(s, value)

        class Steps:

            def __init__(self, eng, s):
                self.eng, self.s, self.n = eng, s, 0

            def did(self, ins):
                ins.then_inc(self.s, 1)
                self.n = self.n + 1

            def settle(self):
                self.eng.wait_ge(self.s, self.n)

        def at(b):
            return slice(b, b + 1) if isinstance(b, int) else bass.ds(b, 1)

        def span(start, size):
            return slice(start, start + size) if isinstance(start, int) else bass.ds(start, size)

        def band_columns(blk):
            lo, hi = max(0, blk * P - WINDOW), min(T, (blk + 1) * P + WINDOW)
            m = lo - (blk * P - WINDOW)
            return slice(lo, hi), slice(m, m + hi - lo)

        @block.sync
        def _(sp):
            def load(dst, src, s):
                sp.dma_start(dst, src).then_inc(S[s], 16)

            xv = x_in.rearrange("b (n p) e -> b p n e", p=P)
            load(x_all[:, 0, :, :], xv[0], "x0_in")
            for dst, src in ((ident, ident_in), (wcat, wcat_in), (bqk, bqk_in), (headmask, headmask_in),
                             (relmask, relmask_in), (ek, ek_in), (ev0, ev_in[0:P]), (ev1, ev_in[P:JH]), (band_f, band_in),
                             (wo, wo_in), (w1, w1_in), (b1, b1_in), (b2, b2_in), (earlier, earlier_in),
                             (batchmask, batchmask_in)):
                load(dst[:, :], src, "weights_in")
            load(edge[:, :, :], edge_in, "weights_in")
            load(w2[:, :, :], w2_in, "weights_in")
            load(brow, brow_in, "weights_in")
            for b in range(1, B):
                load(x_all[:, b, :, :], xv[b], "x_rest_in")
            sp.wait_ge(S["zeros_ready"], 5)
            for rows in (k_rows, v_rows):
                for first in (0, T + WINDOW):
                    load(rows[:, first:first + WINDOW, :].rearrange("b w e -> w b e"), zero_pad, "pads_written")
            load(K[C_ROW:C_ROW + 2, :, :, :].rearrange("p q g t -> p (q g t)"), one_rows, "ones_in")

            def line(b, per, off=0):
                return b[0] * per + (per * b[1] + off)

            def after(b, n=1):
                return (b[0], b[1] + n)

            def part(tensor, b, start=0, size=None):
                names = " ".join("abcdef"[:len(tensor.shape)])
                per = int(np.prod(tensor.shape[1:]))
                size = per if size is None else size
                flat = tensor.rearrange(f"{names} -> ({names})")
                at_ = line(b, per, start)
                return flat[at_:at_ + size] if isinstance(at_, int) else flat[bass.ds(at_, size)]

            def sp_wait(s, value):
                wait(sp, s, value)

            def save_xnT(b):
                sp_wait(S["xnT_ready"], line(b, 1, 1))
                sp.dma_start(part(xnT_dram, b).rearrange("(p t) -> p t", t=T), xnT[:, :]).then_inc(S["xnT_saved"], 16)

            def save_kv(b):
                sp_wait(S["nat_ready"], line(b, TB, TB))
                for rows, c in ((k_rows, E), (v_rows, 2 * E)):
                    dst = part(rows, b, WINDOW * E, T * E).rearrange("(n p e) -> p n e", p=P, e=E)
                    sp.dma_start(dst, nat[:, :, c:c + E]).then_inc(S["kv_saved"], 16)

            def windows(rows, b):
                v = part(rows, b, 0, T * E).rearrange("(n p e) -> p n e", p=P, e=E)
                return bass.AP(tensor=v.tensor, offset=v.offset, ap=[list(v.ap[0]), list(v.ap[1]), [1, J * E]])

            def load_k_near(b):
                sp_wait(S["kv_saved"], line(b, 32, 32))
                sp.dma_start(k_near[:, :, :], windows(k_rows, b)).then_inc(S["k_near_in"], 16)

            def load_v_near(b):
                sp_wait(S["near_v_ready"], line(b, TB))
                sp.dma_start(v_near[:, :, :], windows(v_rows, b)).then_inc(S["v_near_in"], 16)

            def save_parts(b):
                for n, (dst, src) in enumerate(((q_parts_dram, q_parts), (k_parts_dram, k_parts))):
                    sp_wait(S["split_ready"], line(b, 2, n + 1))
                    for i in range(PARTS):
                        d = part(dst, b, i * E * T, E * T).rearrange("(d h t) -> h d t", h=H, t=T)
                        sp.dma_start(d, src[:, i, :]).then_inc(S["parts_saved"], 16)

            def pack(b, q, free):
                sp_wait(S["st_ps"], free)
                sp.dma_start(Q[C_ROW:C_ROW + 2, q, :, :].rearrange("p g t -> p (g t)"), zero_rows[:, :]).then_inc(packed[q], 16)
                sp_wait(S["parts_saved"], line(b, 16 * 2 * PARTS, 16 * 2 * PARTS))
                hs = slice(q * G, q * G + G)
                row = 0
                for n in (3, 2, 1):
                    src = part(q_parts_dram, b, 0, n * E * T).rearrange("(i h t) -> i h t", h=H, t=T)
                    sp.dma_start(Q[row:row + n * D, q, :, :], src[:, hs, :]).then_inc(packed[q], 16)
                    src = part(k_parts_dram, b, (PARTS - n) * E * T, E * T).rearrange("(i h t) -> i h t", h=H, t=T)
                    for r in range(n):
                        sp.dma_start(K[row + r * D:row + (r + 1) * D, q, :, :], src[:, hs, :]).then_inc(packed[q], 16)
                    row += n * D

            def c_rows(b, q):
                sp_wait(S["cT_ready"], line(b, QUADS, q + 1))
                sp.dma_start(Q[C_ROW:C_ROW + 2, q, :, :], cT[:, :]).then_inc(c_rows_in[q], 16)

            zero = (0, 0)
            sp_wait(S["pads_written"], 64)
            save_xnT(zero)
            save_kv(zero)
            load_k_near(zero)
            save_parts(zero)
            sp_wait(S["zeros_ready"], 5)
            for q in range(3):
                pack(zero, q, 0)
            load_v_near(zero)
            c_rows(zero, 0)

            def body(b, first, last):
                units = QUADS * UNITS
                nxt = after(b)
                if not first:
                    load_v_near(b)
                pack(b, 3, line(b, units))
                if not last:
                    save_xnT(nxt)
                    save_kv(nxt)
                    load_k_near(nxt)
                c_rows(b, 1)
                if not last:
                    save_parts(nxt)
                    pack(nxt, 0, line(b, units, UNITS))
                c_rows(b, 2)
                if not last:
                    pack(nxt, 1, line(b, units, 2 * UNITS))
                c_rows(b, 3)
                if not last:
                    pack(nxt, 2, line(b, units, 3 * UNITS))
                    c_rows(nxt, 0)
                if last:
                    sp_wait(S["xnT_saved"], 16 * B)
                    for q in range(QUADS):
                        sp_wait(S["st_ps"], line(b, units, UNITS * (q + 1)))
                        sp.dma_start(xnT_all[:, 2 * q:2 * q + 2, :],
                                     xnT_dram[2 * q:2 * q + 2].rearrange("b p t -> p b t")).then_inc(S["xnT_back"], 16)

            body((0, 0), True, False)
            with sp.Fori(0, B - 2) as i:
                body((i, 1), False, False)
            body((0, B - 1), False, True)

            ov = out.rearrange("b (n p) e -> b p n e", p=P)
            with sp.Fori(0, B // 2) as i:
                for half, s in enumerate(("out_even", "out_odd")):
                    sp_wait(S["ffn_ready"], 2 * i + half + 1)
                    dst = ov[at(2 * i + half), :, :, :].rearrange("o p n e -> p (o n) e")
                    sp.dma_start(dst, ffn_out[:, half, :].rearrange("p (n e) -> p n e", e=E)).then_inc(S[s], 16)
            sp_wait(S["out_even"], 16 * B // 2)
            sp_wait(S["out_odd"], 16 * B // 2)

        @block.tensor
        def _(pe):
            def transposes_xn(b, bank_free):
                bank_free()
                pe.wait_ge(S["xn_ready"], TB * (b + 1))
                for n in range(TB):
                    ins = pe.transpose(m1[:, n * P:(n + 1) * P], xn[:, n, :], ident[:, :])
                ins.then_inc(S["xnT_ps"], 1)

            def project(b, n):
                bank = (m1, m2)[n % 2]
                pe.wait_ge(S["xnT_ready"], b + 1)
                if n >= 2:
                    pe.wait_ge(S["nat_ready"], TB * b + n - 1)
                pe.matmul(bank[:, 0:NPROJ], xnT[:, n * P:(n + 1) * P], wcat[:, :], start=True, stop=False)
                pe.matmul(bank[:, 0:NPROJ], ones_rows[:, :], brow_parts[:, 0:NPROJ], start=False, stop=True)\
                    .then_inc(S["nat_ps"], 1)

            def project_T(b, n):
                pe.wait_ge(S["nat_ready"], TB * b + 3 + n)
                pe.matmul((m1, m2)[n][:, :], wcat[:, n * E:(n + 1) * E], xnT[:, :], start=True, stop=True)\
                    .then_inc(S["qkT_ps"], 1)

            def relative(b, n):
                bank = (m1, m2)[n % 2]
                if n < 2:
                    pe.wait_ge(S["qkT_ready"], 2 * b + n + 1)
                else:
                    pe.wait_ge(S["rel_ready"], TB * b + n - 1)
                at_edge = n in (0, TB - 1)
                ins = pe.matmul(bank[:, 0:JH], qT[:, n * P:(n + 1) * P], ek_block[:, :, :].rearrange("p j h -> p (j h)"),
                                start=True, stop=not at_edge)
                if at_edge:
                    ins = pe.matmul(bank[:, 0:JH], ident[:, :], edge[:, n // (TB - 1), :], start=False, stop=True)
                ins.then_inc(S["rel_ps"], 1)

            def s_unit(b, q, u):
                if u == 0:
                    pe.wait_ge(packed[q], 16 * PACK_DMAS * (b + 1))
                done = QUADS * UNITS * b + UNITS * q + u
                wait(pe, S["max_ready"], done - 1)
                g, n = u // TB, u % TB
                bank = s_bank[u % 2]
                pe.matmul(bank[:, :], Q[:, q, g, n * P:(n + 1) * P], K[:, q, g, :], start=True, stop=True)
                cols, mask = band_columns(n)
                pe.matmul(bank[:, cols], ident_b[:, :], band_b[:, mask], start=False, stop=True,
                          skip_group_check=True).then_inc(S["s_ps"], 1)

            def st_unit(b, q, u):
                if u == 0:
                    pe.wait_ge(c_rows_in[q], 16 * (b + 1))
                done = QUADS * UNITS * b + UNITS * q + u
                wait(pe, S["exp_ready"], done - 1)
                n, g = u // G, u % G
                bank = st_bank[u % 2]
                pe.matmul(bank[:, :], K[:, q, g, n * P:(n + 1) * P], Q[:, q, g, :], start=True, stop=True)
                cols, mask = band_columns(n)
                pe.matmul(bank[:, cols], ident_b[:, :], band_b[:, mask], start=False, stop=True,
                          skip_group_check=True).then_inc(S["st_ps"], 1)

            def pv(b, q, n):
                pe.wait_ge(S["exp_ready"], QUADS * UNITS * b + UNITS * q + G * (n + 1))
                if n == 0:
                    pe.wait_ge(S["vaug_ready"], QUADS * b + q + 1)
                    wait(pe, S["pvT_ready"], QUADS * b + q)
                    if isinstance(b, int) and b == 0 and q == 0:
                        pe.wait_ge(S["pv_clear"], 1)
                for g in range(G):
                    ins = pe.matmul(pv_bank[VW * g:VW * g + D + 1, :], vaug[:, q, n, g, :], PT[:, n, g, :],
                                    start=(n == 0), stop=(n == TB - 1))
                ins.then_inc(S["pv_ps"], 1)

            def transpose_o(b, q):
                pe.wait_ge(S["pvT_ready"], QUADS * b + q + 1)
                wait(pe, S["cT_ready"], QUADS * b + q + 2)
                for n in range(TB):
                    ins = pe.transpose(m0[:, n * P:(n + 1) * P], pvT[:, n * P:(n + 1) * P], ident[:, :])
                ins.then_inc(S["o_ps"], 1)

            def transpose_c(b, q):
                pe.wait_ge(S["c_ready"], QUADS * b + q + 1)
                wait(pe, S["o_raw_ready"], QUADS * b + q - 1)
                pe.transpose(m0_b[0:2 * UNITS, 0:P], c_parts[:, :, :, :].rearrange("p i g n -> p (i g n)"),
                             ident_b[:, :]).then_inc(S["cT_ps"], 1)

            def near_transposes(b, n, bank_free=None):
                if bank_free is not None:
                    bank_free()
                else:
                    pe.wait_ge(S["near_pT_ready"], TB * b + n)
                pe.wait_ge(S["near_p_ready"], b + 1)
                flat = near_p[:, n, :, :].rearrange("p j h -> p (j h)")
                pe.transpose(m1[:, 0:P], flat[:, 0:P], ident[:, :])
                pe.transpose(m1[0:H, P:2 * P], flat[:, P:JH], ident[:, :]).then_inc(S["near_pT_ps"], 1)

            def near_times_ev(b, n, bank_free=None):
                if bank_free is not None:
                    bank_free()
                pe.wait_ge(S["near_pT_ready"], TB * b + n + 1)
                cols = slice(n * P, (n + 1) * P)
                pe.matmul(m2[:, cols], near_pT[:, n % 2, 0, :], ev_block0[:, :, :].rearrange("p h d -> p (h d)"),
                          start=True, stop=False)
                ins = pe.matmul(m2[:, cols], near_pT[0:H, n % 2, 1, :], ev_block1[:, :, :].rearrange("p h d -> p (h d)"),
                                start=False, stop=True)
                ins.then_inc(S["ev_ps"], 1)

            def transpose_attn(b, bank_free):
                bank_free()
                pe.wait_ge(S["o_ready"], b + 1)
                for n in range(TB):
                    ins = pe.transpose(m1[:, n * P:(n + 1) * P], o_nat[:, n, :], ident[:, :])
                ins.then_inc(S["oT_ps"], 1)

            def project_out(b, bank_free):
                bank_free()
                pe.wait_ge(S["oT_ready"], b + 1)
                for n in range(TB):
                    cols = slice(n * P, (n + 1) * P)
                    pe.matmul(m2[:, cols], oT[:, cols], wo[:, :], start=True, stop=False)
                    ins = pe.matmul(m2[:, cols], ones_rows[:, :], brow_parts[:, NPROJ:NPROJ + E], start=False, stop=True)
                ins.then_inc(S["wo_ps"], 1)

            pe.wait_ge(S["weights_in"], 16 * 18)
            pe.wait_ge(S["setup_dve"], 1)
            transposes_xn(0, lambda: None)
            pe.wait_ge(S["bias_ready"], 1)
            for n in range(TB):
                project(0, n)
            for n in range(2):
                project_T(0, n)
            for n in range(TB):
                relative(0, n)
            pe.wait_ge(S["ones_in"], 16)
            for q in range(2):
                for u in range(UNITS):
                    s_unit(0, q, u)
                if q == 0:
                    transpose_c(0, 0)

            def body(b, last):
                first = isinstance(b, int) and b == 0
                m1_after_near = lambda: wait(pe, S["near_pT_ready"], TB * b)
                for q in range(QUADS):
                    for u in range(UNITS):
                        st_unit(b, q, u)
                        if u % G == 1:
                            if u >= G:
                                pv(b, q, u // G - 1)
                            elif q > 0:
                                pv(b, q - 1, TB - 1)
                            elif not first:
                                pv(b - 1, QUADS - 1, TB - 1)
                        if q < 2:
                            s_unit(b, q + 2, u)
                        elif not last:
                            s_unit(b + 1, q - 2, u)
                        if u == 6:
                            if q > 0:
                                transpose_o(b, q - 1)
                            elif not first:
                                transpose_o(b - 1, QUADS - 1)
                        if u == 14:
                            if q < QUADS - 1:
                                transpose_c(b, q + 1)
                            elif not last:
                                transpose_c(b + 1, 0)
                        if q == 0 and not last:
                            if u == 5:
                                transposes_xn(b + 1, m1_after_near)
                            if 8 <= u < 12:
                                if u == 9:
                                    wait(pe, S["near_ev_ready"], b)
                                project(b + 1, u - 8)
                            if u in (12, 13):
                                project_T(b + 1, u - 12)
                        if q == 1:
                            if not last and u in (3, 4, 7, 8):
                                relative(b + 1, (3, 4, 7, 8).index(u))
                            if not first and u == 10:
                                transpose_attn(b - 1, m1_after_near if last else
                                               lambda: pe.wait_ge(S["rel_ready"], TB * (b + 1) + 3))
                            if not first and u == 13:
                                project_out(b - 1, (lambda: pe.wait_ge(S["near_ev_ready"], b)) if last else
                                            (lambda: pe.wait_ge(S["rel_ready"], TB * (b + 1) + 4)))
                        if q == 3:
                            if u in (2, 4, 7, 9):
                                n = (2, 4, 7, 9).index(u)
                                near_transposes(b, n, None if n else
                                                (lambda: pe.wait_ge(S["rel_ready"], TB + 3)) if first else
                                                (lambda: pe.wait_ge(S["oT_ready"], b)))
                            if u in (5, 8, 10, 12):
                                n = (5, 8, 10, 12).index(u)
                                near_times_ev(b, n, None if n else
                                              (lambda: pe.wait_ge(S["rel_ready"], TB + 4)) if first else
                                              (lambda: pe.wait_ge(S["x_res_ready"], b)))
                    if last and q == 2:
                        pe.wait_ge(S["route_ready"], 1)
                        for n in range(TB):
                            ins = pe.transpose(s_bank[0][0:B * NEXP, n * P:(n + 1) * P], route[:, n, :], ident[:, :])
                        ins.then_inc(S["route_ps"], 1)

            body(0, False)
            with pe.Fori(1, B - 1) as b:
                body(b, False)
            body(B - 1, True)
            pv(B - 1, QUADS - 1, TB - 1)
            pe.wait_ge(S["pvT_ready"], QUADS * B)
            pe.wait_ge(S["o_raw_ready"], QUADS * B - 1)
            for n in range(TB):
                ins = pe.transpose(m0[:, n * P:(n + 1) * P], pvT[:, n * P:(n + 1) * P], ident[:, :])
            ins.then_inc(S["o_ps"], 1)
            transpose_attn(B - 1, lambda: pe.wait_ge(S["near_pT_ready"], TB * B))
            project_out(B - 1, lambda: pe.wait_ge(S["near_ev_ready"], B))

            pe.wait_ge(S["xnT_back"], 16 * QUADS)
            pe.wait_ge(S["sel_ready"], 1)
            pe.wait_ge(S["x_res_ready"], B)
            h_bank = (st_bank[0], st_bank[1], s_bank[0], s_bank[1])
            y_bank = (m1, m2)

            def ffn(i):
                for half in range(2):
                    for c in range(2):
                        bank = h_bank[2 * half + c]
                        pe.matmul(bank[:, :], w1[:, c * P:(c + 1) * P],
                                  xnT_all[:, at(2 * i + half), :].rearrange("p o t -> p (o t)"), start=True, stop=False)
                        rows = expert_rows[:, span((2 * i + half) * NEXP + 4 * c, 4), :].rearrange("p e h -> p (e h)")
                        pe.matmul(bank[:, :], rows, sel_m1[:, :], start=False, stop=True).then_inc(S["h_ps"], 1)
                for half in range(2):
                    pe.wait_ge(S["g_ready"], 4 * i + 2 * half + 2)
                    for n in range(TB):
                        cols = slice(n * P, (n + 1) * P)
                        for c in range(2):
                            pe.matmul(y_bank[half][:, cols], g_hid[:, half, c, cols], w2[:, c, :],
                                      start=(c == 0), stop=False)
                        for k in range(PARTS):
                            ins = pe.matmul(y_bank[half][:, cols], sel[:, cols],
                                            b2_rows[:, at(2 * i + half), k, :].rearrange("p o e -> p (o e)"),
                                            start=False, stop=(k == PARTS - 1))
                    ins.then_inc(S["y_ps"], 1)
                pe.wait_ge(S["ffn_ready"], 2 * i + 2)

            ffn(0)
            with pe.Fori(1, B // 2) as i:
                ffn(i)

        @block.scalar
        def _(act):
            def normalize(b):
                wait(act, S["xnT_ps"], b)
                for n in range(TB):
                    c = b * TB + n
                    col = slice(c, c + 1) if isinstance(c, int) else bass.ds(c, 1)
                    act.activation(xn[:, n, :], x_all[:, at(b), n, :].rearrange("p o e -> p (o e)"), ACT.Identity,
                                   bias=shift[:, col], scale=rstd[:, col]).then_inc(S["xn_ready"], 1)

            def copy_xnT(b):
                act.wait_ge(S["xnT_ps"], b + 1)
                wait(act, S["xnT_saved"], 16 * b)
                act.activation(xnT[:, :], m1[:, :], ACT.Copy).then_inc(S["xnT_ready"], 1)

            def copy_nat(b, n):
                act.wait_ge(S["nat_ps"], TB * b + n + 1)
                if n == 0:
                    wait(act, S["kv_saved"], 32 * b)
                    wait(act, S["qk_prod_ready"], TB * b)
                    wait(act, S["vaug_ready"], QUADS * b)
                    wait(act, S["gates_ready"], b)
                act.activation(nat[:, n, :], (m1, m2)[n % 2][:, 0:NPROJ], ACT.Copy).then_inc(S["nat_ready"], 1)

            def copy_qkT(b, n):
                act.wait_ge(S["qkT_ps"], 2 * b + n + 1)
                wait(act, S["split_ready"], 2 * b - 1 + n)
                wait(act, S["parts_saved"], 16 * 2 * PARTS * b)
                act.activation((q_parts, k_parts)[n][:, 0, :], (m1, m2)[n][:, :], ACT.Identity, bias=bqk[:, n:n + 1])
                act.activation((qT, kT)[n][:, :], (m1, m2)[n][:, :], ACT.Identity, bias=bqk[:, n:n + 1])\
                    .then_inc(S["qkT_ready"], 1)

            def copy_rel(b, n):
                act.wait_ge(S["rel_ps"], TB * b + n + 1)
                if n == 0:
                    wait(act, S["near_ready"], TB * b)
                act.activation(rel[:, n, :], (m1, m2)[n % 2][:, 0:JH], ACT.Copy).then_inc(S["rel_ready"], 1)

            def exp_unit(b, q, u):
                done = QUADS * UNITS * b + UNITS * q + u
                act.wait_ge(S["st_ps"], done + 1)
                n, g = u // G, u % G
                if g == 0:
                    wait(act, S["pv_ps"], QUADS * TB * b + TB * q + n - TB + 1)
                act.activation(PT[:, n, g, :], st_bank[u % 2][:, :], ACT.Exp).then_inc(S["exp_ready"], 1)

            def copy_pv(b, q):
                act.wait_ge(S["pv_ps"], QUADS * TB * b + TB * (q + 1))
                wait(act, S["o_ps"], QUADS * b + q)
                act.activation(pvT[:, :], pv_bank[:, :], ACT.Copy).then_inc(S["pvT_ready"], 1)

            def copy_c(b, q):
                act.wait_ge(S["cT_ps"], QUADS * b + q + 1)
                if q > 0:
                    act.wait_ge(c_rows_in[q - 1], 16 * (b + 1))
                elif not (isinstance(b, int) and b == 0):
                    act.wait_ge(c_rows_in[QUADS - 1], 16 * b)
                act.activation(cT[:, :], m0_b[0:2 * UNITS, 0:P], ACT.Copy).then_inc(S["cT_ready"], 1)

            def near_exp(b):
                act.wait_ge(S["near_c_ready"], b + 1)
                wait(act, S["near_pT_ps"], TB * b)
                wait(act, S["near_v_ready"], TB * b)
                wait(act, S["near_den_ready"], b)
                act.activation(near_p[:, :, :, :].rearrange("p n j h -> p (n j h)"),
                               near_p[:, :, :, :].rearrange("p n j h -> p (n j h)"), ACT.Exp).then_inc(S["near_p_ready"], 1)

            def copy_near_pT(b, n):
                act.wait_ge(S["near_pT_ps"], TB * b + n + 1)
                wait(act, S["ev_ps"], TB * b + n - 1)
                act.activation(near_pT[:, n % 2, 0, :], m1[:, 0:P], ACT.Copy)
                act.activation(near_pT[0:H, n % 2, 1, :], m1[0:H, P:2 * P], ACT.Copy).then_inc(S["near_pT_ready"], 1)

            def copy_ev(b):
                act.wait_ge(S["ev_ps"], TB * (b + 1))
                wait(act, S["near_v_ready"], TB * b)
                act.activation(near_ev[:, :, :].rearrange("p n e -> p (n e)"), m2[:, :], ACT.Copy)\
                    .then_inc(S["near_ev_ready"], 1)

            def copy_oT(b):
                act.wait_ge(S["oT_ps"], b + 1)
                wait(act, S["wo_ps"], b)
                act.activation(oT[:, :], m1[:, :], ACT.Copy).then_inc(S["oT_ready"], 1)

            act.wait_ge(S["stats0_ready"], 1)
            act.wait_ge(S["weights_in"], 16 * 18)
            normalize(0)
            copy_xnT(0)
            for n in range(TB):
                copy_nat(0, n)
            act.wait_ge(S["bias_ready"], 1)
            for n in range(2):
                copy_qkT(0, n)
            for n in range(TB):
                copy_rel(0, n)
            copy_c(0, 0)
            act.wait_ge(S["stats_ready"], 1)

            def body(b, last):
                first = isinstance(b, int) and b == 0
                for q in range(QUADS):
                    for u in range(UNITS):
                        exp_unit(b, q, u)
                        if u == 3:
                            if q > 0:
                                copy_pv(b, q - 1)
                            elif not first:
                                copy_pv(b - 1, QUADS - 1)
                        if u == UNITS - 1:
                            if q < QUADS - 1:
                                copy_c(b, q + 1)
                            elif not last:
                                copy_c(b + 1, 0)
                        if q == 0 and not last:
                            if u == 0:
                                normalize(b + 1)
                            if u == 5:
                                copy_xnT(b + 1)
                            if 8 <= u < 12:
                                copy_nat(b + 1, u - 8)
                            if u in (12, 13):
                                copy_qkT(b + 1, u - 12)
                        if q == 1:
                            if not last and u in (3, 4, 7, 8):
                                copy_rel(b + 1, (3, 4, 7, 8).index(u))
                            if not first and u == 10:
                                copy_oT(b - 1)
                        if q == 2 and u == 4:
                            near_exp(b)
                        if last and q == 2 and u == 0:
                            act.wait_ge(S["g_shift_ready"], 1)
                            act.activation(g_exp, g_exp, ACT.Exp).then_inc(S["g_exp_ready"], 1)
                        if q == 3:
                            if u in (2, 4, 7, 9):
                                copy_near_pT(b, (2, 4, 7, 9).index(u))
                            if u == 12:
                                copy_ev(b)

            body(0, False)
            with act.Fori(1, B - 1) as b:
                body(b, False)
            body(B - 1, True)
            copy_pv(B - 1, QUADS - 1)
            copy_oT(B - 1)

            def ffn(i):
                for half in range(2):
                    for c in range(2):
                        act.wait_ge(S["h_ps"], 4 * i + 2 * half + c + 1)
                        wait(act, S["y_ps"], 2 * i)
                        bank = (st_bank[0], st_bank[1], s_bank[0], s_bank[1])[2 * half + c]
                        act.activation(g_hid[:, half, c, :], bank[:, :], ACT.Gelu, bias=b1[:, c:c + 1])\
                            .then_inc(S["g_ready"], 1)

            ffn(0)
            with act.Fori(1, B // 2) as i:
                ffn(i)

        @block.gpsimd
        def _(pool):
            own = Steps(pool, S["pool_step"])

            def split(b, n):
                src, parts = ((qT, q_parts), (kT, k_parts))[n]
                pool.wait_ge(S["qkT_ready"], 2 * b + n + 1)
                wait(pool, S["split_ready"], 2 * b + n)
                own.did(pool.tensor_tensor(rest1[:, :], src[:, :], parts[:, 0, :], ALU.subtract))
                own.did(pool.tensor_tensor(parts[:, 1, :], src[:, :], parts[:, 0, :], ALU.subtract))
                own.settle()
                pool.tensor_tensor(parts[:, 2, :], rest1[:, :], parts[:, 1, :], ALU.subtract).then_inc(S["split_ready"], 1)

            def near_products(b, n):
                pool.wait_ge(S["k_near_in"], 16 * (b + 1))
                pool.wait_ge(S["nat_ready"], TB * b + n + 1)
                wait(pool, S["near_qk_ready"], TB * b + n - 1)
                q_rep = nat[:, n, 0:E].rearrange("p (o e) -> p o e", o=1).to_broadcast([P, J, E])
                pool.tensor_tensor(qk_prod[:, n % 2, :].rearrange("p (j e) -> p j e", j=J),
                                   k_near[:, n, :].rearrange("p (j e) -> p j e", j=J), q_rep, ALU.mult)\
                    .then_inc(S["qk_prod_ready"], 1)

            def fill_vaug(b, q):
                pool.wait_ge(S["nat_ready"], TB * (b + 1))
                wait(pool, S["pv_ps"], QUADS * TB * (b - 1) + TB * (q + 1))
                c = 2 * E + q * G * D
                one = one_col[:, :].rearrange("p (n o) -> p n o", n=1).to_broadcast([P, G, D])
                for n in range(TB):
                    ins = pool.tensor_tensor(vaug[:, q, n, :, 0:D], nat[:, n, c:c + G * D].rearrange("p (g d) -> p g d", d=D),
                                             one, ALU.mult)
                ins.then_inc(S["vaug_ready"], 1)

            def near_values(b, n):
                pool.wait_ge(S["v_near_in"], 16 * (b + 1))
                pool.wait_ge(S["near_p_ready"], b + 1)
                if n == 0:
                    wait(pool, S["o_ready"], b)
                wait(pool, S["near_v_ready"], TB * b + n)
                p_rep = near_p[:, n, :, :].rearrange("p j (h o) -> p (j h) o", o=1).to_broadcast([P, JH, D])
                own.did(pool.tensor_tensor(pv_prod[:, :, :].rearrange("p j (h d) -> p (j h) d", d=D),
                                           v_near[:, n, :].rearrange("p (m d) -> p m d", d=D), p_rep, ALU.mult))
                own.settle()
                for half in (4, 2, 1):
                    own.did(pool.tensor_tensor(pv_prod[:, 0:half, :], pv_prod[:, 0:half, :], pv_prod[:, half:2 * half, :], ALU.add))
                    own.settle()
                own.did(pool.tensor_tensor(pv_prod[:, 0, :], pv_prod[:, 0, :], pv_prod[:, J - 1, :], ALU.add))
                own.settle()
                if n == 0:
                    pool.wait_ge(S["near_ev_ready"], b + 1)
                pool.tensor_tensor(near_v[:, n, :], pv_prod[:, 0, :], near_ev[:, n, :], ALU.add).then_inc(S["near_v_ready"], 1)

            pool.memset(minus_half[:, :], -0.5).then_inc(S["setup_pool"], 1)
            pool.memset(zero_rows[:, :], 0.0).then_inc(S["zeros_ready"], 1)
            pool.memset(zero_pad, 0.0).then_inc(S["zeros_ready"], 1)
            pool.memset(one_rows, 1.0).then_inc(S["zeros_ready"], 1)
            pool.wait_ge(S["setup_pool"], 1)
            pool.wait_ge(S["eps0_ready"], 1)
            pool.tensor_tensor(rstd[:, 0:TB], var_eps[:, 0:TB], minus_half[:, 0:TB], ALU.pow).then_inc(S["pow0_ready"], 1)
            pool.memset(Q[:, :, :, :].rearrange("p q g t -> p (q g t)").bitcast(int32), 0).then_inc(S["zeros_ready"], 1)
            pool.memset(K[:, :, :, :].rearrange("p q g t -> p (q g t)").bitcast(int32), 0).then_inc(S["zeros_ready"], 1)
            pool.wait_ge(S["eps_ready"], 1)
            pool.tensor_tensor(rstd[:, TB:], var_eps[:, TB:], minus_half[:, TB:], ALU.pow).then_inc(S["pow_ready"], 1)
            own.did(pool.memset(one_col[:, :], 1.0))
            own.did(pool.memset(vaug[:, :, :, :, :].rearrange("p q n g c -> p (q n g c)"), 0.0))
            own.settle()
            own.did(pool.memset(vaug[:, :, :, :, D:D + 1].rearrange("p q n g o -> p (q n g) o"), 1.0))
            own.settle()
            for n in range(2):
                split(0, n)
            for q in range(QUADS):
                fill_vaug(0, q)
            for n in range(TB):
                near_products(0, n)

            def body(b, last):
                first = isinstance(b, int) and b == 0
                if not first:
                    fill_vaug(b, QUADS - 1)
                if not last:
                    for n in range(2):
                        split(b + 1, n)
                    for n in range(TB):
                        near_products(b + 1, n)
                    for q in range(2):
                        fill_vaug(b + 1, q)
                for n in range(TB):
                    near_values(b, n)
                if not last:
                    fill_vaug(b + 1, 2)

            body(0, False)
            steps = 2 * 2 + TB * 5
            start = own.n
            with pool.Fori(1, B - 1) as b:
                own.n = (b - 1) * steps + start
                body(b, False)
            own.n = start + (B - 2) * steps
            body(B - 1, True)

        @block.vector
        def _(dve):
            own = Steps(dve, S["dve_step"])

            def three_parts(dst, src, rest, part):
                own.did(dve.tensor_copy(dst(0), src))
                own.settle()
                own.did(dve.tensor_tensor(rest, src, dst(0), ALU.subtract))
                own.settle()
                own.did(dve.tensor_copy(dst(1), rest))
                own.settle()
                own.did(dve.tensor_tensor(dst(2), rest, dst(1), ALU.subtract))
                own.settle()

            def near_logits(b, n):
                dve.wait_ge(S["qk_prod_ready"], TB * b + n + 1)
                wait(dve, S["near_ready"], TB * b + n)
                dve.tensor_reduce(near_qk[:, :], qk_prod[:, n % 2, :].rearrange("p (m d) -> p m d", d=D), AX.X, ALU.add)\
                    .then_inc(S["near_qk_ready"], 1)
                dve.wait_ge(S["near_qk_ready"], TB * b + n + 1)
                dve.wait_ge(S["rel_ready"], TB * b + n + 1)
                dve.tensor_tensor(near[:, n, :, :].rearrange("p j h -> p (j h)"), near_qk[:, :], rel[:, n, :], ALU.add)\
                    .then_inc(S["near_ready"], 1)

            def max_unit(b, q, u):
                dve.wait_ge(S["s_ps"], QUADS * UNITS * b + UNITS * q + u + 1)
                dve.tensor_reduce(neg_max[:, u // TB, u % TB:u % TB + 1], s_bank[u % 2][:, :], AX.X, ALU.max, negate=True)\
                    .then_inc(S["max_ready"], 1)

            def row_maximum(b, q):
                hs = slice(q * G, q * G + G)
                own.settle()
                dve.wait_ge(S["near_ready"], TB * (b + 1))
                own.did(dve.tensor_reduce(neg_near[:, :, :], near[:, :, :, hs].rearrange("p n j g -> p n g j"), AX.X, ALU.max,
                                          negate=True))
                own.settle()
                dve.wait_ge(S["max_ready"], QUADS * UNITS * b + UNITS * (q + 1))
                own.did(dve.tensor_tensor(neg_c[:, :, :], neg_max[:, :, :], neg_near[:, :, :].rearrange("p n g -> p g n"), ALU.min))
                own.settle()
                wait(dve, S["cT_ps"], QUADS * b + q)
                own.did(dve.tensor_copy(c_parts[:, 0, :, :], neg_c[:, :, :]))
                own.settle()
                dve.tensor_tensor(c_parts[:, 1, :, :], neg_c[:, :, :], c_parts[:, 0, :, :], ALU.subtract).then_inc(S["c_ready"], 1)
                dve.wait_ge(S["c_ready"], QUADS * b + q + 1)
                own.did(dve.tensor_tensor(c_used[:, :, hs], c_parts[:, 0, :, :].rearrange("p g n -> p n g"),
                                          c_parts[:, 1, :, :].rearrange("p g n -> p n g"), ALU.add))

            def near_minus_max(b):
                own.settle()
                c_rep = c_used[:, :, :].rearrange("p n (o h) -> p n o h", o=1).to_broadcast([P, TB, J, H])
                wait(dve, S["near_p_ready"], b)
                dve.tensor_tensor(near_p[:, :, :, :], near[:, :, :, :], c_rep, ALU.add).then_inc(S["near_c_ready"], 1)

            def near_sums(b):
                dve.wait_ge(S["near_p_ready"], b + 1)
                dve.tensor_reduce(near_den[:, :, :], near_p[:, :, :, :].rearrange("p n j h -> p n h j"), AX.X, ALU.add)\
                    .then_inc(S["near_den_ready"], 1)

            def keep_gates(b):
                dve.wait_ge(S["nat_ready"], TB * (b + 1))
                dve.tensor_copy(gates[:, :, at(b), :].rearrange("p n o e -> p n (o e)"), nat[:, :, 3 * E:NPROJ])\
                    .then_inc(S["gates_ready"], 1)

            def keep_o(b, q):
                dve.wait_ge(S["o_ps"], QUADS * b + q + 1)
                src = m0[:, :].rearrange("p (n g c) -> p n g c", n=TB, c=VW)
                dve.tensor_copy(o_raw[:, :, q * G:(q + 1) * G, :], src[:, :, :, 0:D + 1]).then_inc(S["o_raw_ready"], 1)

            def finish_attention(b):
                dve.wait_ge(S["o_raw_ready"], QUADS * (b + 1))
                dve.wait_ge(S["near_den_ready"], b + 1)
                own.did(dve.tensor_tensor(den[:, :, :], o_raw[:, :, :, D], near_den[:, :, :], ALU.add))
                own.settle()
                own.did(dve.reciprocal(rden[:, :, :], den[:, :, :]))
                dve.wait_ge(S["near_v_ready"], TB * (b + 1))
                own.did(dve.tensor_tensor(near_v[:, :, :].rearrange("p n (h d) -> p (n h) d", d=D),
                                          o_raw[:, :, :, 0:D].rearrange("p n h d -> p (n h) d"),
                                          near_v[:, :, :].rearrange("p n (h d) -> p (n h) d", d=D), ALU.add))
                own.settle()
                r_rep = rden[:, :, :].rearrange("p n (h o) -> p (n h) o", o=1).to_broadcast([P, TB * H, D])
                wait(dve, S["oT_ps"], b)
                dve.tensor_tensor(o_nat[:, :, :].rearrange("p n (h d) -> p (n h) d", d=D),
                                  near_v[:, :, :].rearrange("p n (h d) -> p (n h) d", d=D), r_rep, ALU.mult)\
                    .then_inc(S["o_ready"], 1)

            def add_residual(b):
                dve.wait_ge(S["wo_ps"], b + 1)
                xb = x_all[:, at(b), :, :].rearrange("p o n e -> p (o n e)")
                dve.tensor_tensor(xb, m2[:, :], xb, ALU.add).then_inc(S["x_res_ready"], 1)

            def batch_stats(b):
                for n in range(TB):
                    c = b * TB + n
                    col = slice(c, c + 1) if isinstance(c, int) else bass.ds(c, 1)
                    own.did(dve.bn_stats(stats[:, col, :].rearrange("p o s -> p (o s)"),
                                         x_all[:, at(b), n, :].rearrange("p o e -> p (o e)")))

            def gather_stats(first, end):
                own.settle()
                for c in range(first * TB, end * TB):
                    own.did(dve.bn_aggr(mean_var[:, c, :], stats[:, c, :]))

            def add_eps(cols, s):
                own.settle()
                dve.tensor_scalar(var_eps[:, cols], mean_var[:, cols, 1], LN_EPS, None, ALU.add).then_inc(S[s], 1)

            def shifts(cols, pow_ready, ready):
                dve.wait_ge(S[pow_ready], 1)
                dve.scalar_tensor_tensor(shift[:, cols], mean_var[:, cols, 0], -1.0, rstd[:, cols], ALU.mult, ALU.mult)\
                    .then_inc(S[ready], 1)

            dve.wait_ge(S["x0_in"], 16)
            batch_stats(0)
            gather_stats(0, 1)
            add_eps(slice(0, TB), "eps0_ready")
            dve.memset(brow_parts[:, :], 0.0).then_inc(S["dve_step"], 1)
            dve.memset(ones_rows[:, :], 1.0).then_inc(S["dve_step"], 1)
            own.n += 2
            shifts(slice(0, TB), "pow0_ready", "stats0_ready")
            dve.wait_ge(S["weights_in"], 16 * 18)
            own.did(dve.tensor_scalar(wcat[:, 0:E], wcat[:, 0:E], SCALING, None, ALU.mult))
            own.did(dve.tensor_scalar(bqk[:, 0:1], bqk[:, 0:1], SCALING, None, ALU.mult))
            own.did(dve.tensor_scalar(brow[:, 0:E], brow[:, 0:E], SCALING, None, ALU.mult))
            own.did(dve.tensor_copy(ident_b[:, :], ident[:, :]))
            own.did(dve.tensor_copy(band_b[:, :], band_f[:, :]))
            own.settle()
            ek_rep = ek[:, :].rearrange("p (j o) -> p j o", o=1).to_broadcast([P, J, H])
            hm_rep = headmask[:, :].rearrange("p (o h) -> p o h", o=1).to_broadcast([P, J, H])
            own.did(dve.tensor_tensor(ek_block[:, :, :], ek_rep, hm_rep, ALU.mult))
            for blk, ev, rows in ((ev_block0, ev0, P), (ev_block1, ev1, H)):
                ev_rep = ev[:, :].rearrange("p (o d) -> p o d", o=1).to_broadcast([rows, H, D])
                rm_rep = relmask[0:rows, :].rearrange("p (h o) -> p h o", o=1).to_broadcast([rows, H, D])
                own.did(dve.tensor_tensor(blk[:, :, :], ev_rep, rm_rep, ALU.mult))
            own.settle()
            dve.tensor_copy(small[0:1, 0:1], ident[0:1, 0:1]).then_inc(S["setup_dve"], 1)
            bp = gtmp[0:PARTS, 0:NPROJ + E]
            br = gtmp[0:PARTS, 1024:1024 + NPROJ + E]
            bparts = qk_prod[0:PARTS, :, :].rearrange("p a n -> p (a n)")[:, 0:3 * (NPROJ + E) // 2 + 2].bitcast(bf16)
            NB = NPROJ + E
            three_parts(lambda i: bparts[:, i * NB:(i + 1) * NB], brow, br, None)
            own.did(dve.tensor_scalar(brow_parts[0:PARTS, :], bparts[:, 0:NB], ident[0:PARTS, 0:1], None, ALU.mult))
            own.settle()
            for i in (1, 2):
                own.did(dve.scalar_tensor_tensor(brow_parts[0:PARTS, :], bparts[:, i * NB:(i + 1) * NB], ident[0:PARTS, i:i + 1],
                                                 brow_parts[0:PARTS, :], ALU.mult, ALU.add))
                own.settle()
            dve.tensor_copy(small[1 - 1:1, 1:2], ident[0:1, 0:1]).then_inc(S["bias_ready"], 1)

            dve.wait_ge(S["x_rest_in"], 16 * (B - 1))
            start = own.n
            with dve.Fori(1, B) as b:
                own.n = (b - 1) * TB + start
                batch_stats(b)
            own.n = start + (B - 1) * TB
            gather_stats(1, B)
            add_eps(slice(TB, B * TB), "eps_ready")
            three_parts(lambda i: b2_parts[:, i, :], b2[:, :], b2_rest[:, :], None)
            dve.memset(pv_bank[:, :], 0.0).then_inc(S["pv_clear"], 1)
            own.did(dve.memset(sel[:, :], 0.0))
            own.did(dve.memset(sel_m1[:, :], 0.0))
            shifts(slice(TB, B * TB), "pow_ready", "stats_ready")
            keep_gates(0)
            for n in range(TB):
                near_logits(0, n)
            for u in range(UNITS):
                max_unit(0, 0, u)
            row_maximum(0, 0)
            for u in range(UNITS):
                max_unit(0, 1, u)

            def selection():
                gl = gates[:, :, :, :].rearrange("p n b e -> p (n b) e")
                NT = TB * B
                dve.wait_ge(S["gates_ready"], B)
                dve.wait_ge(S["qk_prod_ready"], TB * B)
                rep = ident[:, 0:B * NEXP].rearrange("p (n o) -> p n o", o=1).to_broadcast([P, B * NEXP, HID])
                own.did(dve.tensor_scalar(expert_rows, rep, -NEG, None, ALU.mult))
                own.did(dve.tensor_reduce(g_max, gl, AX.X, ALU.max))
                own.settle()
                gm = g_max.rearrange("p (n o) -> p n o", o=1).to_broadcast([P, NT, NEXP])
                dve.tensor_tensor(g_exp, gl, gm, ALU.subtract).then_inc(S["g_shift_ready"], 1)
                other = gates[:, :, :, :].rearrange("p n b (o f) -> p (n b) o f", o=1).to_broadcast([P, NT, NEXP, NEXP])
                mine = gates[:, :, :, :].rearrange("p n b (e o) -> p (n b) e o", o=1).to_broadcast([P, NT, NEXP, NEXP])
                own.did(dve.tensor_tensor(pair_gt, other, mine, ALU.is_gt))
                own.did(dve.tensor_tensor(pair_eq, other, mine, ALU.is_equal))
                own.settle()
                yield
                tri = earlier[:, :].rearrange("p (o m) -> p o m", o=1).to_broadcast([P, NT, NEXP * NEXP])
                flat_eq = pair_eq.rearrange("p n e f -> p n (e f)")
                own.did(dve.tensor_tensor(flat_eq, flat_eq, tri, ALU.mult))
                own.settle()
                own.did(dve.tensor_tensor(pair_gt, pair_gt, pair_eq, ALU.add))
                own.settle()
                own.did(dve.tensor_reduce(g_cnt, pair_gt, AX.X, ALU.add))
                dve.wait_ge(S["g_exp_ready"], 1)
                own.did(dve.tensor_reduce(g_sum, g_exp, AX.X, ALU.add))
                own.settle()
                own.did(dve.reciprocal(g_max, g_sum))
                own.settle()
                own.did(dve.tensor_tensor(score, g_exp, gm, ALU.mult))
                own.settle()
                own.did(dve.scalar_tensor_tensor(score, g_cnt, float(TOPK), score, ALU.is_lt, ALU.mult))
                own.settle()
                own.did(dve.tensor_reduce(g_den, score.rearrange("p (n b) e -> p n e b", n=TB), AX.X, ALU.add))
                own.settle()
                own.did(dve.tensor_scalar(g_den, g_den, GATE_EPS, None, ALU.add))
                own.settle()
                own.did(dve.reciprocal(g_den, g_den))
                own.settle()
                own.did(dve.tensor_scalar(g_den, g_den, CAPACITY, None, ALU.mult))
                own.settle()
                gd = g_den.rearrange("p n (o e) -> p n o e", o=1).to_broadcast([P, TB, B, NEXP])
                dve.tensor_tensor(route.rearrange("p n (b e) -> p n b e", e=NEXP), score.rearrange("p (n b) e -> p n b e", n=TB),
                                  gd, ALU.mult).then_inc(S["route_ready"], 1)
                yield
                dve.wait_ge(S["st_ps"], QUADS * UNITS * (B - 1) + 2 * UNITS)
                for i in range(PARTS):
                    part = b2_parts[:, i, :].rearrange("p (o e) -> p o e", o=1).to_broadcast([P, B, E])
                    mask = batchmask[:, :].rearrange("p (b o) -> p b o", o=1).to_broadcast([P, B, E])
                    own.did(dve.tensor_tensor(b2_rows[:, :, i, :], part, mask, ALU.mult))
                dve.wait_ge(S["route_ps"], 1)
                dve.wait_ge(S["near_v_ready"], TB * B)
                own.did(dve.tensor_copy(route_rows, s_bank[0][0:SROW, :]))
                own.did(dve.memset(cand[:, :], 1 << (SEARCH_BITS - 1)))
                own.did(dve.memset(ones_t, 1.0))
                own.settle()
                value = cand[:, :].bitcast(fp32)
                for bit in range(SEARCH_BITS - 1, -1, -1):
                    own.did(dve.tensor_scalar(above, route_rows, value, None, ALU.is_ge, ALU.add, accum_out=small[:, 2:3]))
                    own.settle()
                    own.did(dve.tensor_scalar(drop[:, :], small[:, 2:3], float(KEEP), float(1 << bit), ALU.is_lt, ALU.mult))
                    own.settle()
                    own.did(dve.scalar_tensor_tensor(cand[:, :], cand[:, :], (1 << bit) >> 1, drop[:, :],
                                                     ALU.bitwise_xor, ALU.bitwise_xor))
                    own.settle()
                    if bit % 16 == 0:
                        yield
                own.did(dve.tensor_scalar(above, route_rows, value, None, ALU.is_gt, ALU.add, accum_out=small[:, 2:3]))
                own.did(dve.tensor_scalar(equal, route_rows, value, None, ALU.is_equal))
                own.settle()
                own.did(dve.tensor_tensor_scan(order, ones_t, equal, 0.0, ALU.mult, ALU.add))
                own.did(dve.tensor_scalar(small[:, 3:4], small[:, 2:3], -1.0, float(KEEP), ALU.mult, ALU.add))
                own.settle()
                own.did(dve.scalar_tensor_tensor(picked, order, small[:, 3:4], equal, ALU.is_le, ALU.mult))
                own.settle()
                own.did(dve.tensor_tensor(sel[0:SROW, :], picked, above, ALU.add))
                own.settle()
                dve.tensor_scalar(sel_m1[0:SROW, :], sel[0:SROW, :], -1.0, None, ALU.add).then_inc(S["sel_ready"], 1)

            def body(b, last):
                first = isinstance(b, int) and b == 0
                select = selection() if last else None
                for q in range(QUADS):
                    if q < QUADS - 1:
                        row_maximum(b, q + 1)
                    elif not last:
                        row_maximum(b + 1, 0)
                    if q == 2:
                        near_minus_max(b)
                    for u in range(UNITS):
                        if q < 2:
                            max_unit(b, q + 2, u)
                        elif not last:
                            max_unit(b + 1, q - 2, u)
                        if u == 7:
                            if q > 0:
                                keep_o(b, q - 1)
                            elif not first:
                                keep_o(b - 1, QUADS - 1)
                        if q == 0 and u == 10 and not first:
                            finish_attention(b - 1)
                        if q == 0 and u == 13 and not last:
                            keep_gates(b + 1)
                        if q == 1 and u == 14 and not first:
                            add_residual(b - 1)
                        if q == 2 and not last and u in (5, 8, 11, 14):
                            near_logits(b + 1, (5, 8, 11, 14).index(u))
                        if q == 3 and u == 2:
                            near_sums(b)
                        if last and (q, u) in ((1, 15), (2, 8)):
                            next(select)
                if last:
                    return select

            body(0, False)
            steps_c = 4
            steps = QUADS * steps_c + 3
            start = own.n
            with dve.Fori(1, B - 1) as b:
                own.n = (b - 1) * steps + start
                body(b, False)
            own.n = start + (B - 2) * steps
            select = body(B - 1, True)
            keep_o(B - 1, QUADS - 1)
            finish_attention(B - 1)
            add_residual(B - 1)
            for _ in select:
                pass

            def ffn(i):
                for half, s in enumerate(("out_even", "out_odd")):
                    wait(dve, S[s], 16 * i)
                    dve.wait_ge(S["y_ps"], 2 * i + half + 1)
                    xb = x_all[:, at(2 * i + half), :, :].rearrange("p o n e -> p (o n e)")
                    dve.tensor_tensor(ffn_out[:, half, :], (m1, m2)[half][:, :], xb, ALU.add).then_inc(S["ffn_ready"], 1)

            ffn(0)
            with dve.Fori(1, B // 2) as i:
                ffn(i)


def kernel(**inputs):
    import concourse.bacc as bacc
    from concourse.bass_utils import run_bass_kernel_spmd as run

    a = {n.split("_", 1)[1]: np.asarray(v) for n, v in inputs.items()}
    a = {n.replace("attn_", "").replace("ffn_", ""): v for n, v in a.items()}
    f = np.float32
    arrays = {
        "x": a["hidden_states"],
        "wcat": np.concatenate([a["Wq"], a["Wk"], a["Wv"], a["w_gate_w"]], axis=1),
        "brow": np.tile(np.concatenate([a["bq"], a["bk"], a["bv"], a["w_gate_b"], a["bo"]])[None], (PARTS, 1)),
        "bqk": np.stack([a["bq"], a["bk"]], axis=1),
        "wo": a["Wo"],
        "bo": a["bo"][None],
        "ek": np.tile(a["emb_rel_k"][0].T, (H, 1)),
        "ev": np.repeat(a["emb_rel_v"][0], H, axis=0),
        "w1": a["W1"].transpose(1, 0, 2).reshape(E, NEXP * HID),
        "b1": a["b1"].reshape(2, P).T,
        "w2": a["W2"].reshape(2, P, E).transpose(1, 0, 2),
        "b2": np.tile(a["b2"], (P // NEXP, 1)),
    }
    p = np.arange(P)
    w = np.arange(BAND)[None, :] - p[:, None]
    band = np.where((w >= 0) & (w <= 2 * WINDOW), NEG, 0.0).astype(f)
    j = np.arange(J)
    edge = np.zeros((P, 2, J, H), f)
    edge[:, 0][(p[:, None] + j[None] - WINDOW) < 0] = NEG
    edge[:, 1][(p[:, None] + j[None] - WINDOW) >= P] = NEG
    arrays |= {
        "ident": np.eye(P, dtype=f),
        "band": band,
        "edge": edge.reshape(P, 2, JH),
        "headmask": (p[:, None] // D == np.arange(H)[None]).astype(f),
        "relmask": (p[:, None] % H == np.arange(H)[None]).astype(f),
        "earlier": np.tile((np.arange(NEXP)[None, :] < np.arange(NEXP)[:, None]).astype(f).reshape(1, -1), (P, 1)),
        "batchmask": (p[:, None] // NEXP == np.arange(B)[None]).astype(f),
    }
    arrays = {f"in_{n}": np.ascontiguousarray(v) for n, v in arrays.items()}
    nc = bacc.Bacc("TRN2", target_bir_lowering=False, num_devices=1)
    args = [nc.dram_tensor(n, v.shape, mybir.dt.from_np(v.dtype), kind="ExternalInput").ap() for n, v in arrays.items()]
    out = nc.dram_tensor("out_0", (B, T, E), fp32, kind="ExternalOutput").ap()
    build_program(nc, *args, out)
    r = run(nc, [arrays], core_ids=[0])
    return r.results[0]["out_0"]
```

```python
import numpy as np
import concourse.bass as bass
from concourse import mybir
from contextlib import ExitStack

fp32 = mybir.dt.float32
bf16 = mybir.dt.bfloat16
int32 = mybir.dt.int32
ALU = mybir.AluOpType
ACT = mybir.ActivationFunctionType
AX = mybir.AxisListType

B, T, E, H = 8, 512, 128, 16
D = E // H
WINDOW = 4
J = 2 * WINDOW + 1
P = 128
TB = T // P
NEXP = 8
HID = 32
TOPK = 2
KEEP = T // 2
CAPACITY = float(B)
GATE_EPS = 1e-6
LN_EPS = 1e-5
SCALING = D ** -0.5
QUADS = 4
G = H // QUADS
UNITS = G * TB
NPROJ = 3 * E + NEXP
JH = J * H
PARTS = 3
QK_ROWS = PARTS * PARTS * D
C_ROW = QK_ROWS
BAND = P + 2 * WINDOW
NEG = -1e30
VW = 32
SEARCH_BITS = 31
TWO_ONES = 0x3F803F80


FIRST_COLUMNS = (("ident", P), ("wcat", NPROJ), ("bqk", 2))
REST_COLUMNS = (("band", BAND), ("edge", 2 * JH), ("headmask", H), ("relmask", H), ("ek", J), ("ev0", D), ("ev1", D),
                ("wo", E), ("earlier", NEXP * NEXP), ("batchmask", B), ("w1", NEXP * HID), ("b1", 2), ("w2", 2 * E), ("b2", E))


def build_program(nc, x_in, first_in, rest_in, brow_in, out):
    ctx = ExitStack()
    with ctx:
        def sb(name, shape, dt=fp32):
            return ctx.enter_context(nc.sbuf_tensor(name, shape, dt))

        def sem(name):
            return ctx.enter_context(nc.semaphore(name))

        def dram(name, shape, dt=fp32):
            return nc.dram_tensor(name, shape, dt, kind="Internal").ap()

        k_rows = dram("k_rows", [B, T + 2 * WINDOW, E])
        v_rows = dram("v_rows", [B, T + 2 * WINDOW, E])
        q_parts_dram = dram("q_parts_dram", [B, PARTS, D, H, T], bf16)
        xnT_dram = dram("xnT_dram", [B, P, T])
        k_parts_dram = dram("k_parts_dram", [B, PARTS, D, H, T], bf16)

        def columns(tensor, layout):
            views, c = [], 0
            for _, width in layout:
                views.append(tensor[:, c:c + width])
                c += width
            return views

        front_data = sb("front_data", [P, sum(w for _, w in FIRST_COLUMNS)])
        rest_data = sb("rest_data", [P, sum(w for _, w in REST_COLUMNS)])
        ident, wcat, bqk = columns(front_data, FIRST_COLUMNS)
        (band_f, edge, headmask, relmask, ek, ev0, ev1, wo, earlier, batchmask, w1, b1, w2, b2) = columns(rest_data, REST_COLUMNS)
        edge = edge.rearrange("p (i m) -> p i m", i=2)
        w2 = w2.rearrange("p (i e) -> p i e", i=2)
        ev1 = ev1[0:H, :]
        ident_b = sb("ident_b", [P, P], bf16)
        band_b = sb("band_b", [P, BAND], bf16)
        brow_parts = sb("brow_parts", [P, NPROJ + E], bf16)
        ones_rows = sb("ones_rows", [P, P], bf16)
        ek_block = sb("ek_block", [P, J, H])
        ev_block0 = sb("ev_block0", [P, H, D])
        ev_block1 = sb("ev_block1", [H, H, D])
        b2_rest = sb("b2_rest", [P, E])
        b2_parts = sb("b2_parts", [P, PARTS, E], bf16)
        zero_rows = sb("zero_rows", [2, G * T], bf16)
        one_col = sb("one_col", [P, 1])
        minus_half = sb("minus_half", [P, B * TB])

        x_all = sb("x_all", [P, B, TB, E])
        stats = sb("stats", [P, B * TB, 6])
        mean_var = sb("mean_var", [P, B * TB, 2])
        var_eps = sb("var_eps", [P, B * TB])
        rstd = sb("rstd", [P, B * TB])
        shift = sb("shift", [P, B * TB])
        scores = sb("scores", [P, TB, B, NEXP])
        g_exp = sb("g_exp", [P, TB, NEXP])
        g_max = sb("g_max", [P, TB])
        g_sum = sb("g_sum", [P, TB])
        g_count = sb("g_count", [P, TB, NEXP])
        pair_gt = sb("pair_gt", [P, TB, NEXP, NEXP], bf16)
        pair_eq = sb("pair_eq", [P, TB, NEXP, NEXP], bf16)

        xn = sb("xn", [P, TB, E])
        xnT = sb("xnT", [P, T])
        nat = sb("nat", [P, TB, NPROJ])
        qT = sb("qT", [P, T])
        kT = sb("kT", [P, T])
        rest1 = sb("rest1", [P, T])
        q_parts = sb("q_parts", [P, PARTS, T], bf16)
        k_parts = sb("k_parts", [P, PARTS, T], bf16)
        Q = sb("Q", [P, QUADS, G, T], bf16)
        K = sb("K", [P, QUADS, G, T], bf16)
        vaug = sb("vaug", [P, QUADS, TB, G, D + 1])

        k_near = sb("k_near", [P, TB, J * E])
        v_near = sb("v_near", [P, TB, J * E])
        qk_prod = sb("qk_prod", [P, 2, J * E])
        pv_prod = sb("pv_prod", [P, J, E])
        near_qk = sb("near_qk", [P, TB, JH])
        rel = sb("rel", [P, TB, JH])
        near = sb("near", [P, TB, J, H])
        near_p = sb("near_p", [P, TB, J, H])
        near_pT = sb("near_pT", [P, 2, 2, P])
        near_ev = sb("near_ev", [P, TB, E])
        near_v = sb("near_v", [P, TB, E])
        near_den = sb("near_den", [P, TB, H])

        neg_max = sb("neg_max", [P, G, TB])
        neg_near = sb("neg_near", [P, TB, H])
        neg_c = sb("neg_c", [P, G, TB])
        c_parts = sb("c_parts", [P, 2, G, TB], bf16)
        c_used = sb("c_used", [P, TB, H])
        cT = sb("cT", [2 * UNITS, P], bf16)
        PT = sb("PT", [P, TB, G, T])
        pvT = sb("pvT", [P, T])
        o_raw = sb("o_raw", [P, TB, H, D + 1])
        den = sb("den", [P, TB, H])
        rden = sb("rden", [P, TB, H])
        o_nat = sb("o_nat", [P, TB, E])
        oT = sb("oT", [P, T])

        s_bank = [ctx.enter_context(nc.psum_tensor(f"s_bank{i}", [P, T], fp32)) for i in range(2)]
        st_bank = [ctx.enter_context(nc.psum_tensor(f"st_bank{i}", [P, T], fp32)) for i in range(2)]
        pv_bank = ctx.enter_context(nc.psum_tensor("pv_bank", [P, T], fp32))
        m0 = ctx.enter_context(nc.psum_tensor("m0", [P, T], fp32))
        m1 = ctx.enter_context(nc.psum_tensor("m1", [P, T], fp32))
        m2 = ctx.enter_context(nc.psum_tensor("m2", [P, T], fp32))
        m0_b = m0[:, :].bitcast(bf16)

        PT_flat = PT[:, :, :, :].rearrange("p a g t -> p (a g t)")
        zero_pad = PT_flat[0:WINDOW, 4096:4096 + B * E].rearrange("p (b e) -> p b e", e=E)
        brow = PT_flat[0:PARTS, 6144:6144 + NPROJ + E]

        xnT_all = Q[:, :, :, :].rearrange("p q g t -> p (q g t)").bitcast(fp32).rearrange("p (b t) -> p b t", t=T)
        b2_rows = K[:, :, :, :].rearrange("p q g t -> p (q g t)")[:, 0:B * PARTS * E].rearrange("p (b i e) -> p b i e", i=PARTS, e=E)
        g_hid = PT[:, :, :, :].rearrange("p a g t -> p (a g t)")[:, 0:4 * T].rearrange("p (i c t) -> p i c t", i=2, c=2)
        ffn_out = PT[:, :, :, :].rearrange("p a g t -> p (a g t)")[:, 4 * T:6 * T].rearrange("p (i n) -> p i n", i=2)
        gtmp = k_near[:, :, :].rearrange("p a n -> p (a n)")
        g_den = gtmp[:, 0:TB * NEXP].rearrange("p (t e) -> p t e", e=NEXP)
        route = gtmp[:, TB * NEXP:TB * NEXP * (B + 1)].rearrange("p (t n) -> p t n", t=TB)
        expert_rows = gtmp[:, 3200:3200 + B * NEXP * HID // 2].bitcast(bf16).rearrange("p (n h) -> p n h", h=HID)
        SROW = B * NEXP
        srow = gtmp[0:SROW, 1152:3200]
        srow2 = qk_prod[0:SROW, :, :].rearrange("p a n -> p (a n)")
        route_rows = srow[:, 0:T]
        above = srow[:, T:2 * T]
        equal = srow[:, 2 * T:3 * T]
        ones_t = srow[:, 3 * T:4 * T]
        order = srow2[:, 0:T]
        picked = srow2[:, T:2 * T]
        small = sb("small", [SROW, 8])
        cand = sb("cand", [SROW, 1], int32)
        drop = sb("drop", [SROW, 1], int32)
        sel = sb("sel", [P, T], bf16)
        sel_m1 = sb("sel_m1", [P, T], bf16)

        names = ("x0_in x_rest_in first_in rest_in brow_in pads_written zero_pad_ready rows_set scaled masks_ready blocks_ready setup_pool bias_ready "
                 "stats0_ready stats_ready eps0_ready eps_ready pow0_ready pow_ready "
                 "xn_ready xnT_ps xnT_ready xnT_saved xnT_back xnT_back_first pv_clear nat_ps nat_ready qkT_ps qkT_ready split_ready parts_saved kv_saved "
                 "k_near_in v_near_in qk_prod_ready near_qk_ready rel_ps rel_ready near_ready gates_ready vaug_ready "
                 "st_ps exp_ready s_ps max_ready pv_ps pvT_ready o_ps o_raw_ready c_ready cT_ps cT_ready "
                 "near_c_ready near_p_ready near_pT_ps near_pT_ready ev_ps near_ev_ready near_v_parts near_v_ready near_den_ready "
                 "o_ready oT_ps oT_ready wo_ps x_res_ready dve_step pool_step "
                 "g_shift_ready g_exp_ready route_ready route_ps route_kept sel_ready b2_rows_ready h_ps g_ready y_ps ffn_ready out_even out_odd").split()
        S = {n: sem(n) for n in names}
        packed = [sem(f"packed{q}") for q in range(QUADS)]
        c_rows_in = [sem(f"c_rows_in{q}") for q in range(QUADS)]
        PACK_DMAS = 2 + PARTS

        block = ctx.enter_context(nc.Block())

        def wait(eng, s, value):
            if isinstance(value, int) and value <= 0:
                return
            eng.wait_ge(s, value)

        class Steps:

            def __init__(self, eng, s):
                self.eng, self.s, self.n = eng, s, 0

            def did(self, ins):
                ins.then_inc(self.s, 1)
                self.n = self.n + 1

            def settle(self):
                self.eng.wait_ge(self.s, self.n)

        def at(b):
            return slice(b, b + 1) if isinstance(b, int) else bass.ds(b, 1)

        def span(start, size):
            return slice(start, start + size) if isinstance(start, int) else bass.ds(start, size)

        def band_columns(blk):
            lo, hi = max(0, blk * P - WINDOW), min(T, (blk + 1) * P + WINDOW)
            m = lo - (blk * P - WINDOW)
            return slice(lo, hi), slice(m, m + hi - lo)

        @block.sync
        def _(sp):
            def load(dst, src, s):
                sp.dma_start(dst, src).then_inc(S[s], 16)

            xv = x_in.rearrange("b (n p) e -> b p n e", p=P)
            load(x_all[:, 0, :, :], xv[0], "x0_in")
            load(brow, brow_in, "brow_in")
            load(x_all[:, 1:B, :, :], x_in[1:B].rearrange("b (n p) e -> p b n e", p=P), "x_rest_in")
            sp.wait_ge(S["zero_pad_ready"], 1)
            for rows in (k_rows, v_rows):
                for edge_row in (0, T + WINDOW):
                    load(rows[:, edge_row:edge_row + WINDOW, :].rearrange("b w e -> w b e"), zero_pad, "pads_written")

            def line(b, per, off=0):
                return b[0] * per + (per * b[1] + off)

            def after(b, n=1):
                return (b[0], b[1] + n)

            def part(tensor, b, start=0, size=None):
                names = " ".join("abcdef"[:len(tensor.shape)])
                per = int(np.prod(tensor.shape[1:]))
                size = per if size is None else size
                flat = tensor.rearrange(f"{names} -> ({names})")
                at_ = line(b, per, start)
                return flat[at_:at_ + size] if isinstance(at_, int) else flat[bass.ds(at_, size)]

            def sp_wait(s, value):
                wait(sp, s, value)

            def save_xnT(b):
                sp_wait(S["xnT_ready"], line(b, 1, 1))
                sp.dma_start(part(xnT_dram, b).rearrange("(p t) -> p t", t=T), xnT[:, :]).then_inc(S["xnT_saved"], 16)

            def save_kv(b):
                sp_wait(S["nat_ready"], line(b, TB, TB))
                for rows, c in ((k_rows, E), (v_rows, 2 * E)):
                    dst = part(rows, b, WINDOW * E, T * E).rearrange("(n p e) -> p n e", p=P, e=E)
                    sp.dma_start(dst, nat[:, :, c:c + E]).then_inc(S["kv_saved"], 16)

            def windows(rows, b):
                v = part(rows, b, 0, T * E).rearrange("(n p e) -> p n e", p=P, e=E)
                return bass.AP(tensor=v.tensor, offset=v.offset, ap=[list(v.ap[0]), list(v.ap[1]), [1, J * E]])

            def load_k_near(b):
                sp_wait(S["kv_saved"], line(b, 32, 32))
                sp.dma_start(k_near[:, :, :], windows(k_rows, b)).then_inc(S["k_near_in"], 16)

            def load_v_near(b):
                sp_wait(S["near_v_parts"], line(b, TB))
                sp.dma_start(v_near[:, :, :], windows(v_rows, b)).then_inc(S["v_near_in"], 16)

            def save_parts(b):
                for n, (dst, src) in enumerate(((q_parts_dram, q_parts), (k_parts_dram, k_parts))):
                    sp_wait(S["split_ready"], line(b, 2, n + 1))
                    for i in range(PARTS):
                        d = part(dst, b, i * E * T, E * T).rearrange("(d h t) -> h d t", h=H, t=T)
                        sp.dma_start(d, src[:, i, :]).then_inc(S["parts_saved"], 16)

            def pack(b, q, free):
                sp_wait(S["st_ps"], free)
                sp.dma_start(Q[C_ROW:C_ROW + 2, q, :, :].rearrange("p g t -> p (g t)"), zero_rows[:, :]).then_inc(packed[q], 16)
                sp_wait(S["parts_saved"], line(b, 16 * 2 * PARTS, 16 * 2 * PARTS))
                size, row = G * T, H * T
                src = part(q_parts_dram, b, q * size, size)
                src = bass.AP(tensor=src.tensor, offset=src.offset, ap=[[0, PARTS], [row, PARTS * D], [1, size]])
                dst = Q[0:QK_ROWS, q, :, :].rearrange("p g t -> p (g t)")
                sp.dma_start(dst, src).then_inc(packed[q], 16)
                for i in range(PARTS):
                    src = part(k_parts_dram, b, i * E * T + q * size, size)
                    src = bass.AP(tensor=src.tensor, offset=src.offset, ap=[[0, PARTS], [row, D], [1, size]])
                    dst = K[i * PARTS * D:(i + 1) * PARTS * D, q, :, :].rearrange("p g t -> p (g t)")
                    sp.dma_start(dst, src).then_inc(packed[q], 16)

            zero = (0, 0)
            save_xnT(zero)
            save_kv(zero)
            sp_wait(S["pads_written"], 64)
            load_k_near(zero)
            save_parts(zero)
            sp_wait(S["rows_set"], 3)
            for q in range(3):
                pack(zero, q, 0)
            load_v_near(zero)

            def body(b, first, last):
                units = QUADS * UNITS
                nxt = after(b)
                if not first:
                    load_v_near(b)
                pack(b, 3, line(b, units))
                if not last:
                    save_xnT(nxt)
                    save_kv(nxt)
                    load_k_near(nxt)
                    save_parts(nxt)
                    for q in range(QUADS - 1):
                        pack(nxt, q, line(b, units, UNITS * (q + 1)))
                if last:
                    sp_wait(S["xnT_saved"], 16 * B)
                    for q in range(QUADS):
                        sp_wait(S["st_ps"], line(b, units, UNITS * (q + 1)))
                        sp.dma_start(xnT_all[:, 2 * q:2 * q + 2, :],
                                     xnT_dram[2 * q:2 * q + 2].rearrange("b p t -> p b t"))\
                            .then_inc(S["xnT_back"] if q else S["xnT_back_first"], 16)

            body((0, 0), True, False)
            with sp.Fori(0, B - 2) as i:
                body((i, 1), False, False)
            body((0, B - 1), False, True)

            ov = out.rearrange("b (n p) e -> b p n e", p=P)
            with sp.Fori(0, B // 2) as i:
                for half, s in enumerate(("out_even", "out_odd")):
                    sp_wait(S["ffn_ready"], 2 * i + half + 1)
                    dst = ov[at(2 * i + half), :, :, :].rearrange("o p n e -> p (o n) e")
                    sp.dma_start(dst, ffn_out[:, half, :].rearrange("p (n e) -> p n e", e=E)).then_inc(S[s], 16)
            sp_wait(S["out_even"], 16 * B // 2)
            sp_wait(S["out_odd"], 16 * B // 2)

        @block.tensor
        def _(pe):
            def transposes_xn(b, bank_free):
                bank_free()
                pe.wait_ge(S["xn_ready"], TB * (b + 1))
                for n in range(TB):
                    ins = pe.transpose(m1[:, n * P:(n + 1) * P], xn[:, n, :], ident[:, :])
                ins.then_inc(S["xnT_ps"], 1)

            def project(b, n):
                bank = (m1, m2)[n % 2]
                pe.wait_ge(S["xnT_ready"], b + 1)
                if n >= 2:
                    pe.wait_ge(S["nat_ready"], TB * b + n - 1)
                pe.matmul(bank[:, 0:NPROJ], xnT[:, n * P:(n + 1) * P], wcat[:, :], start=True, stop=False)
                pe.matmul(bank[:, 0:NPROJ], ones_rows[:, :], brow_parts[:, 0:NPROJ], start=False, stop=True)\
                    .then_inc(S["nat_ps"], 1)

            def project_T(b, n):
                pe.wait_ge(S["nat_ready"], TB * b + 3 + n)
                pe.matmul((m1, m2)[n][:, :], wcat[:, n * E:(n + 1) * E], xnT[:, :], start=True, stop=True)\
                    .then_inc(S["qkT_ps"], 1)

            def relative(b, n):
                bank = (m1, m2)[n % 2]
                if n < 2:
                    pe.wait_ge(S["qkT_ready"], 2 * b + n + 1)
                else:
                    pe.wait_ge(S["rel_ready"], TB * b + n - 1)
                at_edge = n in (0, TB - 1)
                ins = pe.matmul(bank[:, 0:JH], qT[:, n * P:(n + 1) * P], ek_block[:, :, :].rearrange("p j h -> p (j h)"),
                                start=True, stop=not at_edge)
                if at_edge:
                    ins = pe.matmul(bank[:, 0:JH], ident[:, :], edge[:, n // (TB - 1), :], start=False, stop=True)
                ins.then_inc(S["rel_ps"], 1)

            def s_unit(b, q, u):
                if u == 0:
                    pe.wait_ge(packed[q], 16 * PACK_DMAS * (b + 1))
                done = QUADS * UNITS * b + UNITS * q + u
                wait(pe, S["max_ready"], done - 1)
                g, n = u // TB, u % TB
                bank = s_bank[u % 2]
                pe.matmul(bank[:, :], Q[:, q, g, n * P:(n + 1) * P], K[:, q, g, :], start=True, stop=True)
                cols, mask = band_columns(n)
                pe.matmul(bank[:, cols], ident_b[:, :], band_b[:, mask], start=False, stop=True,
                          skip_group_check=True).then_inc(S["s_ps"], 1)

            def st_unit(b, q, u):
                if u == 0:
                    pe.wait_ge(c_rows_in[q], 16 * (b + 1))
                done = QUADS * UNITS * b + UNITS * q + u
                wait(pe, S["exp_ready"], done - 1)
                n, g = u // G, u % G
                bank = st_bank[u % 2]
                pe.matmul(bank[:, :], K[:, q, g, n * P:(n + 1) * P], Q[:, q, g, :], start=True, stop=True)
                cols, mask = band_columns(n)
                pe.matmul(bank[:, cols], ident_b[:, :], band_b[:, mask], start=False, stop=True,
                          skip_group_check=True).then_inc(S["st_ps"], 1)

            def pv(b, q, n):
                pe.wait_ge(S["exp_ready"], QUADS * UNITS * b + UNITS * q + G * (n + 1))
                if n == 0:
                    pe.wait_ge(S["vaug_ready"], QUADS * b + q + 1)
                    wait(pe, S["pvT_ready"], QUADS * b + q)
                    if isinstance(b, int) and b == 0 and q == 0:
                        pe.wait_ge(S["pv_clear"], 1)
                for g in range(G):
                    ins = pe.matmul(pv_bank[VW * g:VW * g + D + 1, :], vaug[:, q, n, g, :], PT[:, n, g, :],
                                    start=(n == 0), stop=(n == TB - 1))
                ins.then_inc(S["pv_ps"], 1)

            def transpose_o(b, q):
                pe.wait_ge(S["pvT_ready"], QUADS * b + q + 1)
                if isinstance(b, int) and QUADS * b + q + 3 > QUADS * B:
                    pe.wait_ge(S["o_raw_ready"], QUADS * b + q)
                else:
                    wait(pe, S["cT_ready"], QUADS * b + q + 3)
                for n in range(TB):
                    ins = pe.transpose(m0[:, n * P:(n + 1) * P], pvT[:, n * P:(n + 1) * P], ident[:, :])
                ins.then_inc(S["o_ps"], 1)

            def transpose_c(b, q):
                pe.wait_ge(S["c_ready"], QUADS * b + q + 1)
                wait(pe, S["o_raw_ready"], QUADS * b + q - 2)
                pe.transpose(m0_b[0:2 * UNITS, 0:P], c_parts[:, :, :, :].rearrange("p i g n -> p (i g n)"),
                             ident_b[:, :]).then_inc(S["cT_ps"], 1)

            def near_transposes(b, n, bank_free=None):
                if bank_free is not None:
                    bank_free()
                else:
                    pe.wait_ge(S["near_pT_ready"], TB * b + n)
                pe.wait_ge(S["near_p_ready"], b + 1)
                flat = near_p[:, n, :, :].rearrange("p j h -> p (j h)")
                pe.transpose(m1[:, 0:P], flat[:, 0:P], ident[:, :])
                pe.transpose(m1[0:H, P:2 * P], flat[:, P:JH], ident[:, :]).then_inc(S["near_pT_ps"], 1)

            def near_times_ev(b, n, bank_free=None):
                if bank_free is not None:
                    bank_free()
                pe.wait_ge(S["near_pT_ready"], TB * b + n + 1)
                cols = slice(n * P, (n + 1) * P)
                pe.matmul(m2[:, cols], near_pT[:, n % 2, 0, :], ev_block0[:, :, :].rearrange("p h d -> p (h d)"),
                          start=True, stop=False)
                ins = pe.matmul(m2[:, cols], near_pT[0:H, n % 2, 1, :], ev_block1[:, :, :].rearrange("p h d -> p (h d)"),
                                start=False, stop=True)
                ins.then_inc(S["ev_ps"], 1)

            def transpose_attn(b, bank_free):
                bank_free()
                pe.wait_ge(S["o_ready"], b + 1)
                for n in range(TB):
                    ins = pe.transpose(m1[:, n * P:(n + 1) * P], o_nat[:, n, :], ident[:, :])
                ins.then_inc(S["oT_ps"], 1)

            def project_out(b, bank_free):
                bank_free()
                pe.wait_ge(S["oT_ready"], b + 1)
                for n in range(TB):
                    cols = slice(n * P, (n + 1) * P)
                    pe.matmul(m2[:, cols], oT[:, cols], wo[:, :], start=True, stop=False)
                    ins = pe.matmul(m2[:, cols], ones_rows[:, :], brow_parts[:, NPROJ:NPROJ + E], start=False, stop=True)
                ins.then_inc(S["wo_ps"], 1)

            pe.wait_ge(S["first_in"], 16)
            transposes_xn(0, lambda: None)
            pe.wait_ge(S["scaled"], 2)
            pe.wait_ge(S["bias_ready"], 1)
            for n in range(TB):
                project(0, n)
            for n in range(2):
                project_T(0, n)
            pe.wait_ge(S["blocks_ready"], 3)
            for n in range(TB):
                relative(0, n)
            pe.wait_ge(S["masks_ready"], 2)
            for q in range(2):
                for u in range(UNITS):
                    s_unit(0, q, u)
                if q == 0:
                    transpose_c(0, 0)

            def body(b, last):
                first = isinstance(b, int) and b == 0
                m1_after_near = lambda: wait(pe, S["near_pT_ready"], TB * b)
                for q in range(QUADS):
                    for u in range(UNITS):
                        st_unit(b, q, u)
                        if u % G == 1:
                            if u >= G:
                                pv(b, q, u // G - 1)
                            elif q > 0:
                                pv(b, q - 1, TB - 1)
                            elif not first:
                                pv(b - 1, QUADS - 1, TB - 1)
                        if q < 2:
                            s_unit(b, q + 2, u)
                        elif not last:
                            s_unit(b + 1, q - 2, u)
                        if u == 8:
                            if q > 0:
                                transpose_o(b, q - 1)
                            elif not first:
                                transpose_o(b - 1, QUADS - 1)
                        if u == 3:
                            if q < QUADS - 1:
                                transpose_c(b, q + 1)
                            elif not last:
                                transpose_c(b + 1, 0)
                        if last and q == 0 and u == 4:
                            m1_after_near()
                            pe.wait_ge(S["route_ready"], 1)
                            for n in range(TB):
                                ins = pe.transpose(m1[0:B * NEXP, n * P:(n + 1) * P], route[:, n, :], ident[:, :])
                            ins.then_inc(S["route_ps"], 1)
                        if q == 0 and not last:
                            if u == 5:
                                transposes_xn(b + 1, m1_after_near)
                            if 8 <= u < 12:
                                if u == 9:
                                    wait(pe, S["near_ev_ready"], b)
                                project(b + 1, u - 8)
                            if u in (12, 13):
                                project_T(b + 1, u - 12)
                        if q == 1:
                            if not last and u in (3, 4, 7, 8):
                                relative(b + 1, (3, 4, 7, 8).index(u))
                            if not first and u == 10:
                                transpose_attn(b - 1, (lambda: pe.wait_ge(S["route_kept"], 1)) if last else
                                               lambda: pe.wait_ge(S["rel_ready"], TB * (b + 1) + 3))
                            if not first and u == 13:
                                project_out(b - 1, (lambda: pe.wait_ge(S["near_ev_ready"], b)) if last else
                                            (lambda: pe.wait_ge(S["rel_ready"], TB * (b + 1) + 4)))
                        if q == 2:
                            if u in (6, 8, 10, 12):
                                n = (6, 8, 10, 12).index(u)
                                near_transposes(b, n, None if n else
                                                (lambda: pe.wait_ge(S["rel_ready"], TB + 3)) if first else
                                                (lambda: pe.wait_ge(S["oT_ready"], b)))
                            if u in (8, 10, 12, 14):
                                n = (8, 10, 12, 14).index(u)
                                near_times_ev(b, n, None if n else
                                              (lambda: pe.wait_ge(S["rel_ready"], TB + 4)) if first else
                                              (lambda: pe.wait_ge(S["x_res_ready"], b)))

            body(0, False)
            with pe.Fori(1, B - 1) as b:
                body(b, False)
            body(B - 1, True)
            pv(B - 1, QUADS - 1, TB - 1)
            h_bank = (st_bank[0], st_bank[1], s_bank[0], s_bank[1])
            y_bank = (pv_bank, m0)

            def ffn_hidden(i):
                for half in range(2):
                    for c in range(2):
                        bank = h_bank[2 * half + c]
                        pe.matmul(bank[:, :], w1[:, c * P:(c + 1) * P],
                                  xnT_all[:, at(2 * i + half), :].rearrange("p o t -> p (o t)"), start=True, stop=False)
                        rows = expert_rows[:, span((2 * i + half) * NEXP + 4 * c, 4), :].rearrange("p e h -> p (e h)")
                        pe.matmul(bank[:, :], rows, sel_m1[:, :], start=False, stop=True).then_inc(S["h_ps"], 1)

            def ffn_sums(i):
                for half in range(2):
                    pe.wait_ge(S["g_ready"], 4 * i + 2 * half + 2)
                    if isinstance(i, int) and half == 0:
                        pe.wait_ge(S["b2_rows_ready"], PARTS)
                    wait(pe, S["ffn_ready"], 2 * i + half - 1)
                    for n in range(TB):
                        cols = slice(n * P, (n + 1) * P)
                        for c in range(2):
                            pe.matmul(y_bank[half][:, cols], g_hid[:, half, c, cols], w2[:, c, :],
                                      start=(c == 0), stop=False)
                        for k in range(PARTS):
                            ins = pe.matmul(y_bank[half][:, cols], sel[:, cols],
                                            b2_rows[:, at(2 * i + half), k, :].rearrange("p o e -> p (o e)"),
                                            start=False, stop=(k == PARTS - 1))
                    ins.then_inc(S["y_ps"], 1)

            pe.wait_ge(S["xnT_back_first"], 16)
            pe.wait_ge(S["sel_ready"], 1)
            ffn_hidden(0)
            pe.wait_ge(S["pvT_ready"], QUADS * B)
            pe.wait_ge(S["o_raw_ready"], QUADS * B - 1)
            for n in range(TB):
                ins = pe.transpose(m0[:, n * P:(n + 1) * P], pvT[:, n * P:(n + 1) * P], ident[:, :])
            ins.then_inc(S["o_ps"], 1)
            pe.wait_ge(S["o_raw_ready"], QUADS * B)
            ffn_sums(0)
            transpose_attn(B - 1, lambda: pe.wait_ge(S["near_pT_ready"], TB * B))
            project_out(B - 1, lambda: pe.wait_ge(S["near_ev_ready"], B))
            pe.wait_ge(S["xnT_back"], 16 * (QUADS - 1))
            with pe.Fori(1, B // 2) as i:
                ffn_hidden(i)
                ffn_sums(i)

        @block.scalar
        def _(act):
            def normalize(b, blocks):
                for n in blocks:
                    if n == 0:
                        wait(act, S["xnT_ps"], b)
                    c = b * TB + n
                    col = slice(c, c + 1) if isinstance(c, int) else bass.ds(c, 1)
                    act.activation(xn[:, n, :], x_all[:, at(b), n, :].rearrange("p o e -> p (o e)"), ACT.Identity,
                                   bias=shift[:, col], scale=rstd[:, col]).then_inc(S["xn_ready"], 1)

            def copy_xnT(b):
                act.wait_ge(S["xnT_ps"], b + 1)
                wait(act, S["xnT_saved"], 16 * b)
                act.activation(xnT[:, :], m1[:, :], ACT.Copy).then_inc(S["xnT_ready"], 1)

            def copy_nat(b, n):
                act.wait_ge(S["nat_ps"], TB * b + n + 1)
                if n == 0:
                    wait(act, S["kv_saved"], 32 * b)
                    wait(act, S["qk_prod_ready"], TB * b)
                    wait(act, S["vaug_ready"], QUADS * b)
                    wait(act, S["gates_ready"], b)
                act.activation(nat[:, n, :], (m1, m2)[n % 2][:, 0:NPROJ], ACT.Copy).then_inc(S["nat_ready"], 1)

            def copy_qkT(b, n):
                act.wait_ge(S["qkT_ps"], 2 * b + n + 1)
                wait(act, S["split_ready"], 2 * b - 1 + n)
                wait(act, S["parts_saved"], 16 * 2 * PARTS * b)
                act.activation((q_parts, k_parts)[n][:, 0, :], (m1, m2)[n][:, :], ACT.Identity, bias=bqk[:, n:n + 1])
                act.activation((qT, kT)[n][:, :], (m1, m2)[n][:, :], ACT.Identity, bias=bqk[:, n:n + 1])\
                    .then_inc(S["qkT_ready"], 1)

            def copy_rel(b, n):
                act.wait_ge(S["rel_ps"], TB * b + n + 1)
                if n == 0:
                    wait(act, S["near_ready"], b)
                act.activation(rel[:, n, :], (m1, m2)[n % 2][:, 0:JH], ACT.Copy).then_inc(S["rel_ready"], 1)

            def exp_unit(b, q, u):
                done = QUADS * UNITS * b + UNITS * q + u
                act.wait_ge(S["st_ps"], done + 1)
                n, g = u // G, u % G
                if g == 0:
                    wait(act, S["pv_ps"], QUADS * TB * b + TB * q + n - TB + 1)
                act.activation(PT[:, n, g, :], st_bank[u % 2][:, :], ACT.Exp).then_inc(S["exp_ready"], 1)

            def copy_pv(b, q):
                act.wait_ge(S["pv_ps"], QUADS * TB * b + TB * (q + 1))
                wait(act, S["o_ps"], QUADS * b + q)
                act.activation(pvT[:, :], pv_bank[:, :], ACT.Copy).then_inc(S["pvT_ready"], 1)

            def copy_c(b, q):
                act.wait_ge(S["cT_ps"], QUADS * b + q + 1)
                if q > 0:
                    act.wait_ge(c_rows_in[q - 1], 16 * (b + 1))
                elif not (isinstance(b, int) and b == 0):
                    act.wait_ge(c_rows_in[QUADS - 1], 16 * b)
                act.activation(cT[:, :], m0_b[0:2 * UNITS, 0:P], ACT.Copy).then_inc(S["cT_ready"], 1)
                act.wait_ge(S["cT_ready"], QUADS * b + q + 1)
                act.dma_start(Q[C_ROW:C_ROW + 2, q, :, :], cT[:, :]).then_inc(c_rows_in[q], 16)

            def gates_exp(b):
                act.wait_ge(S["g_shift_ready"], b + 1)
                act.activation(g_exp[:, :, :], g_exp[:, :, :], ACT.Exp).then_inc(S["g_exp_ready"], 1)

            def near_exp(b):
                act.wait_ge(S["near_c_ready"], b + 1)
                wait(act, S["near_pT_ps"], TB * b)
                wait(act, S["near_v_ready"], b)
                wait(act, S["near_den_ready"], b)
                act.activation(near_p[:, :, :, :].rearrange("p n j h -> p (n j h)"),
                               near_p[:, :, :, :].rearrange("p n j h -> p (n j h)"), ACT.Exp).then_inc(S["near_p_ready"], 1)

            def copy_near_pT(b, n):
                act.wait_ge(S["near_pT_ps"], TB * b + n + 1)
                wait(act, S["ev_ps"], TB * b + n - 1)
                act.activation(near_pT[:, n % 2, 0, :], m1[:, 0:P], ACT.Copy)
                act.activation(near_pT[0:H, n % 2, 1, :], m1[0:H, P:2 * P], ACT.Copy).then_inc(S["near_pT_ready"], 1)

            def copy_ev(b):
                act.wait_ge(S["ev_ps"], TB * (b + 1))
                wait(act, S["near_v_ready"], b)
                act.activation(near_ev[:, :, :].rearrange("p n e -> p (n e)"), m2[:, :], ACT.Copy)\
                    .then_inc(S["near_ev_ready"], 1)

            def copy_oT(b):
                act.wait_ge(S["oT_ps"], b + 1)
                wait(act, S["wo_ps"], b)
                act.activation(oT[:, :], m1[:, :], ACT.Copy).then_inc(S["oT_ready"], 1)

            act.dma_start(front_data[:, :], first_in).then_inc(S["first_in"], 16)
            act.dma_start(rest_data[:, :], rest_in).then_inc(S["rest_in"], 16)
            act.wait_ge(S["stats0_ready"], 1)
            normalize(0, range(TB))
            copy_xnT(0)
            for n in range(TB):
                copy_nat(0, n)
            act.wait_ge(S["scaled"], 2)
            for n in range(2):
                copy_qkT(0, n)
            for n in range(TB):
                copy_rel(0, n)
            gates_exp(0)
            copy_c(0, 0)
            act.wait_ge(S["stats_ready"], 1)

            def body(b, last):
                first = isinstance(b, int) and b == 0
                for q in range(QUADS):
                    for u in range(UNITS):
                        exp_unit(b, q, u)
                        if u == 3:
                            if q > 0:
                                copy_pv(b, q - 1)
                            elif not first:
                                copy_pv(b - 1, QUADS - 1)
                        if u == 4:
                            if q < QUADS - 1:
                                copy_c(b, q + 1)
                            elif not last:
                                copy_c(b + 1, 0)
                        if q == 0 and not last:
                            if u < TB:
                                normalize(b + 1, (u,))
                            if u == 5:
                                copy_xnT(b + 1)
                            if 8 <= u < 12:
                                copy_nat(b + 1, u - 8)
                            if u in (12, 13):
                                copy_qkT(b + 1, u - 12)
                        if q == 1:
                            if not last and u in (3, 4, 7, 8):
                                copy_rel(b + 1, (3, 4, 7, 8).index(u))
                            if not first and u == 10:
                                copy_oT(b - 1)
                        if q == 2 and u == 2:
                            near_exp(b)
                        if q == 1 and u == 1 and not last:
                            gates_exp(b + 1)
                        if q == 2 and u in (6, 8, 10, 12):
                            copy_near_pT(b, (6, 8, 10, 12).index(u))
                        if q == 2 and u == 15:
                            copy_ev(b)

            body(0, False)
            with act.Fori(1, B - 1) as b:
                body(b, False)
            body(B - 1, True)
            copy_pv(B - 1, QUADS - 1)

            def ffn(i):
                for half in range(2):
                    for c in range(2):
                        act.wait_ge(S["h_ps"], 4 * i + 2 * half + c + 1)
                        wait(act, S["y_ps"], 2 * i + half - 1)
                        bank = (st_bank[0], st_bank[1], s_bank[0], s_bank[1])[2 * half + c]
                        act.activation(g_hid[:, half, c, :], bank[:, :], ACT.Gelu, bias=b1[:, c:c + 1])\
                            .then_inc(S["g_ready"], 1)

            ffn(0)
            copy_oT(B - 1)
            with act.Fori(1, B // 2) as i:
                ffn(i)

        @block.gpsimd
        def _(pool):
            own = Steps(pool, S["pool_step"])

            def split(b, n):
                src, parts = ((qT, q_parts), (kT, k_parts))[n]
                pool.wait_ge(S["qkT_ready"], 2 * b + n + 1)
                wait(pool, S["split_ready"], 2 * b + n)
                own.did(pool.tensor_tensor(rest1[:, :], src[:, :], parts[:, 0, :], ALU.subtract))
                own.did(pool.tensor_tensor(parts[:, 1, :], src[:, :], parts[:, 0, :], ALU.subtract))
                own.settle()
                pool.tensor_tensor(parts[:, 2, :], rest1[:, :], parts[:, 1, :], ALU.subtract).then_inc(S["split_ready"], 1)

            def near_products(b, n):
                pool.wait_ge(S["k_near_in"], 16 * (b + 1))
                pool.wait_ge(S["nat_ready"], TB * b + n + 1)
                wait(pool, S["near_qk_ready"], TB * b + n - 1)
                q_rep = nat[:, n, 0:E].rearrange("p (o e) -> p o e", o=1).to_broadcast([P, J, E])
                own.did(pool.tensor_tensor(qk_prod[:, n % 2, :].rearrange("p (j e) -> p j e", j=J),
                                           k_near[:, n, :].rearrange("p (j e) -> p j e", j=J), q_rep, ALU.mult))
                own.settle()
                halves = qk_prod[:, n % 2, :].rearrange("p (m i d) -> p m i d", i=2, d=D // 2)
                pool.tensor_tensor(halves[:, :, 0, :], halves[:, :, 0, :], halves[:, :, 1, :], ALU.add)\
                    .then_inc(S["qk_prod_ready"], 1)

            def fill_vaug(b, q):
                pool.wait_ge(S["nat_ready"], TB * (b + 1))
                wait(pool, S["pv_ps"], QUADS * TB * (b - 1) + TB * (q + 1))
                c = 2 * E + q * G * D
                one = one_col[:, :].rearrange("p (n o) -> p n o", n=1).to_broadcast([P, G, D])
                for n in range(TB):
                    ins = pool.tensor_tensor(vaug[:, q, n, :, 0:D], nat[:, n, c:c + G * D].rearrange("p (g d) -> p g d", d=D),
                                             one, ALU.mult)
                ins.then_inc(S["vaug_ready"], 1)

            def near_values(b, n):
                pool.wait_ge(S["v_near_in"], 16 * (b + 1))
                pool.wait_ge(S["near_p_ready"], b + 1)
                if n == 0:
                    wait(pool, S["o_ready"], b)
                wait(pool, S["near_v_parts"], TB * b + n)
                p_rep = near_p[:, n, :, :].rearrange("p j (h o) -> p (j h) o", o=1).to_broadcast([P, JH, D])
                own.did(pool.tensor_tensor(pv_prod[:, :, :].rearrange("p j (h d) -> p (j h) d", d=D),
                                           v_near[:, n, :].rearrange("p (m d) -> p m d", d=D), p_rep, ALU.mult))
                own.settle()
                for half in (4, 2, 1):
                    own.did(pool.tensor_tensor(pv_prod[:, 0:half, :], pv_prod[:, 0:half, :], pv_prod[:, half:2 * half, :], ALU.add))
                    own.settle()
                pool.tensor_tensor(near_v[:, n, :], pv_prod[:, 0, :], pv_prod[:, J - 1, :], ALU.add).then_inc(S["near_v_parts"], 1)

            def add_near_ev(b):
                pool.wait_ge(S["near_v_parts"], TB * (b + 1))
                pool.wait_ge(S["near_ev_ready"], b + 1)
                pool.tensor_tensor(near_v[:, :, :], near_v[:, :, :], near_ev[:, :, :], ALU.add).then_inc(S["near_v_ready"], 1)

            pool.memset(minus_half[:, :], -0.5).then_inc(S["setup_pool"], 1)
            pool.memset(zero_pad, 0.0).then_inc(S["zero_pad_ready"], 1)
            pool.wait_ge(S["setup_pool"], 1)
            pool.wait_ge(S["eps0_ready"], 1)
            pool.tensor_tensor(rstd[:, 0:TB], var_eps[:, 0:TB], minus_half[:, 0:TB], ALU.pow).then_inc(S["pow0_ready"], 1)
            pool.memset(zero_rows[:, :], 0.0).then_inc(S["rows_set"], 1)
            pool.memset(Q[:, :, :, :].rearrange("p q g t -> p (q g t)").bitcast(int32), 0).then_inc(S["rows_set"], 1)
            pool.memset(K[:, :, :, :].rearrange("p q g t -> p (q g t)").bitcast(int32), TWO_ONES).then_inc(S["rows_set"], 1)
            own.did(pool.memset(one_col[:, :], 1.0))
            own.did(pool.memset(vaug[:, :, :, :, :].rearrange("p q n g c -> p (q n g c)"), 0.0))
            own.settle()
            own.did(pool.memset(vaug[:, :, :, :, D:D + 1].rearrange("p q n g o -> p (q n g) o"), 1.0))
            own.settle()
            for n in range(TB):
                near_products(0, n)
                if n == 1:
                    pool.wait_ge(S["eps_ready"], 1)
                    pool.tensor_tensor(rstd[:, TB:], var_eps[:, TB:], minus_half[:, TB:], ALU.pow).then_inc(S["pow_ready"], 1)
            for q in range(QUADS):
                fill_vaug(0, q)

            def body(b, last):
                first = isinstance(b, int) and b == 0
                if not first:
                    fill_vaug(b, QUADS - 1)
                if not last:
                    for n in range(2):
                        split(b + 1, n)
                    for n in range(TB):
                        near_products(b + 1, n)
                    for q in range(2):
                        fill_vaug(b + 1, q)
                for n in range(TB):
                    near_values(b, n)
                add_near_ev(b)
                if not last:
                    fill_vaug(b + 1, 2)

            body(0, False)
            steps = 2 * 2 + TB * (4 + 1)
            start = own.n
            with pool.Fori(1, B - 1) as b:
                own.n = (b - 1) * steps + start
                body(b, False)
            own.n = start + (B - 2) * steps
            body(B - 1, True)

        @block.vector
        def _(dve):
            own = Steps(dve, S["dve_step"])

            def three_parts(dst, src, rest, part):
                own.did(dve.tensor_copy(dst(0), src))
                own.settle()
                own.did(dve.tensor_tensor(rest, src, dst(0), ALU.subtract))
                own.settle()
                own.did(dve.tensor_copy(dst(1), rest))
                own.settle()
                own.did(dve.tensor_tensor(dst(2), rest, dst(1), ALU.subtract))
                own.settle()

            def sum_near_qk(b, n):
                dve.wait_ge(S["qk_prod_ready"], TB * b + n + 1)
                if n == 0:
                    wait(dve, S["near_ready"], b)
                dve.tensor_reduce(near_qk[:, n, :], qk_prod[:, n % 2, :].rearrange("p (m d) -> p m d", d=D)[:, :, 0:D // 2],
                                  AX.X, ALU.add)\
                    .then_inc(S["near_qk_ready"], 1)

            def near_logits(b):
                own.settle()
                dve.wait_ge(S["near_qk_ready"], TB * (b + 1))
                dve.wait_ge(S["rel_ready"], TB * (b + 1))
                wait(dve, S["near_c_ready"], b)
                dve.tensor_tensor(near[:, :, :, :].rearrange("p n j h -> p n (j h)"), near_qk[:, :, :], rel[:, :, :], ALU.add)\
                    .then_inc(S["near_ready"], 1)

            def near_maxima(b):
                dve.wait_ge(S["near_ready"], b + 1)
                own.did(dve.tensor_reduce(neg_near[:, :, :], near[:, :, :, :].rearrange("p n j h -> p n h j"), AX.X, ALU.max,
                                          negate=True))

            def max_unit(b, q, u):
                dve.wait_ge(S["s_ps"], QUADS * UNITS * b + UNITS * q + u + 1)
                dve.tensor_reduce(neg_max[:, u // TB, u % TB:u % TB + 1], s_bank[u % 2][:, :], AX.X, ALU.max, negate=True)\
                    .then_inc(S["max_ready"], 1)

            def row_maximum(b, q):
                hs = slice(q * G, q * G + G)
                own.settle()
                dve.wait_ge(S["max_ready"], QUADS * UNITS * b + UNITS * (q + 1))
                own.did(dve.tensor_tensor(neg_c[:, :, :], neg_max[:, :, :], neg_near[:, :, hs].rearrange("p n g -> p g n"), ALU.min))
                own.settle()
                wait(dve, S["cT_ps"], QUADS * b + q)
                own.did(dve.tensor_copy(c_parts[:, 0, :, :], neg_c[:, :, :]))
                own.settle()
                dve.tensor_tensor(c_parts[:, 1, :, :], neg_c[:, :, :], c_parts[:, 0, :, :], ALU.subtract).then_inc(S["c_ready"], 1)
                dve.wait_ge(S["c_ready"], QUADS * b + q + 1)
                own.did(dve.tensor_tensor(c_used[:, :, hs], c_parts[:, 0, :, :].rearrange("p g n -> p n g"),
                                          c_parts[:, 1, :, :].rearrange("p g n -> p n g"), ALU.add))

            def near_minus_max(b):
                own.settle()
                c_rep = c_used[:, :, :].rearrange("p n (o h) -> p n o h", o=1).to_broadcast([P, TB, J, H])
                wait(dve, S["near_p_ready"], b)
                dve.tensor_tensor(near_p[:, :, :, :], near[:, :, :, :], c_rep, ALU.add).then_inc(S["near_c_ready"], 1)

            def near_sums(b):
                dve.wait_ge(S["near_p_ready"], b + 1)
                dve.tensor_reduce(near_den[:, :, :], near_p[:, :, :, :].rearrange("p n j h -> p n h j"), AX.X, ALU.add)\
                    .then_inc(S["near_den_ready"], 1)

            def gates_shift(b):
                dve.wait_ge(S["nat_ready"], TB * (b + 1))
                gl = nat[:, :, 3 * E:NPROJ]
                own.did(dve.tensor_reduce(g_max[:, :], gl, AX.X, ALU.max))
                own.settle()
                gm = g_max[:, :].rearrange("p (n o) -> p n o", o=1).to_broadcast([P, TB, NEXP])
                dve.tensor_tensor(g_exp[:, :, :], gl, gm, ALU.subtract).then_inc(S["g_shift_ready"], 1)

            def gates_compare(b):
                other = nat[:, :, 3 * E:NPROJ].rearrange("p n (o f) -> p n o f", o=1).to_broadcast([P, TB, NEXP, NEXP])
                mine = nat[:, :, 3 * E:NPROJ].rearrange("p n (e o) -> p n e o", o=1).to_broadcast([P, TB, NEXP, NEXP])
                own.did(dve.tensor_tensor(pair_eq[:, :, :, :], other, mine, ALU.is_equal))
                dve.tensor_tensor(pair_gt[:, :, :, :], other, mine, ALU.is_gt).then_inc(S["gates_ready"], 1)

            def gates_count(b):
                own.settle()
                tri = earlier[:, :].rearrange("p (o m) -> p o m", o=1).to_broadcast([P, TB, NEXP * NEXP])
                flat_eq = pair_eq[:, :, :, :].rearrange("p n e f -> p n (e f)")
                own.did(dve.tensor_tensor(flat_eq, flat_eq, tri, ALU.mult))
                own.settle()
                dve.wait_ge(S["gates_ready"], b + 1)
                own.did(dve.tensor_tensor(pair_gt[:, :, :, :], pair_gt[:, :, :, :], pair_eq[:, :, :, :], ALU.add))
                own.settle()
                own.did(dve.tensor_reduce(g_count[:, :, :], pair_gt[:, :, :, :], AX.X, ALU.add))

            def gates_score(b):
                dve.wait_ge(S["g_exp_ready"], b + 1)
                own.did(dve.tensor_reduce(g_sum[:, :], g_exp[:, :, :], AX.X, ALU.add))
                own.settle()
                own.did(dve.reciprocal(g_sum[:, :], g_sum[:, :]))
                own.settle()
                gr = g_sum[:, :].rearrange("p (n o) -> p n o", o=1).to_broadcast([P, TB, NEXP])
                own.did(dve.tensor_tensor(g_exp[:, :, :], g_exp[:, :, :], gr, ALU.mult))
                own.settle()
                own.did(dve.scalar_tensor_tensor(scores[:, :, at(b), :].rearrange("p n o e -> p n (o e)"), g_count[:, :, :],
                                                 float(TOPK), g_exp[:, :, :], ALU.is_lt, ALU.mult))

            def keep_o(b, q):
                dve.wait_ge(S["o_ps"], QUADS * b + q + 1)
                src = m0[:, :].rearrange("p (n g c) -> p n g c", n=TB, c=VW)
                dve.tensor_copy(o_raw[:, :, q * G:(q + 1) * G, :], src[:, :, :, 0:D + 1]).then_inc(S["o_raw_ready"], 1)

            def finish_attention(b):
                dve.wait_ge(S["o_raw_ready"], QUADS * (b + 1))
                dve.wait_ge(S["near_den_ready"], b + 1)
                own.did(dve.tensor_tensor(den[:, :, :], o_raw[:, :, :, D], near_den[:, :, :], ALU.add))
                own.settle()
                own.did(dve.reciprocal(rden[:, :, :], den[:, :, :]))
                dve.wait_ge(S["near_v_ready"], b + 1)
                own.did(dve.tensor_tensor(near_v[:, :, :].rearrange("p n (h d) -> p (n h) d", d=D),
                                          o_raw[:, :, :, 0:D].rearrange("p n h d -> p (n h) d"),
                                          near_v[:, :, :].rearrange("p n (h d) -> p (n h) d", d=D), ALU.add))
                own.settle()
                r_rep = rden[:, :, :].rearrange("p n (h o) -> p (n h) o", o=1).to_broadcast([P, TB * H, D])
                wait(dve, S["oT_ps"], b)
                dve.tensor_tensor(o_nat[:, :, :].rearrange("p n (h d) -> p (n h) d", d=D),
                                  near_v[:, :, :].rearrange("p n (h d) -> p (n h) d", d=D), r_rep, ALU.mult)\
                    .then_inc(S["o_ready"], 1)

            def add_residual(b):
                dve.wait_ge(S["wo_ps"], b + 1)
                xb = x_all[:, at(b), :, :].rearrange("p o n e -> p (o n e)")
                dve.tensor_tensor(xb, m2[:, :], xb, ALU.add).then_inc(S["x_res_ready"], 1)

            def batch_stats(b):
                for n in range(TB):
                    c = b * TB + n
                    col = slice(c, c + 1) if isinstance(c, int) else bass.ds(c, 1)
                    own.did(dve.bn_stats(stats[:, col, :].rearrange("p o s -> p (o s)"),
                                         x_all[:, at(b), n, :].rearrange("p o e -> p (o e)")))

            def gather_stats(first, end):
                own.settle()
                for c in range(first * TB, end * TB):
                    own.did(dve.bn_aggr(mean_var[:, c, :], stats[:, c, :]))

            def add_eps(cols, s):
                own.settle()
                dve.tensor_scalar(var_eps[:, cols], mean_var[:, cols, 1], LN_EPS, None, ALU.add).then_inc(S[s], 1)

            def shifts(cols, pow_ready, ready):
                dve.wait_ge(S[pow_ready], 1)
                dve.scalar_tensor_tensor(shift[:, cols], mean_var[:, cols, 0], -1.0, rstd[:, cols], ALU.mult, ALU.mult)\
                    .then_inc(S[ready], 1)

            dve.wait_ge(S["x0_in"], 16)
            batch_stats(0)
            gather_stats(0, 1)
            add_eps(slice(0, TB), "eps0_ready")
            dve.memset(brow_parts[:, :], 0.0).then_inc(S["dve_step"], 1)
            dve.memset(ones_rows[:, :], 1.0).then_inc(S["dve_step"], 1)
            own.n += 2
            dve.wait_ge(S["first_in"], 16)
            dve.tensor_scalar(wcat[:, 0:E], wcat[:, 0:E], SCALING, None, ALU.mult).then_inc(S["scaled"], 1)
            dve.tensor_scalar(bqk[:, 0:1], bqk[:, 0:1], SCALING, None, ALU.mult).then_inc(S["scaled"], 1)
            shifts(slice(0, TB), "pow0_ready", "stats0_ready")
            dve.wait_ge(S["brow_in"], 16)
            own.did(dve.tensor_scalar(brow[:, 0:E], brow[:, 0:E], SCALING, None, ALU.mult))
            own.settle()
            br = gtmp[0:PARTS, 1024:1024 + NPROJ + E]
            bparts = qk_prod[0:PARTS, :, :].rearrange("p a n -> p (a n)")[:, 0:3 * (NPROJ + E) // 2 + 2].bitcast(bf16)
            NB = NPROJ + E
            three_parts(lambda i: bparts[:, i * NB:(i + 1) * NB], brow, br, None)
            own.did(dve.tensor_scalar(brow_parts[0:PARTS, :], bparts[:, 0:NB], ident[0:PARTS, 0:1], None, ALU.mult))
            for i in (1, 2):
                own.settle()
                ins = dve.scalar_tensor_tensor(brow_parts[0:PARTS, :], bparts[:, i * NB:(i + 1) * NB], ident[0:PARTS, i:i + 1],
                                               brow_parts[0:PARTS, :], ALU.mult, ALU.add)
                if i == 1:
                    own.did(ins)
            ins.then_inc(S["bias_ready"], 1)
            dve.tensor_copy(ident_b[:, :], ident[:, :]).then_inc(S["masks_ready"], 1)
            dve.wait_ge(S["rest_in"], 16)
            dve.tensor_copy(band_b[:, :], band_f[:, :]).then_inc(S["masks_ready"], 1)
            ek_rep = ek[:, :].rearrange("p (j o) -> p j o", o=1).to_broadcast([P, J, H])
            hm_rep = headmask[:, :].rearrange("p (o h) -> p o h", o=1).to_broadcast([P, J, H])
            dve.tensor_tensor(ek_block[:, :, :], ek_rep, hm_rep, ALU.mult).then_inc(S["blocks_ready"], 1)
            for blk, ev, rows in ((ev_block0, ev0, P), (ev_block1, ev1, H)):
                ev_rep = ev[:, :].rearrange("p (o d) -> p o d", o=1).to_broadcast([rows, H, D])
                rm_rep = relmask[0:rows, :].rearrange("p (h o) -> p h o", o=1).to_broadcast([rows, H, D])
                dve.tensor_tensor(blk[:, :, :], ev_rep, rm_rep, ALU.mult).then_inc(S["blocks_ready"], 1)

            dve.wait_ge(S["x_rest_in"], 16)
            half_way = B // 2 + 1
            start = own.n
            with dve.Fori(1, half_way) as b:
                own.n = (b - 1) * TB + start
                batch_stats(b)
            own.n = start + (half_way - 1) * TB
            for n, (src, parts) in enumerate(((qT, q_parts), (kT, k_parts))):
                own.settle()
                dve.wait_ge(S["qkT_ready"], n + 1)
                own.did(dve.tensor_tensor(rest1[:, :], src[:, :], parts[:, 0, :], ALU.subtract))
                own.did(dve.tensor_tensor(parts[:, 1, :], src[:, :], parts[:, 0, :], ALU.subtract))
                own.settle()
                dve.tensor_tensor(parts[:, 2, :], rest1[:, :], parts[:, 1, :], ALU.subtract).then_inc(S["split_ready"], 1)
                dve.wait_ge(S["split_ready"], n + 1)
            start = own.n
            with dve.Fori(half_way, B) as b:
                own.n = (b - half_way) * TB + start
                batch_stats(b)
            own.n = start + (B - half_way) * TB
            gather_stats(1, B)
            add_eps(slice(TB, B * TB), "eps_ready")
            three_parts(lambda i: b2_parts[:, i, :], b2[:, :], b2_rest[:, :], None)
            dve.memset(pv_bank[:, :], 0.0).then_inc(S["pv_clear"], 1)
            own.did(dve.memset(sel[:, :], 0.0))
            own.did(dve.memset(sel_m1[:, :], 0.0))
            gates_shift(0)
            gates_compare(0)
            gates_count(0)
            gates_score(0)
            for u in range(UNITS):
                max_unit(0, 0, u)
                if u % 4 == 3:
                    sum_near_qk(0, u // 4)
            near_logits(0)
            near_maxima(0)
            row_maximum(0, 0)
            shifts(slice(TB, B * TB), "pow_ready", "stats_ready")
            for u in range(UNITS):
                max_unit(0, 1, u)

            def selection():
                dve.wait_ge(S["qk_prod_ready"], TB * B)
                own.settle()
                own.did(dve.tensor_reduce(g_den, scores[:, :, :, :].rearrange("p n b e -> p n e b"), AX.X, ALU.add))
                own.settle()
                own.did(dve.tensor_scalar(g_den, g_den, GATE_EPS, None, ALU.add))
                own.settle()
                own.did(dve.reciprocal(g_den, g_den))
                own.settle()
                own.did(dve.tensor_scalar(g_den, g_den, CAPACITY, None, ALU.mult))
                own.settle()
                gd = g_den.rearrange("p n (o e) -> p n o e", o=1).to_broadcast([P, TB, B, NEXP])
                dve.tensor_tensor(route.rearrange("p n (b e) -> p n b e", e=NEXP), scores[:, :, :, :], gd, ALU.mult).then_inc(S["route_ready"], 1)
                yield
                dve.wait_ge(S["route_ps"], 1)
                dve.tensor_copy(route_rows, m1[0:SROW, :]).then_inc(S["route_kept"], 1)
                dve.wait_ge(S["route_kept"], 1)
                own.did(dve.memset(cand[:, :], 1 << (SEARCH_BITS - 1)))
                own.did(dve.memset(ones_t, 1.0))
                own.settle()
                value = cand[:, :].bitcast(fp32)
                for bit in range(SEARCH_BITS - 1, -1, -1):
                    own.did(dve.tensor_scalar(above, route_rows, value, None, ALU.is_ge, ALU.add, accum_out=small[:, 2:3]))
                    own.settle()
                    own.did(dve.tensor_scalar(drop[:, :], small[:, 2:3], float(KEEP), float(1 << bit), ALU.is_lt, ALU.mult))
                    own.settle()
                    own.did(dve.scalar_tensor_tensor(cand[:, :], cand[:, :], (1 << bit) >> 1, drop[:, :],
                                                     ALU.bitwise_xor, ALU.bitwise_xor))
                    own.settle()
                    yield
                own.did(dve.tensor_scalar(above, route_rows, value, None, ALU.is_gt, ALU.add, accum_out=small[:, 2:3]))
                own.did(dve.tensor_scalar(equal, route_rows, value, None, ALU.is_equal))
                own.settle()
                own.did(dve.tensor_tensor_scan(order, ones_t, equal, 0.0, ALU.mult, ALU.add))
                own.did(dve.tensor_scalar(small[:, 3:4], small[:, 2:3], -1.0, float(KEEP), ALU.mult, ALU.add))
                own.settle()
                own.did(dve.scalar_tensor_tensor(picked, order, small[:, 3:4], equal, ALU.is_le, ALU.mult))
                own.settle()
                own.did(dve.tensor_tensor(sel[0:SROW, :], picked, above, ALU.add))
                own.settle()
                own.did(dve.tensor_scalar(sel_m1[0:SROW, :], sel[0:SROW, :], -1.0, None, ALU.add))
                yield
                own.settle()
                rep = ident[:, 0:B * NEXP].rearrange("p (n o) -> p n o", o=1).to_broadcast([P, B * NEXP, HID])
                dve.tensor_scalar(expert_rows, rep, -NEG, None, ALU.mult).then_inc(S["sel_ready"], 1)
                yield
                dve.wait_ge(S["st_ps"], QUADS * UNITS * (B - 1) + 2 * UNITS)
                for i in range(PARTS):
                    part = b2_parts[:, i, :].rearrange("p (o e) -> p o e", o=1).to_broadcast([P, B, E])
                    mask = batchmask[:, :].rearrange("p (b o) -> p b o", o=1).to_broadcast([P, B, E])
                    dve.tensor_tensor(b2_rows[:, :, i, :], part, mask, ALU.mult).then_inc(S["b2_rows_ready"], 1)
                    yield

            NEAR_QK_AT = ((1, 8), (1, 12), (2, 3), (2, 6))
            GATE_STEPS_AT = ((0, 13), (0, 15), (1, 2), (1, 5))

            def body(b, last):
                first = isinstance(b, int) and b == 0
                select = selection() if last else None
                for q in range(QUADS):
                    if q < QUADS - 1:
                        row_maximum(b, q + 1)
                    elif not last:
                        row_maximum(b + 1, 0)
                    for u in range(UNITS):
                        if q < 2:
                            max_unit(b, q + 2, u)
                        elif not last:
                            max_unit(b + 1, q - 2, u)
                        if q == 2 and u == 0:
                            near_minus_max(b)
                        if u == 9:
                            if q > 0:
                                keep_o(b, q - 1)
                            elif not first:
                                keep_o(b - 1, QUADS - 1)
                        if q == 0 and u == 11 and not first:
                            finish_attention(b - 1)
                        if not last and (q, u) in GATE_STEPS_AT:
                            (gates_shift, gates_compare, gates_count, gates_score)[GATE_STEPS_AT.index((q, u))](b + 1)
                        if q == 1 and u == 14 and not first:
                            add_residual(b - 1)
                        if not last and (q, u) in NEAR_QK_AT:
                            sum_near_qk(b + 1, NEAR_QK_AT.index((q, u)))
                        if not last and (q, u) == (2, 8):
                            near_logits(b + 1)
                        if not last and (q, u) == (2, 11):
                            near_maxima(b + 1)
                        if q == 3 and u == 2:
                            near_sums(b)
                        if last and (q >= 2 or u % 2 == 1):
                            next(select, None)
                if last:
                    return select

            body(0, False)
            steps = QUADS * 3 + 1 + 3 + 9
            start = own.n
            with dve.Fori(1, B - 1) as b:
                own.n = (b - 1) * steps + start
                body(b, False)
            own.n = start + (B - 2) * steps
            select = body(B - 1, True)
            for _ in select:
                pass
            keep_o(B - 1, QUADS - 1)
            finish_attention(B - 1)

            def ffn(i):
                for half, s in enumerate(("out_even", "out_odd")):
                    wait(dve, S[s], 16 * i)
                    dve.wait_ge(S["y_ps"], 2 * i + half + 1)
                    xb = x_all[:, at(2 * i + half), :, :].rearrange("p o n e -> p (o n e)")
                    dve.tensor_tensor(ffn_out[:, half, :], (pv_bank, m0)[half][:, :], xb, ALU.add).then_inc(S["ffn_ready"], 1)

            ffn(0)
            add_residual(B - 1)
            with dve.Fori(1, B // 2) as i:
                ffn(i)


def kernel(**inputs):
    import concourse.bacc as bacc
    from concourse.bass_utils import run_bass_kernel_spmd as run

    a = {n.split("_", 1)[1]: np.asarray(v) for n, v in inputs.items()}
    a = {n.replace("attn_", "").replace("ffn_", ""): v for n, v in a.items()}
    f = np.float32
    arrays = {
        "x": a["hidden_states"],
        "brow": np.tile(np.concatenate([a["bq"], a["bk"], a["bv"], a["w_gate_b"], a["bo"]])[None], (PARTS, 1)),
    }
    ev = np.repeat(a["emb_rel_v"][0], H, axis=0)
    blocks = {
        "wcat": np.concatenate([a["Wq"], a["Wk"], a["Wv"], a["w_gate_w"]], axis=1),
        "bqk": np.stack([a["bq"], a["bk"]], axis=1),
        "wo": a["Wo"],
        "ek": np.tile(a["emb_rel_k"][0].T, (H, 1)),
        "ev0": ev[0:P],
        "ev1": np.concatenate([ev[P:JH], np.zeros((P - H, D), f)]),
        "w1": a["W1"].transpose(1, 0, 2).reshape(E, NEXP * HID),
        "b1": a["b1"].reshape(2, P).T,
        "w2": a["W2"].reshape(2, P, E).transpose(1, 0, 2).reshape(P, 2 * E),
        "b2": np.tile(a["b2"], (P // NEXP, 1)),
    }
    p = np.arange(P)
    w = np.arange(BAND)[None, :] - p[:, None]
    band = np.where((w >= 0) & (w <= 2 * WINDOW), NEG, 0.0).astype(f)
    j = np.arange(J)
    edge = np.zeros((P, 2, J, H), f)
    edge[:, 0][(p[:, None] + j[None] - WINDOW) < 0] = NEG
    edge[:, 1][(p[:, None] + j[None] - WINDOW) >= P] = NEG
    blocks |= {
        "ident": np.eye(P, dtype=f),
        "band": band,
        "edge": edge.reshape(P, 2 * JH),
        "headmask": (p[:, None] // D == np.arange(H)[None]).astype(f),
        "relmask": (p[:, None] % H == np.arange(H)[None]).astype(f),
        "earlier": np.tile((np.arange(NEXP)[None, :] < np.arange(NEXP)[:, None]).astype(f).reshape(1, -1), (P, 1)),
        "batchmask": (p[:, None] // NEXP == np.arange(B)[None]).astype(f),
    }
    x, brow = arrays["x"], arrays["brow"]
    arrays = {"x": x} | {n: np.concatenate([blocks[c] for c, _ in layout], axis=1)
                         for n, layout in (("first", FIRST_COLUMNS), ("rest", REST_COLUMNS))} | {"brow": brow}
    arrays = {f"in_{n}": np.ascontiguousarray(v) for n, v in arrays.items()}
    nc = bacc.Bacc("TRN2", target_bir_lowering=False, num_devices=1)
    args = [nc.dram_tensor(n, v.shape, mybir.dt.from_np(v.dtype), kind="ExternalInput").ap() for n, v in arrays.items()]
    out = nc.dram_tensor("out_0", (B, T, E), fp32, kind="ExternalOutput").ap()
    build_program(nc, *args, out)
    r = run(nc, [arrays], core_ids=[0])
    return r.results[0]["out_0"]
```

```python
import numpy as np
import concourse.bass as bass
from concourse import mybir
from contextlib import ExitStack

fp32 = mybir.dt.float32
bf16 = mybir.dt.bfloat16
int32 = mybir.dt.int32
ALU = mybir.AluOpType
ACT = mybir.ActivationFunctionType
AX = mybir.AxisListType

B, T, E, H = 8, 512, 128, 16
D = E // H
WINDOW = 4
J = 2 * WINDOW + 1
P = 128
TB = T // P
NEXP = 8
HID = 32
TOPK = 2
KEEP = T // 2
CAPACITY = float(B)
GATE_EPS = 1e-6
LN_EPS = 1e-5
SCALING = D ** -0.5
QUADS = 4
G = H // QUADS
UNITS = G * TB
NPROJ = 3 * E + NEXP
JH = J * H
PARTS = 3
QK_ROWS = PARTS * PARTS * D
C_ROW = QK_ROWS
BAND = P + 2 * WINDOW
NEG = -1e30
VW = 32
SEARCH_BITS = 31
TWO_ONES = 0x3F803F80
LATE = 5


FIRST_COLUMNS = (("ident", P), ("wcat", NPROJ), ("bqk", 2))
REST_COLUMNS = (("band", BAND), ("edge", 2 * JH), ("headmask", H), ("ek", J), ("ev", J * D),
                ("wo", E), ("earlier", NEXP * NEXP), ("batchmask", B), ("w1", NEXP * HID), ("b1", 2), ("w2", 2 * E), ("b2", E))


def build_program(nc, x_in, first_in, rest_in, brow_in, out):
    ctx = ExitStack()
    with ctx:
        def sb(name, shape, dt=fp32):
            return ctx.enter_context(nc.sbuf_tensor(name, shape, dt))

        def sem(name):
            return ctx.enter_context(nc.semaphore(name))

        def dram(name, shape, dt=fp32):
            return nc.dram_tensor(name, shape, dt, kind="Internal").ap()

        k_rows = dram("k_rows", [B, T + 2 * WINDOW, E])
        v_rows = dram("v_rows", [B, T + 2 * WINDOW, E])
        q_parts_dram = dram("q_parts_dram", [B, PARTS, D, H, T], bf16)
        xnT_dram = dram("xnT_dram", [B, P, T])
        k_parts_dram = dram("k_parts_dram", [B, PARTS, D, H, T], bf16)

        def columns(tensor, layout):
            views, c = [], 0
            for _, width in layout:
                views.append(tensor[:, c:c + width])
                c += width
            return views

        front_data = sb("front_data", [P, sum(w for _, w in FIRST_COLUMNS)])
        rest_data = sb("rest_data", [P, sum(w for _, w in REST_COLUMNS)])
        ident, wcat, bqk = columns(front_data, FIRST_COLUMNS)
        (band_f, edge, headmask, ek, ev, wo, earlier, batchmask, w1, b1, w2, b2) = columns(rest_data, REST_COLUMNS)
        edge = edge.rearrange("p (i m) -> p i m", i=2)
        w2 = w2.rearrange("p (i e) -> p i e", i=2)
        ident_b = sb("ident_b", [P, P], bf16)
        band_b = sb("band_b", [P, BAND], bf16)
        brow_parts = sb("brow_parts", [P, NPROJ + E], bf16)
        ones_rows = sb("ones_rows", [P, P], bf16)
        ek_block = sb("ek_block", [P, J, H])
        b2_rest = sb("b2_rest", [P, E])
        b2_parts = sb("b2_parts", [P, PARTS, E], bf16)
        zero_rows = sb("zero_rows", [2, G * T], bf16)
        one_col = sb("one_col", [P, 1])
        minus_half = sb("minus_half", [P, B * TB])

        x_all = sb("x_all", [P, B, TB, E])
        stats = sb("stats", [P, B * TB, 6])
        mean_var = sb("mean_var", [P, B * TB, 2])
        var_eps = sb("var_eps", [P, B * TB])
        rstd = sb("rstd", [P, B * TB])
        shift = sb("shift", [P, B * TB])
        scores = sb("scores", [P, TB, B, NEXP])
        g_exp = sb("g_exp", [P, TB, NEXP])
        g_max = sb("g_max", [P, TB])
        g_sum = sb("g_sum", [P, TB])
        g_count = sb("g_count", [P, TB, NEXP])
        pair_gt = sb("pair_gt", [P, TB, NEXP, NEXP], bf16)
        pair_eq = sb("pair_eq", [P, TB, NEXP, NEXP], bf16)

        xn = sb("xn", [P, TB, E])
        xnT = sb("xnT", [P, T])
        nat = sb("nat", [P, TB, NPROJ])
        qT = sb("qT", [P, T])
        kT = sb("kT", [P, T])
        rest1 = sb("rest1", [P, T])
        q_parts = sb("q_parts", [P, PARTS, T], bf16)
        k_parts = sb("k_parts", [P, PARTS, T], bf16)
        Q = sb("Q", [P, QUADS, G, T], bf16)
        K = sb("K", [P, QUADS, G, T], bf16)
        vaug = sb("vaug", [P, QUADS, TB, G, D + 1])

        k_near = sb("k_near", [P, TB, J * E])
        v_near = sb("v_near", [P, TB, J * E])
        qk_prod = sb("qk_prod", [P, 2, J * E])
        pv_prod = sb("pv_prod", [P, J, E])
        near_qk = sb("near_qk", [P, TB, JH])
        rel = sb("rel", [P, TB, JH])
        near = sb("near", [P, TB, J, H])
        near_p = sb("near_p", [P, TB, J, H])
        near_v = sb("near_v", [P, TB, E])
        near_den = sb("near_den", [P, TB, H])

        neg_max = sb("neg_max", [P, 2, G, TB])
        neg_near = sb("neg_near", [P, TB, H])
        neg_c = sb("neg_c", [P, G, TB])
        c_parts = sb("c_parts", [P, 2, G, TB], bf16)
        c_used = sb("c_used", [P, TB, H])
        cT = sb("cT", [2 * UNITS, P], bf16)
        PT = sb("PT", [P, TB, G, T])
        pvT = sb("pvT", [P, T])
        o_raw = sb("o_raw", [P, TB, H, D + 1])
        den = sb("den", [P, TB, H])
        rden = sb("rden", [P, TB, H])
        o_nat = sb("o_nat", [P, TB, E])
        oT = sb("oT", [P, T])

        s_bank = [ctx.enter_context(nc.psum_tensor(f"s_bank{i}", [P, T], fp32)) for i in range(2)]
        st_bank = [ctx.enter_context(nc.psum_tensor(f"st_bank{i}", [P, T], fp32)) for i in range(2)]
        pv_bank = ctx.enter_context(nc.psum_tensor("pv_bank", [P, T], fp32))
        m0 = ctx.enter_context(nc.psum_tensor("m0", [P, T], fp32))
        m1 = ctx.enter_context(nc.psum_tensor("m1", [P, T], fp32))
        m2 = ctx.enter_context(nc.psum_tensor("m2", [P, T], fp32))
        m0_b = m0[:, :].bitcast(bf16)

        PT_flat = PT[:, :, :, :].rearrange("p a g t -> p (a g t)")
        zero_pad = PT_flat[0:WINDOW, 4096:4096 + B * E].rearrange("p (b e) -> p b e", e=E)
        brow = PT_flat[0:PARTS, 6144:6144 + NPROJ + E]

        xnT_all = Q[:, :, :, :].rearrange("p q g t -> p (q g t)").bitcast(fp32).rearrange("p (b t) -> p b t", t=T)
        g_hid = PT[:, :, :, :].rearrange("p a g t -> p (a g t)")[:, 0:4 * T].rearrange("p (i c t) -> p i c t", i=2, c=2)
        ffn_out = PT[:, :, :, :].rearrange("p a g t -> p (a g t)")[:, 4 * T:6 * T].rearrange("p (i n) -> p i n", i=2)
        k_near_flat = k_near[:, :, :].rearrange("p a n -> p (a n)")
        expert_rows = k_near_flat[:, 0:B * NEXP * HID // 2].bitcast(bf16).rearrange("p (n h) -> p n h", h=HID)
        SROW = B * NEXP
        srow = k_near_flat[0:SROW, B * NEXP * HID // 2:]
        equal = srow[:, 0:T]
        ones_t = srow[:, T:2 * T]
        order = srow[:, 2 * T:3 * T]
        picked = srow[:, 3 * T:4 * T]
        b2_rows = k_near_flat[:, B * NEXP * HID // 2 + 4 * T:][:, 0:B * PARTS * E // 2].bitcast(bf16).rearrange(
            "p (b i e) -> p b i e", i=PARTS, e=E)
        g_den = sb("g_den", [P, TB, NEXP])
        route = sb("route", [P, TB, SROW])
        route_rows = sb("route_rows", [SROW, T])
        route_high = sb("route_high", [SROW, T], bf16)
        above = sb("above", [SROW, T], bf16)
        taken = sb("taken", [SROW, 1])
        room = sb("room", [SROW, 1])
        candidate = sb("candidate", [SROW, 1], int32)
        drop = sb("drop", [SROW, 1], int32)
        sel = sb("sel", [P, T], bf16)
        sel_m1 = sb("sel_m1", [P, T], bf16)

        names = ("x0_in x_rest_in first_in rest_in brow_in pads_written zero_pad_ready rows_set scaled masks_ready "
                 "block_ready setup_pool bias_ready "
                 "stats0_ready stats_ready eps0_ready eps_ready pow0_ready pow_ready "
                 "xn_ready xnT_ps xnT_ready xnT_saved xnT_back xnT_back_first pv_clear nat_ps nat_ready qkT_ps qkT_ready "
                 "split_ready parts_saved kv_saved "
                 "v_near_in qk_prod_ready near_qk_ready rel_ps rel_ready near_ready gates_ready vaug_ready "
                 "st_ps exp_ready s_ps max_ready pv_ps pvT_ready o_ps o_raw_ready c_ready cT_ps cT_ready "
                 "near_c_ready near_p_ready near_v_ready near_den_ready "
                 "o_ready oT_ps oT_ready wo_ps x_res_ready dve_step pool_step "
                 "g_shift_ready g_exp_ready route_ready route_ps route_kept sel_ready expert_rows_ready b2_parts_ready "
                 "b2_rows_ready h_ps g_ready y_ps ffn_ready out_even out_odd").split()
        S = {n: sem(n) for n in names}
        packed = [sem(f"packed{q}") for q in range(QUADS)]
        c_rows_in = [sem(f"c_rows_in{q}") for q in range(QUADS)]
        k_near_in = [sem(f"k_near_in{half}") for half in range(2)]
        PACK_DMAS = 2 + PARTS

        block = ctx.enter_context(nc.Block())

        def wait(eng, s, value):
            if isinstance(value, int) and value <= 0:
                return
            eng.wait_ge(s, value)

        class Steps:

            def __init__(self, eng, s):
                self.eng, self.s, self.n = eng, s, 0

            def did(self, ins):
                ins.then_inc(self.s, 1)
                self.n = self.n + 1

            def settle(self):
                self.eng.wait_ge(self.s, self.n)

        def at(b):
            return slice(b, b + 1) if isinstance(b, int) else bass.ds(b, 1)

        def span(start, size):
            return slice(start, start + size) if isinstance(start, int) else bass.ds(start, size)

        def max_bank(q, u):
            return (s_bank[0], s_bank[1], m1, m2)[u % 4] if q < 2 else s_bank[u % 2]

        def band_columns(blk):
            lo, hi = max(0, blk * P - WINDOW), min(T, (blk + 1) * P + WINDOW)
            m = lo - (blk * P - WINDOW)
            return slice(lo, hi), slice(m, m + hi - lo)

        @block.sync
        def _(sp):
            def load(dst, src, s):
                sp.dma_start(dst, src).then_inc(S[s], 16)

            xv = x_in.rearrange("b (n p) e -> b p n e", p=P)
            load(x_all[:, 0, :, :], xv[0], "x0_in")
            load(brow, brow_in, "brow_in")
            load(x_all[:, 1:B, :, :], x_in[1:B].rearrange("b (n p) e -> p b n e", p=P), "x_rest_in")
            sp.wait_ge(S["zero_pad_ready"], 1)
            for rows in (k_rows, v_rows):
                for edge_row in (0, T + WINDOW):
                    load(rows[:, edge_row:edge_row + WINDOW, :].rearrange("b w e -> w b e"), zero_pad, "pads_written")

            def line(b, per, off=0):
                return b[0] * per + (per * b[1] + off)

            def after(b, n=1):
                return (b[0], b[1] + n)

            def part(tensor, b, start=0, size=None):
                names = " ".join("abcdef"[:len(tensor.shape)])
                per = int(np.prod(tensor.shape[1:]))
                size = per if size is None else size
                flat = tensor.rearrange(f"{names} -> ({names})")
                at_ = line(b, per, start)
                return flat[at_:at_ + size] if isinstance(at_, int) else flat[bass.ds(at_, size)]

            def save_xnT(b):
                wait(sp, S["xnT_ready"], line(b, 1, 1))
                sp.dma_start(part(xnT_dram, b).rearrange("(p t) -> p t", t=T), xnT[:, :]).then_inc(S["xnT_saved"], 16)

            def save_kv(b):
                wait(sp, S["nat_ready"], line(b, TB, TB))
                for rows, c in ((k_rows, E), (v_rows, 2 * E)):
                    dst = part(rows, b, WINDOW * E, T * E).rearrange("(n p e) -> p n e", p=P, e=E)
                    sp.dma_start(dst, nat[:, :, c:c + E]).then_inc(S["kv_saved"], 16)

            def windows(rows, b, blocks=slice(0, TB)):
                v = part(rows, b, 0, T * E).rearrange("(n p e) -> p n e", p=P, e=E)[:, blocks, :]
                return bass.AP(tensor=v.tensor, offset=v.offset, ap=[list(v.ap[0]), list(v.ap[1]), [1, J * E]])

            def load_k_near(b):
                wait(sp, S["kv_saved"], line(b, 32, 32))
                for half in range(2):
                    load_k_near_half(b, half)

            def load_k_near_half(b, half):
                n = slice(half * TB // 2, (half + 1) * TB // 2)
                sp.dma_start(k_near[:, n, :], windows(k_rows, b, n)).then_inc(k_near_in[half], 16)

            def load_v_near(b):
                wait(sp, S["near_v_ready"], line(b, TB))
                sp.dma_start(v_near[:, :, :], windows(v_rows, b)).then_inc(S["v_near_in"], 16)

            def save_parts(b):
                for n, (dst, src) in enumerate(((q_parts_dram, q_parts), (k_parts_dram, k_parts))):
                    wait(sp, S["split_ready"], line(b, 2, n + 1))
                    for i in range(PARTS):
                        d = part(dst, b, i * E * T, E * T).rearrange("(d h t) -> h d t", h=H, t=T)
                        sp.dma_start(d, src[:, i, :]).then_inc(S["parts_saved"], 16)

            def pack(b, q, free):
                wait(sp, S["st_ps"], free)
                sp.dma_start(Q[C_ROW:C_ROW + 2, q, :, :].rearrange("p g t -> p (g t)"), zero_rows[:, :]).then_inc(packed[q], 16)
                wait(sp, S["parts_saved"], line(b, 16 * 2 * PARTS, 16 * 2 * PARTS))
                size, row = G * T, H * T
                src = part(q_parts_dram, b, q * size, size)
                src = bass.AP(tensor=src.tensor, offset=src.offset, ap=[[0, PARTS], [row, PARTS * D], [1, size]])
                dst = Q[0:QK_ROWS, q, :, :].rearrange("p g t -> p (g t)")
                sp.dma_start(dst, src).then_inc(packed[q], 16)
                for i in range(PARTS):
                    src = part(k_parts_dram, b, i * E * T + q * size, size)
                    src = bass.AP(tensor=src.tensor, offset=src.offset, ap=[[0, PARTS], [row, D], [1, size]])
                    dst = K[i * PARTS * D:(i + 1) * PARTS * D, q, :, :].rearrange("p g t -> p (g t)")
                    sp.dma_start(dst, src).then_inc(packed[q], 16)

            zero = (0, 0)
            save_kv(zero)
            wait(sp, S["pads_written"], 64)
            wait(sp, S["kv_saved"], 32)
            load_k_near_half(zero, 0)
            save_parts(zero)
            wait(sp, S["rows_set"], 3)
            pack(zero, 0, 0)
            load_k_near_half(zero, 1)
            for q in (1, 2):
                pack(zero, q, 0)
            save_xnT(zero)
            load_v_near(zero)

            def body(b, first, last):
                units = QUADS * UNITS
                nxt = after(b)
                if not first:
                    load_v_near(b)
                pack(b, 3, line(b, units))
                if not last:
                    save_xnT(nxt)
                    save_kv(nxt)
                    load_k_near(nxt)
                    save_parts(nxt)
                    for q in range(QUADS - 1):
                        pack(nxt, q, line(b, units, UNITS * (q + 1)))
                if last:
                    wait(sp, S["xnT_saved"], 16 * B)
                    for q in range(QUADS):
                        wait(sp, S["st_ps"], line(b, units, UNITS * (q + 1)))
                        sp.dma_start(xnT_all[:, 2 * q:2 * q + 2, :],
                                     xnT_dram[2 * q:2 * q + 2].rearrange("b p t -> p b t"))\
                            .then_inc(S["xnT_back"] if q else S["xnT_back_first"], 16)

            body((0, 0), True, False)
            with sp.Fori(0, B - 2) as i:
                body((i, 1), False, False)
            body((0, B - 1), False, True)

            ov = out.rearrange("b (n p) e -> b p n e", p=P)
            with sp.Fori(0, B // 2) as i:
                for half, s in enumerate(("out_even", "out_odd")):
                    wait(sp, S["ffn_ready"], 2 * i + half + 1)
                    dst = ov[at(2 * i + half), :, :, :].rearrange("o p n e -> p (o n) e")
                    sp.dma_start(dst, ffn_out[:, half, :].rearrange("p (n e) -> p n e", e=E)).then_inc(S[s], 16)
            wait(sp, S["out_even"], 16 * B // 2)
            wait(sp, S["out_odd"], 16 * B // 2)

        @block.tensor
        def _(pe):
            def transposes_xn(b):
                pe.wait_ge(S["xn_ready"], TB * (b + 1))
                for n in range(TB):
                    ins = pe.transpose(m1[:, n * P:(n + 1) * P], xn[:, n, :], ident[:, :])
                ins.then_inc(S["xnT_ps"], 1)

            def project(b, n):
                bank = (m1, m2)[n % 2]
                pe.wait_ge(S["xnT_ready"], b + 1)
                if n >= 2:
                    pe.wait_ge(S["nat_ready"], TB * b + n - 1)
                pe.matmul(bank[:, 0:NPROJ], xnT[:, n * P:(n + 1) * P], wcat[:, :], start=True, stop=False)
                pe.matmul(bank[:, 0:NPROJ], ones_rows[:, :], brow_parts[:, 0:NPROJ], start=False, stop=True)\
                    .then_inc(S["nat_ps"], 1)

            def project_T(b, n):
                pe.wait_ge(S["nat_ready"], TB * b + 3 + n)
                pe.matmul((m1, m2)[n][:, :], wcat[:, n * E:(n + 1) * E], xnT[:, :], start=True, stop=True)\
                    .then_inc(S["qkT_ps"], 1)

            def relative(b, n):
                bank = (m1, m2)[n % 2]
                if n < 2:
                    pe.wait_ge(S["qkT_ready"], 2 * b + n + 1)
                else:
                    pe.wait_ge(S["rel_ready"], TB * b + n - 1)
                at_edge = n in (0, TB - 1)
                ins = pe.matmul(bank[:, 0:JH], qT[:, n * P:(n + 1) * P], ek_block[:, :, :].rearrange("p j h -> p (j h)"),
                                start=True, stop=not at_edge)
                if at_edge:
                    ins = pe.matmul(bank[:, 0:JH], ident[:, :], edge[:, n // (TB - 1), :], start=False, stop=True)
                ins.then_inc(S["rel_ps"], 1)

            def s_unit(b, q, u):
                if u == 0:
                    pe.wait_ge(packed[q], 16 * PACK_DMAS * (b + 1))
                done = QUADS * UNITS * b + UNITS * q + u
                if q == 0 and u in (2, 3):
                    if isinstance(b, int) and b < 2:
                        pe.wait_ge(S["rel_ready"], TB * (b + 1))
                    elif u == 2:
                        pe.wait_ge(S["oT_ready"], b - 1)
                        if isinstance(b, int) and b == B - 1:
                            pe.wait_ge(S["route_kept"], 1)
                    else:
                        pe.wait_ge(S["x_res_ready"], b - 1)
                else:
                    four = (0, 1) < (q, u) < (2, 2)
                    wait(pe, S["max_ready"], done - 3 if four else done - 1)
                g, n = u // TB, u % TB
                bank = max_bank(q, u)
                pe.matmul(bank[:, :], Q[:, q, g, n * P:(n + 1) * P], K[:, q, g, :], start=True, stop=True)
                cols, mask = band_columns(n)
                pe.matmul(bank[:, cols], ident_b[:, :], band_b[:, mask], start=False, stop=True,
                          skip_group_check=True).then_inc(S["s_ps"], 1)

            def st_unit(b, q, u):
                if u == 0:
                    pe.wait_ge(c_rows_in[q], 16 * (b + 1))
                done = QUADS * UNITS * b + UNITS * q + u
                wait(pe, S["exp_ready"], done - 1)
                n, g = u // G, u % G
                bank = st_bank[u % 2]
                pe.matmul(bank[:, :], K[:, q, g, n * P:(n + 1) * P], Q[:, q, g, :], start=True, stop=True)
                cols, mask = band_columns(n)
                pe.matmul(bank[:, cols], ident_b[:, :], band_b[:, mask], start=False, stop=True,
                          skip_group_check=True).then_inc(S["st_ps"], 1)

            def pv(b, q, n):
                pe.wait_ge(S["exp_ready"], QUADS * UNITS * b + UNITS * q + G * (n + 1))
                if n == 0:
                    pe.wait_ge(S["vaug_ready"], QUADS * b + q + 1)
                    wait(pe, S["pvT_ready"], QUADS * b + q)
                    if isinstance(b, int) and b == 0 and q == 0:
                        pe.wait_ge(S["pv_clear"], 1)
                for g in range(G):
                    ins = pe.matmul(pv_bank[VW * g:VW * g + D + 1, :], vaug[:, q, n, g, :], PT[:, n, g, :],
                                    start=(n == 0), stop=(n == TB - 1))
                ins.then_inc(S["pv_ps"], 1)

            def transpose_o(b, q):
                pe.wait_ge(S["pvT_ready"], QUADS * b + q + 1)
                if isinstance(b, int) and QUADS * b + q + 3 > QUADS * B:
                    pe.wait_ge(S["o_raw_ready"], QUADS * b + q)
                else:
                    wait(pe, S["cT_ready"], QUADS * b + q + 3)
                for n in range(TB):
                    ins = pe.transpose(m0[:, n * P:(n + 1) * P], pvT[:, n * P:(n + 1) * P], ident[:, :])
                ins.then_inc(S["o_ps"], 1)

            def transpose_c(b, q):
                pe.wait_ge(S["c_ready"], QUADS * b + q + 1)
                wait(pe, S["o_raw_ready"], QUADS * b + q - 2)
                pe.transpose(m0_b[0:2 * UNITS, 0:P], c_parts[:, :, :, :].rearrange("p i g n -> p (i g n)"),
                             ident_b[:, :]).then_inc(S["cT_ps"], 1)

            def transpose_attn(b, bank_free):
                bank_free()
                pe.wait_ge(S["o_ready"], b + 1)
                for n in range(TB):
                    ins = pe.transpose(m1[:, n * P:(n + 1) * P], o_nat[:, n, :], ident[:, :])
                ins.then_inc(S["oT_ps"], 1)

            def project_out(b, bank_free):
                bank_free()
                pe.wait_ge(S["oT_ready"], b + 1)
                for n in range(TB):
                    cols = slice(n * P, (n + 1) * P)
                    pe.matmul(m2[:, cols], oT[:, cols], wo[:, :], start=True, stop=False)
                    ins = pe.matmul(m2[:, cols], ones_rows[:, :], brow_parts[:, NPROJ:NPROJ + E], start=False, stop=True)
                ins.then_inc(S["wo_ps"], 1)

            pe.wait_ge(S["first_in"], 16)
            transposes_xn(0)
            pe.wait_ge(S["scaled"], 2)
            pe.wait_ge(S["bias_ready"], 1)
            for n in range(TB):
                project(0, n)
            for n in range(2):
                project_T(0, n)
            pe.wait_ge(S["block_ready"], 1)
            for n in range(TB):
                relative(0, n)
            pe.wait_ge(S["masks_ready"], 2)
            for q in range(2):
                for u in range(UNITS):
                    s_unit(0, q, u)
                    if q == 1 and u == 1:
                        transpose_c(0, 0)

            def body(b, last):
                first = isinstance(b, int) and b == 0
                for q in range(QUADS):
                    for u in range(UNITS):
                        st_unit(b, q, u)
                        if u % G == 1:
                            if u >= G:
                                pv(b, q, u // G - 1)
                            elif q > 0:
                                pv(b, q - 1, TB - 1)
                            elif not first:
                                pv(b - 1, QUADS - 1, TB - 1)
                        if q < 2:
                            s_unit(b, q + 2, u)
                        elif not last:
                            s_unit(b + 1, q - 2, u)
                        if u == 8:
                            if q > 0:
                                transpose_o(b, q - 1)
                            elif not first:
                                transpose_o(b - 1, QUADS - 1)
                        if u == 4:
                            if q < QUADS - 1:
                                transpose_c(b, q + 1)
                            elif not last:
                                transpose_c(b + 1, 0)
                        if isinstance(b, int) and b == B - 2 and (q, u) == (1, 15):
                            pe.wait_ge(S["oT_ready"], b)
                            pe.wait_ge(S["route_ready"], 1)
                            for n in range(TB):
                                ins = pe.transpose(m1[0:B * NEXP, n * P:(n + 1) * P], route[:, n, :], ident[:, :])
                            ins.then_inc(S["route_ps"], 1)
                        if q == 0 and not last:
                            if u == 6:
                                transposes_xn(b + 1)
                            if 8 <= u < 12:
                                project(b + 1, u - 8)
                            if u in (12, 13):
                                project_T(b + 1, u - 12)
                        if q == 1:
                            if not last and u in (3, 4, 7, 8):
                                relative(b + 1, (3, 4, 7, 8).index(u))
                            if not first and u == 10:
                                transpose_attn(b - 1, (lambda: pe.wait_ge(S["route_kept"], 1)) if last else
                                               lambda: pe.wait_ge(S["rel_ready"], TB * (b + 1) + 3))
                            if not first and u == 13:
                                project_out(b - 1, (lambda: pe.wait_ge(S["x_res_ready"], b - 1)) if last else
                                            (lambda: pe.wait_ge(S["rel_ready"], TB * (b + 1) + 4)))
            body(0, False)
            with pe.Fori(1, B - 2) as b:
                body(b, False)
            body(B - 2, False)
            body(B - 1, True)
            pv(B - 1, QUADS - 1, TB - 1)
            h_bank = (st_bank[0], st_bank[1], s_bank[0], s_bank[1])
            y_bank = (pv_bank, m0)

            def ffn_hidden(i):
                for half in range(2):
                    for c in range(2):
                        bank = h_bank[2 * half + c]
                        pe.matmul(bank[:, :], w1[:, c * P:(c + 1) * P],
                                  xnT_all[:, at(2 * i + half), :].rearrange("p o t -> p (o t)"), start=True, stop=False)
                        rows = expert_rows[:, span((2 * i + half) * NEXP + 4 * c, 4), :].rearrange("p e h -> p (e h)")
                        pe.matmul(bank[:, :], rows, sel_m1[:, :], start=False, stop=True).then_inc(S["h_ps"], 1)

            def ffn_sums(i):
                for half in range(2):
                    pe.wait_ge(S["g_ready"], 4 * i + 2 * half + 2)
                    if isinstance(i, int) and half == 0:
                        pe.wait_ge(S["b2_rows_ready"], PARTS)
                    wait(pe, S["ffn_ready"], 2 * i + half - 1)
                    for n in range(TB):
                        cols = slice(n * P, (n + 1) * P)
                        for c in range(2):
                            pe.matmul(y_bank[half][:, cols], g_hid[:, half, c, cols], w2[:, c, :],
                                      start=(c == 0), stop=False)
                        for k in range(PARTS):
                            ins = pe.matmul(y_bank[half][:, cols], sel[:, cols],
                                            b2_rows[:, at(2 * i + half), k, :].rearrange("p o e -> p (o e)"),
                                            start=False, stop=(k == PARTS - 1))
                    ins.then_inc(S["y_ps"], 1)

            pe.wait_ge(S["xnT_back_first"], 16)
            pe.wait_ge(S["sel_ready"], 1)
            ffn_hidden(0)
            pe.wait_ge(S["pvT_ready"], QUADS * B)
            pe.wait_ge(S["o_raw_ready"], QUADS * B - 1)
            for n in range(TB):
                ins = pe.transpose(m0[:, n * P:(n + 1) * P], pvT[:, n * P:(n + 1) * P], ident[:, :])
            ins.then_inc(S["o_ps"], 1)
            pe.wait_ge(S["o_raw_ready"], QUADS * B)
            ffn_sums(0)
            transpose_attn(B - 1, lambda: pe.wait_ge(S["oT_ready"], B - 1))
            project_out(B - 1, lambda: pe.wait_ge(S["x_res_ready"], B - 1))
            pe.wait_ge(S["xnT_back"], 16 * (QUADS - 1))
            with pe.Fori(1, B // 2) as i:
                ffn_hidden(i)
                ffn_sums(i)

        @block.scalar
        def _(act):
            def normalize(b, blocks):
                for n in blocks:
                    if n == 0:
                        wait(act, S["xnT_ps"], b)
                    c = b * TB + n
                    col = slice(c, c + 1) if isinstance(c, int) else bass.ds(c, 1)
                    act.activation(xn[:, n, :], x_all[:, at(b), n, :].rearrange("p o e -> p (o e)"), ACT.Identity,
                                   bias=shift[:, col], scale=rstd[:, col]).then_inc(S["xn_ready"], 1)

            def copy_xnT(b):
                act.wait_ge(S["xnT_ps"], b + 1)
                wait(act, S["xnT_saved"], 16 * b)
                act.activation(xnT[:, :], m1[:, :], ACT.Copy).then_inc(S["xnT_ready"], 1)

            def copy_nat(b, n):
                act.wait_ge(S["nat_ps"], TB * b + n + 1)
                if n == 0:
                    wait(act, S["kv_saved"], 32 * b)
                    wait(act, S["qk_prod_ready"], TB * b)
                    wait(act, S["vaug_ready"], QUADS * b)
                    wait(act, S["gates_ready"], b)
                act.activation(nat[:, n, :], (m1, m2)[n % 2][:, 0:NPROJ], ACT.Copy).then_inc(S["nat_ready"], 1)

            def copy_qkT(b, n):
                act.wait_ge(S["qkT_ps"], 2 * b + n + 1)
                wait(act, S["split_ready"], 2 * b - 1 + n)
                wait(act, S["parts_saved"], 16 * 2 * PARTS * b)
                act.activation((q_parts, k_parts)[n][:, 0, :], (m1, m2)[n][:, :], ACT.Identity, bias=bqk[:, n:n + 1])

            def keep_qkT(b, n):
                act.activation((qT, kT)[n][:, :], (m1, m2)[n][:, :], ACT.Identity, bias=bqk[:, n:n + 1])\
                    .then_inc(S["qkT_ready"], 1)

            def copy_rel(b, n):
                act.wait_ge(S["rel_ps"], TB * b + n + 1)
                if n == 0:
                    wait(act, S["near_ready"], b)
                act.activation(rel[:, n, :], (m1, m2)[n % 2][:, 0:JH], ACT.Copy).then_inc(S["rel_ready"], 1)

            def exp_unit(b, q, u):
                done = QUADS * UNITS * b + UNITS * q + u
                act.wait_ge(S["st_ps"], done + 1)
                n, g = u // G, u % G
                if g == 0:
                    wait(act, S["pv_ps"], QUADS * TB * b + TB * q + n - TB + 1)
                act.activation(PT[:, n, g, :], st_bank[u % 2][:, :], ACT.Exp).then_inc(S["exp_ready"], 1)

            def copy_pv(b, q):
                act.wait_ge(S["pv_ps"], QUADS * TB * b + TB * (q + 1))
                wait(act, S["o_ps"], QUADS * b + q)
                act.activation(pvT[:, :], pv_bank[:, :], ACT.Copy).then_inc(S["pvT_ready"], 1)

            def copy_c(b, q):
                act.wait_ge(S["cT_ps"], QUADS * b + q + 1)
                if q > 0:
                    act.wait_ge(c_rows_in[q - 1], 16 * (b + 1))
                elif not (isinstance(b, int) and b == 0):
                    act.wait_ge(c_rows_in[QUADS - 1], 16 * b)
                act.activation(cT[:, :], m0_b[0:2 * UNITS, 0:P], ACT.Copy).then_inc(S["cT_ready"], 1)
                act.wait_ge(S["cT_ready"], QUADS * b + q + 1)
                act.dma_start(Q[C_ROW:C_ROW + 2, q, :, :], cT[:, :]).then_inc(c_rows_in[q], 16)

            def gates_exp(b):
                act.wait_ge(S["g_shift_ready"], b + 1)
                act.activation(g_exp[:, :, :], g_exp[:, :, :], ACT.Exp).then_inc(S["g_exp_ready"], 1)

            def near_exp(b):
                act.wait_ge(S["near_c_ready"], b + 1)
                wait(act, S["near_v_ready"], TB * b)
                wait(act, S["near_den_ready"], b)
                act.activation(near_p[:, :, :, :].rearrange("p n j h -> p (n j h)"),
                               near_p[:, :, :, :].rearrange("p n j h -> p (n j h)"), ACT.Exp).then_inc(S["near_p_ready"], 1)

            def copy_oT(b):
                act.wait_ge(S["oT_ps"], b + 1)
                wait(act, S["wo_ps"], b)
                act.activation(oT[:, :], m1[:, :], ACT.Copy).then_inc(S["oT_ready"], 1)

            act.dma_start(front_data[:, :], first_in).then_inc(S["first_in"], 16)
            act.dma_start(rest_data[:, :], rest_in).then_inc(S["rest_in"], 16)
            act.wait_ge(S["stats0_ready"], 1)
            normalize(0, range(TB))
            copy_xnT(0)
            for n in range(TB):
                copy_nat(0, n)
            act.wait_ge(S["scaled"], 2)
            for n in range(2):
                copy_qkT(0, n)
                keep_qkT(0, n)
            for n in range(TB):
                copy_rel(0, n)
            copy_c(0, 0)
            gates_exp(0)
            act.wait_ge(S["stats_ready"], 1)

            def body(b, last):
                first = isinstance(b, int) and b == 0
                for q in range(QUADS):
                    for u in range(UNITS):
                        exp_unit(b, q, u)
                        if u == 3:
                            if q > 0:
                                copy_pv(b, q - 1)
                            elif not first:
                                copy_pv(b - 1, QUADS - 1)
                        if u == 4:
                            if q < QUADS - 1:
                                copy_c(b, q + 1)
                            elif not last:
                                copy_c(b + 1, 0)
                        if q == 0 and not last:
                            if u < TB:
                                normalize(b + 1, (u,))
                            if u == 6:
                                copy_xnT(b + 1)
                            if 8 <= u < 12:
                                copy_nat(b + 1, u - 8)
                            if u in (12, 14):
                                copy_qkT(b + 1, (u - 12) // 2)
                            if u in (13, 15):
                                keep_qkT(b + 1, (u - 13) // 2)
                        if q == 1:
                            if not last and u in (3, 4, 7, 8):
                                copy_rel(b + 1, (3, 4, 7, 8).index(u))
                            if not first and u == 10:
                                copy_oT(b - 1)
                        if q == 2 and u == 6:
                            near_exp(b)
                        if q == 1 and u == 1 and not last:
                            gates_exp(b + 1)

            body(0, False)
            act.wait_ge(S["stats_ready"], 2)
            with act.Fori(1, B - 1) as b:
                body(b, False)
            body(B - 1, True)
            copy_pv(B - 1, QUADS - 1)

            def ffn(i):
                for half in range(2):
                    for c in range(2):
                        act.wait_ge(S["h_ps"], 4 * i + 2 * half + c + 1)
                        wait(act, S["y_ps"], 2 * i + half - 1)
                        bank = (st_bank[0], st_bank[1], s_bank[0], s_bank[1])[2 * half + c]
                        act.activation(g_hid[:, half, c, :], bank[:, :], ACT.Gelu, bias=b1[:, c:c + 1])\
                            .then_inc(S["g_ready"], 1)

            ffn(0)
            copy_oT(B - 1)
            with act.Fori(1, B // 2) as i:
                ffn(i)

        @block.gpsimd
        def _(pool):
            own = Steps(pool, S["pool_step"])

            def split(b, n):
                src, parts = ((qT, q_parts), (kT, k_parts))[n]
                pool.wait_ge(S["qkT_ready"], 2 * b + n + 1)
                wait(pool, S["split_ready"], 2 * b + n)
                own.did(pool.tensor_tensor(rest1[:, :], src[:, :], parts[:, 0, :], ALU.subtract))
                own.did(pool.tensor_tensor(parts[:, 1, :], src[:, :], parts[:, 0, :], ALU.subtract))
                own.settle()
                pool.tensor_tensor(parts[:, 2, :], rest1[:, :], parts[:, 1, :], ALU.subtract).then_inc(S["split_ready"], 1)

            def near_products(b, n):
                pool.wait_ge(k_near_in[n // 2], 16 * (b + 1))
                pool.wait_ge(S["nat_ready"], TB * b + n + 1)
                wait(pool, S["near_qk_ready"], TB * b + n - 1)
                q_rep = nat[:, n, 0:E].rearrange("p (o e) -> p o e", o=1).to_broadcast([P, J, E])
                own.did(pool.tensor_tensor(qk_prod[:, n % 2, :].rearrange("p (j e) -> p j e", j=J),
                                           k_near[:, n, :].rearrange("p (j e) -> p j e", j=J), q_rep, ALU.mult))
                own.settle()
                halves = qk_prod[:, n % 2, :].rearrange("p (m i d) -> p m i d", i=2, d=D // 2)
                pool.tensor_tensor(halves[:, :, 0, :], halves[:, :, 0, :], halves[:, :, 1, :], ALU.add)\
                    .then_inc(S["qk_prod_ready"], 1)

            def fill_vaug(b, q):
                pool.wait_ge(S["nat_ready"], TB * (b + 1))
                wait(pool, S["pv_ps"], QUADS * TB * (b - 1) + TB * (q + 1))
                c = 2 * E + q * G * D
                one = one_col[:, :].rearrange("p (n o) -> p n o", n=1).to_broadcast([P, G, D])
                for n in range(TB):
                    ins = pool.tensor_tensor(vaug[:, q, n, :, 0:D], nat[:, n, c:c + G * D].rearrange("p (g d) -> p g d", d=D),
                                             one, ALU.mult)
                ins.then_inc(S["vaug_ready"], 1)

            def near_values(b, n):
                pool.wait_ge(S["near_p_ready"], b + 1)
                own.settle()
                if n == 0:
                    wait(pool, S["o_ready"], b)
                wait(pool, S["near_v_ready"], TB * b + n)
                p_rep = near_p[:, n, :, :].rearrange("p j (h o) -> p (j h) o", o=1).to_broadcast([P, JH, D])
                own.did(pool.tensor_tensor(pv_prod[:, :, :].rearrange("p j (h d) -> p (j h) d", d=D),
                                           v_near[:, n, :].rearrange("p (m d) -> p m d", d=D), p_rep, ALU.mult))
                own.settle()
                for half in (4, 2, 1):
                    own.did(pool.tensor_tensor(pv_prod[:, 0:half, :], pv_prod[:, 0:half, :], pv_prod[:, half:2 * half, :], ALU.add))
                    own.settle()
                pool.tensor_tensor(near_v[:, n, :], pv_prod[:, 0, :], pv_prod[:, J - 1, :], ALU.add).then_inc(S["near_v_ready"], 1)

            def add_emb_v(b):
                pool.wait_ge(S["rest_in"], 16)
                pool.wait_ge(S["v_near_in"], 16 * (b + 1))
                for n in range(TB):
                    v4 = v_near[:, n, :].rearrange("p (j h d) -> p j h d", j=J, h=H)
                    e4 = ev[:, :].rearrange("p (j o d) -> p j o d", j=J, o=1).to_broadcast([P, J, H, D])
                    own.did(pool.tensor_tensor(v4, v4, e4, ALU.add))

            pool.memset(minus_half[:, :], -0.5).then_inc(S["setup_pool"], 1)
            pool.memset(zero_pad, 0.0).then_inc(S["zero_pad_ready"], 1)
            pool.wait_ge(S["setup_pool"], 1)
            pool.wait_ge(S["eps0_ready"], 1)
            pool.tensor_tensor(rstd[:, 0:TB], var_eps[:, 0:TB], minus_half[:, 0:TB], ALU.pow).then_inc(S["pow0_ready"], 1)
            pool.memset(zero_rows[:, :], 0.0).then_inc(S["rows_set"], 1)
            pool.memset(Q[:, :, :, :].rearrange("p q g t -> p (q g t)").bitcast(int32), 0).then_inc(S["rows_set"], 1)
            pool.memset(K[:, :, :, :].rearrange("p q g t -> p (q g t)").bitcast(int32), TWO_ONES).then_inc(S["rows_set"], 1)
            own.did(pool.memset(one_col[:, :], 1.0))
            own.did(pool.memset(vaug[:, :, :, :, :].rearrange("p q n g c -> p (q n g c)"), 0.0))
            own.settle()
            own.did(pool.memset(vaug[:, :, :, :, D:D + 1].rearrange("p q n g o -> p (q n g) o"), 1.0))
            own.settle()

            def inverse_deviations(first_batch, end, count):
                pool.wait_ge(S["eps_ready"], count)
                c = slice(first_batch * TB, end * TB)
                pool.tensor_tensor(rstd[:, c], var_eps[:, c], minus_half[:, c], ALU.pow).then_inc(S["pow_ready"], 1)

            inverse_deviations(1, LATE, 1)
            for n in range(TB):
                near_products(0, n)
            for q in range(QUADS):
                fill_vaug(0, q)

            def body(b, last):
                first = isinstance(b, int) and b == 0
                if not first:
                    fill_vaug(b, QUADS - 1)
                add_emb_v(b)
                if not last:
                    for n in range(2):
                        split(b + 1, n)
                    for n in range(TB):
                        near_products(b + 1, n)
                    if first:
                        inverse_deviations(LATE, B, 2)
                    for q in range(2):
                        fill_vaug(b + 1, q)
                if last:
                    own.settle()
                    rep = ident[:, 0:B * NEXP].rearrange("p (n o) -> p n o", o=1).to_broadcast([P, B * NEXP, HID])
                    pool.tensor_scalar(expert_rows, rep, -NEG, 0.0, ALU.mult, ALU.add).then_inc(S["expert_rows_ready"], 1)
                    pool.memset(ones_t, 1.0).then_inc(S["expert_rows_ready"], 1)
                    pool.wait_ge(S["b2_parts_ready"], 1)
                    for i in range(PARTS):
                        part = b2_parts[:, i, :].rearrange("p (o e) -> p o e", o=1).to_broadcast([P, B, E])
                        mask = batchmask[:, :].rearrange("p (b o) -> p b o", o=1).to_broadcast([P, B, E])
                        pool.tensor_tensor(b2_rows[:, :, i, :], part, mask, ALU.mult).then_inc(S["b2_rows_ready"], 1)
                for n in range(TB):
                    near_values(b, n)
                if not last:
                    fill_vaug(b + 1, 2)

            body(0, False)
            steps = TB + 2 * 2 + TB * (4 + 1)
            start = own.n
            with pool.Fori(1, B - 1) as b:
                own.n = (b - 1) * steps + start
                body(b, False)
            own.n = start + (B - 2) * steps
            body(B - 1, True)

        @block.vector
        def _(dve):
            own = Steps(dve, S["dve_step"])

            def three_parts(dst, src, rest, ready=None):
                own.did(dve.tensor_copy(dst(0), src))
                own.settle()
                own.did(dve.tensor_tensor(rest, src, dst(0), ALU.subtract))
                own.settle()
                own.did(dve.tensor_copy(dst(1), rest))
                own.settle()
                ins = dve.tensor_tensor(dst(2), rest, dst(1), ALU.subtract)
                if ready is not None:
                    ins.then_inc(ready, 1)
                else:
                    own.did(ins)
                    own.settle()

            def sum_near_qk(b, n):
                dve.wait_ge(S["qk_prod_ready"], TB * b + n + 1)
                if n == 0:
                    wait(dve, S["near_ready"], b)
                dve.tensor_reduce(near_qk[:, n, :], qk_prod[:, n % 2, :].rearrange("p (m d) -> p m d", d=D)[:, :, 0:D // 2],
                                  AX.X, ALU.add)\
                    .then_inc(S["near_qk_ready"], 1)

            def near_logits(b):
                own.settle()
                dve.wait_ge(S["near_qk_ready"], TB * (b + 1))
                dve.wait_ge(S["rel_ready"], TB * (b + 1))
                wait(dve, S["near_c_ready"], b)
                dve.tensor_tensor(near[:, :, :, :].rearrange("p n j h -> p n (j h)"), near_qk[:, :, :], rel[:, :, :], ALU.add)\
                    .then_inc(S["near_ready"], 1)

            def near_maxima(b):
                dve.wait_ge(S["near_ready"], b + 1)
                own.did(dve.tensor_reduce(neg_near[:, :, :], near[:, :, :, :].rearrange("p n j h -> p n h j"), AX.X, ALU.max,
                                          negate=True))

            def max_unit(b, q, u):
                dve.wait_ge(S["s_ps"], QUADS * UNITS * b + UNITS * q + u + 1)
                dve.tensor_reduce(neg_max[:, q % 2, u // TB, u % TB:u % TB + 1], max_bank(q, u)[:, :], AX.X, ALU.max, negate=True)\
                    .then_inc(S["max_ready"], 1)

            def row_maximum(b, q, step):
                hs = slice(q * G, q * G + G)
                own.settle()
                if step == 0:
                    dve.wait_ge(S["max_ready"], QUADS * UNITS * b + UNITS * (q + 1))
                    own.did(dve.tensor_tensor(neg_c[:, :, :], neg_max[:, q % 2, :, :], neg_near[:, :, hs].rearrange("p n g -> p g n"),
                                              ALU.min))
                elif step == 1:
                    wait(dve, S["cT_ps"], QUADS * b + q)
                    own.did(dve.tensor_copy(c_parts[:, 0, :, :], neg_c[:, :, :]))
                elif step == 2:
                    dve.tensor_tensor(c_parts[:, 1, :, :], neg_c[:, :, :], c_parts[:, 0, :, :], ALU.subtract)\
                        .then_inc(S["c_ready"], 1)
                else:
                    dve.wait_ge(S["c_ready"], QUADS * b + q + 1)
                    own.did(dve.tensor_tensor(c_used[:, :, hs], c_parts[:, 0, :, :].rearrange("p g n -> p n g"),
                                              c_parts[:, 1, :, :].rearrange("p g n -> p n g"), ALU.add))

            def near_minus_max(b):
                own.settle()
                c_rep = c_used[:, :, :].rearrange("p n (o h) -> p n o h", o=1).to_broadcast([P, TB, J, H])
                wait(dve, S["near_p_ready"], b)
                dve.tensor_tensor(near_p[:, :, :, :], near[:, :, :, :], c_rep, ALU.add).then_inc(S["near_c_ready"], 1)

            def near_sums(b):
                dve.wait_ge(S["near_p_ready"], b + 1)
                dve.tensor_reduce(near_den[:, :, :], near_p[:, :, :, :].rearrange("p n j h -> p n h j"), AX.X, ALU.add)\
                    .then_inc(S["near_den_ready"], 1)

            def gates_shift(b):
                dve.wait_ge(S["nat_ready"], TB * (b + 1))
                gl = nat[:, :, 3 * E:NPROJ]
                own.did(dve.tensor_reduce(g_max[:, :], gl, AX.X, ALU.max))
                own.settle()
                gm = g_max[:, :].rearrange("p (n o) -> p n o", o=1).to_broadcast([P, TB, NEXP])
                dve.tensor_tensor(g_exp[:, :, :], gl, gm, ALU.subtract).then_inc(S["g_shift_ready"], 1)

            def gate_pairs(b):
                other = nat[:, :, 3 * E:NPROJ].rearrange("p n (o f) -> p n o f", o=1).to_broadcast([P, TB, NEXP, NEXP])
                mine = nat[:, :, 3 * E:NPROJ].rearrange("p n (e o) -> p n e o", o=1).to_broadcast([P, TB, NEXP, NEXP])
                return other, mine

            def gates_equal(b):
                own.did(dve.tensor_tensor(pair_eq[:, :, :, :], *gate_pairs(b), ALU.is_equal))

            def gates_above(b):
                dve.tensor_tensor(pair_gt[:, :, :, :], *gate_pairs(b), ALU.is_gt).then_inc(S["gates_ready"], 1)

            def gates_earlier(b):
                own.settle()
                tri = earlier[:, :].rearrange("p (o m) -> p o m", o=1).to_broadcast([P, TB, NEXP * NEXP])
                flat_eq = pair_eq[:, :, :, :].rearrange("p n e f -> p n (e f)")
                own.did(dve.tensor_tensor(flat_eq, flat_eq, tri, ALU.mult))

            def gates_before(b):
                own.settle()
                dve.wait_ge(S["gates_ready"], b + 1)
                own.did(dve.tensor_tensor(pair_gt[:, :, :, :], pair_gt[:, :, :, :], pair_eq[:, :, :, :], ALU.add))

            def gates_count(b):
                own.settle()
                own.did(dve.tensor_reduce(g_count[:, :, :], pair_gt[:, :, :, :], AX.X, ALU.add))

            def gates_sum(b):
                dve.wait_ge(S["g_exp_ready"], b + 1)
                own.did(dve.tensor_reduce(g_sum[:, :], g_exp[:, :, :], AX.X, ALU.add))
                own.settle()
                own.did(dve.reciprocal(g_sum[:, :], g_sum[:, :]))

            def gates_score(b):
                own.settle()
                gr = g_sum[:, :].rearrange("p (n o) -> p n o", o=1).to_broadcast([P, TB, NEXP])
                own.did(dve.tensor_tensor(g_exp[:, :, :], g_exp[:, :, :], gr, ALU.mult))
                own.settle()
                own.did(dve.scalar_tensor_tensor(scores[:, :, at(b), :].rearrange("p n o e -> p n (o e)"), g_count[:, :, :],
                                                 float(TOPK), g_exp[:, :, :], ALU.is_lt, ALU.mult))

            def keep_o(b, q):
                dve.wait_ge(S["o_ps"], QUADS * b + q + 1)
                src = m0[:, :].rearrange("p (n g c) -> p n g c", n=TB, c=VW)
                dve.tensor_copy(o_raw[:, :, q * G:(q + 1) * G, :], src[:, :, :, 0:D + 1]).then_inc(S["o_raw_ready"], 1)

            def finish_attention(b, step):
                own.settle()
                if step == 0:
                    dve.wait_ge(S["o_raw_ready"], QUADS * (b + 1))
                    dve.wait_ge(S["near_den_ready"], b + 1)
                    own.did(dve.tensor_tensor(den[:, :, :], o_raw[:, :, :, D], near_den[:, :, :], ALU.add))
                elif step == 1:
                    own.did(dve.reciprocal(rden[:, :, :], den[:, :, :]))
                    dve.wait_ge(S["near_v_ready"], TB * (b + 1))
                    own.did(dve.tensor_tensor(near_v[:, :, :].rearrange("p n (h d) -> p (n h) d", d=D),
                                              o_raw[:, :, :, 0:D].rearrange("p n h d -> p (n h) d"),
                                              near_v[:, :, :].rearrange("p n (h d) -> p (n h) d", d=D), ALU.add))
                else:
                    r_rep = rden[:, :, :].rearrange("p n (h o) -> p (n h) o", o=1).to_broadcast([P, TB * H, D])
                    wait(dve, S["oT_ps"], b)
                    dve.tensor_tensor(o_nat[:, :, :].rearrange("p n (h d) -> p (n h) d", d=D),
                                      near_v[:, :, :].rearrange("p n (h d) -> p (n h) d", d=D), r_rep, ALU.mult)\
                        .then_inc(S["o_ready"], 1)

            def add_residual(b):
                dve.wait_ge(S["wo_ps"], b + 1)
                xb = x_all[:, at(b), :, :].rearrange("p o n e -> p (o n e)")
                dve.tensor_tensor(xb, m2[:, :], xb, ALU.add).then_inc(S["x_res_ready"], 1)

            def block_stats(c):
                own.did(dve.bn_stats(stats[:, c, :], x_all[:, c // TB, c % TB, :]))

            def batch_stats(b):
                if isinstance(b, int):
                    for n in range(TB):
                        block_stats(b * TB + n)
                else:
                    for n in range(TB):
                        own.did(dve.bn_stats(stats[:, bass.ds(b * TB + n, 1), :].rearrange("p o s -> p (o s)"),
                                             x_all[:, at(b), n, :].rearrange("p o e -> p (o e)")))

            def gather_stats(first, end):
                own.settle()
                for c in range(first * TB, end * TB):
                    own.did(dve.bn_aggr(mean_var[:, c, :], stats[:, c, :]))

            def add_eps(cols, s):
                own.settle()
                dve.tensor_scalar(var_eps[:, cols], mean_var[:, cols, 1], LN_EPS, None, ALU.add).then_inc(S[s], 1)

            def shifts(cols, pow_ready, ready, count=1):
                dve.wait_ge(S[pow_ready], count)
                dve.scalar_tensor_tensor(shift[:, cols], mean_var[:, cols, 0], -1.0, rstd[:, cols], ALU.mult, ALU.mult)\
                    .then_inc(S[ready], 1)

            dve.wait_ge(S["x0_in"], 16)
            batch_stats(0)
            gather_stats(0, 1)
            add_eps(slice(0, TB), "eps0_ready")
            dve.memset(brow_parts[:, :], 0.0).then_inc(S["dve_step"], 1)
            dve.memset(ones_rows[:, :], 1.0).then_inc(S["dve_step"], 1)
            own.n += 2
            dve.wait_ge(S["first_in"], 16)
            dve.tensor_scalar(wcat[:, 0:E], wcat[:, 0:E], SCALING, None, ALU.mult).then_inc(S["scaled"], 1)
            dve.tensor_scalar(bqk[:, 0:1], bqk[:, 0:1], SCALING, None, ALU.mult).then_inc(S["scaled"], 1)
            shifts(slice(0, TB), "pow0_ready", "stats0_ready")
            dve.wait_ge(S["brow_in"], 16)
            own.did(dve.tensor_scalar(brow[:, 0:E], brow[:, 0:E], SCALING, None, ALU.mult))
            own.settle()
            br = k_near_flat[0:PARTS, 1024:1024 + NPROJ + E]
            bparts = qk_prod[0:PARTS, :, :].rearrange("p a n -> p (a n)")[:, 0:3 * (NPROJ + E) // 2 + 2].bitcast(bf16)
            NB = NPROJ + E
            three_parts(lambda i: bparts[:, i * NB:(i + 1) * NB], brow, br)
            own.did(dve.tensor_scalar(brow_parts[0:PARTS, :], bparts[:, 0:NB], ident[0:PARTS, 0:1], None, ALU.mult))
            for i in (1, 2):
                own.settle()
                ins = dve.scalar_tensor_tensor(brow_parts[0:PARTS, :], bparts[:, i * NB:(i + 1) * NB], ident[0:PARTS, i:i + 1],
                                               brow_parts[0:PARTS, :], ALU.mult, ALU.add)
                if i == 1:
                    own.did(ins)
            ins.then_inc(S["bias_ready"], 1)
            dve.tensor_copy(ident_b[:, :], ident[:, :]).then_inc(S["masks_ready"], 1)
            dve.wait_ge(S["rest_in"], 16)
            dve.tensor_copy(band_b[:, :], band_f[:, :]).then_inc(S["masks_ready"], 1)
            ek_rep = ek[:, :].rearrange("p (j o) -> p j o", o=1).to_broadcast([P, J, H])
            hm_rep = headmask[:, :].rearrange("p (o h) -> p o h", o=1).to_broadcast([P, J, H])
            dve.tensor_tensor(ek_block[:, :, :], ek_rep, hm_rep, ALU.mult).then_inc(S["block_ready"], 1)

            dve.wait_ge(S["x_rest_in"], 16)
            start = own.n
            with dve.Fori(1, LATE) as b:
                own.n = (b - 1) * TB + start
                batch_stats(b)
            own.n = start + (LATE - 1) * TB
            gather_stats(1, LATE)
            add_eps(slice(TB, LATE * TB), "eps_ready")
            for n, (src, parts) in enumerate(((qT, q_parts), (kT, k_parts))):
                own.settle()
                dve.wait_ge(S["qkT_ready"], n + 1)
                own.did(dve.tensor_tensor(rest1[:, :], src[:, :], parts[:, 0, :], ALU.subtract))
                own.did(dve.tensor_tensor(parts[:, 1, :], src[:, :], parts[:, 0, :], ALU.subtract))
                own.settle()
                dve.tensor_tensor(parts[:, 2, :], rest1[:, :], parts[:, 1, :], ALU.subtract).then_inc(S["split_ready"], 1)
                dve.wait_ge(S["split_ready"], n + 1)
            shifts(slice(TB, LATE * TB), "pow_ready", "stats_ready")
            dve.memset(pv_bank[:, :], 0.0).then_inc(S["pv_clear"], 1)
            for u in range(UNITS):
                max_unit(0, 0, u)
                if u % 4 == 3:
                    sum_near_qk(0, u // 4)
            near_logits(0)
            near_maxima(0)
            for step in range(4):
                row_maximum(0, 0, step)
            gate_steps = (gates_shift, gates_equal, gates_above, gates_earlier, gates_before, gates_count, gates_sum, gates_score)
            for u in range(UNITS):
                max_unit(0, 1, u)
                if u < len(gate_steps):
                    gate_steps[u](0)

            def during_first_batch(q, u):
                blocks = (B - LATE) * TB
                if q * UNITS + u < blocks:
                    block_stats(LATE * TB + q * UNITS + u)
                if (q, u) == (1, 1):
                    gather_stats(LATE, B)
                    add_eps(slice(LATE * TB, B * TB), "eps_ready")
                if (q, u) == (3, 8):
                    shifts(slice(LATE * TB, B * TB), "pow_ready", "stats_ready", 2)
                if (q, u) == (3, 10):
                    own.did(dve.memset(sel[:, :], 0.0))
                if (q, u) == (3, 11):
                    own.did(dve.memset(sel_m1[:, :], 0.0))
                if (q, u) == (3, 12):
                    three_parts(lambda i: b2_parts[:, i, :], b2[:, :], b2_rest[:, :], S["b2_parts_ready"])

            def selection():
                own.settle()
                own.did(dve.tensor_reduce(g_den[:, :, :], scores[:, :, :, :].rearrange("p n b e -> p n e b"), AX.X, ALU.add))
                yield
                own.settle()
                own.did(dve.tensor_scalar(g_den[:, :, :], g_den[:, :, :], GATE_EPS, None, ALU.add))
                yield
                own.settle()
                own.did(dve.reciprocal(g_den[:, :, :], g_den[:, :, :]))
                yield
                own.settle()
                own.did(dve.tensor_scalar(g_den[:, :, :], g_den[:, :, :], CAPACITY, None, ALU.mult))
                yield
                own.settle()
                gd = g_den[:, :, :].rearrange("p n (o e) -> p n o e", o=1).to_broadcast([P, TB, B, NEXP])
                dve.tensor_tensor(route[:, :, :].rearrange("p n (b e) -> p n b e", e=NEXP), scores[:, :, :, :], gd, ALU.mult)\
                    .then_inc(S["route_ready"], 1)
                yield
                dve.wait_ge(S["route_ps"], 1)
                dve.tensor_copy(route_rows[:, :], m1[0:SROW, :]).then_inc(S["route_kept"], 1)
                dve.wait_ge(S["route_kept"], 1)
                high = route_rows[:, :].bitcast(bf16).rearrange("p (t i) -> p t i", i=2)[:, :, 1]
                own.did(dve.tensor_copy(route_high[:, :], high))
                own.did(dve.memset(candidate[:, :], 1 << (SEARCH_BITS - 1)))
                own.settle()
                value = candidate[:, :].bitcast(fp32)
                for bit in range(SEARCH_BITS - 1, -1, -1):
                    routes = route_high if bit >= 16 else route_rows
                    own.did(dve.tensor_scalar(above[:, :], routes[:, :], value, None, ALU.is_ge, ALU.add,
                                              accum_out=taken[:, :]))
                    yield
                    own.settle()
                    own.did(dve.tensor_scalar(drop[:, :], taken[:, :], float(KEEP), float(1 << bit), ALU.is_lt, ALU.mult))
                    yield
                    own.settle()
                    own.did(dve.scalar_tensor_tensor(candidate[:, :], candidate[:, :], (1 << bit) >> 1, drop[:, :],
                                                     ALU.bitwise_xor, ALU.bitwise_xor))
                    yield
                    own.settle()
                dve.wait_ge(S["qk_prod_ready"], TB * B)
                dve.wait_ge(S["expert_rows_ready"], 2)
                own.did(dve.tensor_scalar(above[:, :], route_rows[:, :], value, None, ALU.is_gt, ALU.add, accum_out=taken[:, :]))
                own.did(dve.tensor_scalar(equal, route_rows[:, :], value, None, ALU.is_equal))
                own.settle()
                own.did(dve.tensor_tensor_scan(order, ones_t, equal, 0.0, ALU.mult, ALU.add))
                own.did(dve.tensor_scalar(room[:, :], taken[:, :], -1.0, float(KEEP), ALU.mult, ALU.add))
                own.settle()
                own.did(dve.scalar_tensor_tensor(picked, order, room[:, :], equal, ALU.is_le, ALU.mult))
                own.settle()
                own.did(dve.tensor_tensor(sel[0:SROW, :], picked, above[:, :], ALU.add))
                own.settle()
                dve.tensor_scalar(sel_m1[0:SROW, :], sel[0:SROW, :], -1.0, None, ALU.add).then_inc(S["sel_ready"], 1)

            FINISH_AT = ((0, 10), (0, 11), (1, 3))
            NEAR_QK_AT = ((1, 10), (1, 12), (2, 6), (2, 8))
            GATE_STEPS_AT = ((0, 13), (0, 14), (0, 15), (1, 4), (1, 5), (1, 6), (1, 7), (1, 8))

            def body(b, last, select=None):
                first = isinstance(b, int) and b == 0
                for q in range(QUADS):
                    due = (b, q + 1) if q < QUADS - 1 else (b + 1, 0)
                    if q < QUADS - 1 or not last:
                        row_maximum(*due, 0)
                    for u in range(UNITS):
                        if q < 2:
                            max_unit(b, q + 2, u)
                        elif not last:
                            max_unit(b + 1, q - 2, u)
                        if u < 3 and (q < QUADS - 1 or not last):
                            row_maximum(*due, u + 1)
                        if u == 9:
                            if q > 0:
                                keep_o(b, q - 1)
                            elif not first:
                                keep_o(b - 1, QUADS - 1)
                        if not first:
                            if (q, u) in FINISH_AT:
                                finish_attention(b - 1, FINISH_AT.index((q, u)))
                            if (q, u) == (1, 14):
                                add_residual(b - 1)
                        if not last:
                            if (q, u) in GATE_STEPS_AT:
                                gate_steps[GATE_STEPS_AT.index((q, u))](b + 1)
                            if (q, u) in NEAR_QK_AT:
                                sum_near_qk(b + 1, NEAR_QK_AT.index((q, u)))
                            if (q, u) == (2, 11):
                                near_logits(b + 1)
                            if (q, u) == (2, 13):
                                near_maxima(b + 1)
                        if first:
                            during_first_batch(q, u)
                        if (q, u) == (2, 4):
                            near_minus_max(b)
                        if (q, u) == (3, 5):
                            near_sums(b)
                        if select is not None:
                            if last and (q, u) > (2, 4):
                                for _ in range(4):
                                    next(select, None)
                            elif last and q < 2 and u > 2 and u % 4 != 1:
                                next(select, None)
                            elif not last and ((1, 9) <= (q, u) < (1, 14) or (q, u) == (1, 15) or q >= 2 and u > 2 and u != 9):
                                next(select, None)

            body(0, False)
            steps = QUADS * 3 + 1 + 3 + 9
            start = own.n
            with dve.Fori(1, B - 2) as b:
                own.n = (b - 1) * steps + start
                body(b, False)
            own.n = start + (B - 3) * steps
            select = selection()
            body(B - 2, False, select)
            body(B - 1, True, select)
            for _ in select:
                pass
            keep_o(B - 1, QUADS - 1)
            for step in range(3):
                finish_attention(B - 1, step)

            def ffn(i):
                for half, s in enumerate(("out_even", "out_odd")):
                    wait(dve, S[s], 16 * i)
                    dve.wait_ge(S["y_ps"], 2 * i + half + 1)
                    xb = x_all[:, at(2 * i + half), :, :].rearrange("p o n e -> p (o n e)")
                    dve.tensor_tensor(ffn_out[:, half, :], (pv_bank, m0)[half][:, :], xb, ALU.add).then_inc(S["ffn_ready"], 1)

            ffn(0)
            add_residual(B - 1)
            with dve.Fori(1, B // 2) as i:
                ffn(i)


def kernel(**inputs):
    import concourse.bacc as bacc
    from concourse.bass_utils import run_bass_kernel_spmd as run

    a = {n.split("_", 1)[1]: np.asarray(v) for n, v in inputs.items()}
    a = {n.replace("attn_", "").replace("ffn_", ""): v for n, v in a.items()}
    f = np.float32
    arrays = {
        "x": a["hidden_states"],
        "brow": np.tile(np.concatenate([a["bq"], a["bk"], a["bv"], a["w_gate_b"], a["bo"]])[None], (PARTS, 1)),
    }
    blocks = {
        "wcat": np.concatenate([a["Wq"], a["Wk"], a["Wv"], a["w_gate_w"]], axis=1),
        "bqk": np.stack([a["bq"], a["bk"]], axis=1),
        "wo": a["Wo"],
        "ek": np.tile(a["emb_rel_k"][0].T, (H, 1)),
        "ev": np.tile(a["emb_rel_v"].reshape(1, J * D), (P, 1)),
        "w1": a["W1"].transpose(1, 0, 2).reshape(E, NEXP * HID),
        "b1": a["b1"].reshape(2, P).T,
        "w2": a["W2"].reshape(2, P, E).transpose(1, 0, 2).reshape(P, 2 * E),
        "b2": np.tile(a["b2"], (P // NEXP, 1)),
    }
    p = np.arange(P)
    w = np.arange(BAND)[None, :] - p[:, None]
    band = np.where((w >= 0) & (w <= 2 * WINDOW), NEG, 0.0).astype(f)
    j = np.arange(J)
    edge = np.zeros((P, 2, J, H), f)
    edge[:, 0][(p[:, None] + j[None] - WINDOW) < 0] = NEG
    edge[:, 1][(p[:, None] + j[None] - WINDOW) >= P] = NEG
    blocks |= {
        "ident": np.eye(P, dtype=f),
        "band": band,
        "edge": edge.reshape(P, 2 * JH),
        "headmask": (p[:, None] // D == np.arange(H)[None]).astype(f),
        "earlier": np.tile((np.arange(NEXP)[None, :] < np.arange(NEXP)[:, None]).astype(f).reshape(1, -1), (P, 1)),
        "batchmask": (p[:, None] // NEXP == np.arange(B)[None]).astype(f),
    }
    x, brow = arrays["x"], arrays["brow"]
    arrays = {"x": x} | {n: np.concatenate([blocks[c] for c, _ in layout], axis=1)
                         for n, layout in (("first", FIRST_COLUMNS), ("rest", REST_COLUMNS))} | {"brow": brow}
    arrays = {f"in_{n}": np.ascontiguousarray(v) for n, v in arrays.items()}
    nc = bacc.Bacc("TRN2", target_bir_lowering=False, num_devices=1)
    args = [nc.dram_tensor(n, v.shape, mybir.dt.from_np(v.dtype), kind="ExternalInput").ap() for n, v in arrays.items()]
    out = nc.dram_tensor("out_0", (B, T, E), fp32, kind="ExternalOutput").ap()
    build_program(nc, *args, out)
    r = run(nc, [arrays], core_ids=[0])
    return r.results[0]["out_0"]
```
